# Optimizing a Trainium2 kernel written in Bass

```python
import numpy as np
import jax
import jax.numpy as jnp

def _softmax(x, axis=-1):
    return jax.nn.softmax(x, axis=axis)

def _gelu(x):
    return jax.nn.gelu(x, approximate=True)

def _silu(x):
    return jax.nn.silu(x)

def _sigmoid(x):
    return jax.nn.sigmoid(x)

def _layernorm(x, axis=-1, eps=1e-05):
    m = jnp.mean(x, axis=axis, keepdims=True)
    v = jnp.var(x, axis=axis, keepdims=True)
    return (x - m) / jnp.sqrt(v + eps)

def _scatter_add(tgt, idx, src, axis=0):
    return tgt.at[idx].add(src)

def _segment_sum(src, seg, n):
    return jax.ops.segment_sum(src, seg, n)
kernel_name = 'mk_xattn_ffn_d2_seqx_r4_0f9454'

def setup_inputs(seed: int=0):
    np.random.seed(seed)
    _w = jnp.asarray

    def _rec_inputs():
        import jax
        import jax.numpy as jnp
        _rk = jax.random.key(seed)
        x = -0.0003929 + 0.9999 * jax.random.normal(jax.random.fold_in(_rk, 1), (1, 2048, 256), jnp.float32)
        _lenS = 2048 - jax.random.randint(jax.random.fold_in(_rk, 7), (1,), 0, max(1, 2048 // 4) + 1, jnp.int32)
        _lenS2 = 1601 - jax.random.randint(jax.random.fold_in(_rk, 8), (1,), 0, max(1, 1601 // 4) + 1, jnp.int32)
        _ctx_1024P = jax.random.normal(jax.random.fold_in(_rk, 11), (1, 16, 256), jnp.float32)
        _ctx_1024c = jax.random.dirichlet(jax.random.fold_in(_rk, 511), 0.3 * jnp.ones((16,), jnp.float32), (1, 1601))
        _ctx_1024t = jnp.einsum('bsk,bkd->bsd', _ctx_1024c, _ctx_1024P)
        _ctx_1024t = _ctx_1024t * jax.lax.rsqrt(jnp.mean(jnp.square(_ctx_1024t)) + 1e-12) * 0.953939
        ctx_1024 = 2.81802e-05 + 1.00001 * (_ctx_1024t + 0.3 * jax.random.normal(jax.random.fold_in(_rk, 611), (1, 1601, 256), jnp.float32))
        return (x, ctx_1024)
    x, ctx_1024 = _rec_inputs()

    def _L0_xattn_setup():
        import jax, jax.numpy as jnp
        import numpy as np
        EMBED = 256
        HIDDEN = 128
        LN_EPS = 1e-05
        key = jax.random.key(seed)
        ks = jax.random.split(key, 9)
        B, Sq, Skv = (4, 1024, 1024)
        q_feat = jax.random.normal(ks[0], (B, Sq, EMBED), dtype=jnp.float32)
        kv_feat = jax.random.normal(ks[1], (B, Skv, EMBED), dtype=jnp.float32)

        def w(k, fan_in, fan_out):
            s = (6.0 / (fan_in + fan_out)) ** 0.5
            return jax.random.uniform(k, (fan_in, fan_out), jnp.float32, -s, s)
        Wq = w(ks[2], EMBED, HIDDEN)
        Wk = w(ks[3], EMBED, HIDDEN)
        Wv = w(ks[4], EMBED, HIDDEN)
        Wo = w(ks[5], HIDDEN, EMBED)
        bo = jnp.zeros((EMBED,), jnp.float32)
        Wfc = w(ks[6], EMBED, EMBED)
        ln_gamma = jnp.ones((EMBED,), jnp.float32)
        ln_beta = jnp.zeros((EMBED,), jnp.float32)
        return {'q_feat': q_feat, 'kv_feat': kv_feat, 'Wq': Wq, 'Wk': Wk, 'Wv': Wv, 'Wo': Wo, 'bo': bo, 'Wfc': Wfc, 'ln_gamma': ln_gamma, 'ln_beta': ln_beta}
    _L0_xattn_all = _L0_xattn_setup()
    _L0_xattn_in = {k: v for k, v in _L0_xattn_all.items() if k in ('Wq', 'Wk', 'Wv', 'Wo', 'bo', 'Wfc', 'ln_gamma', 'ln_beta')}
    del _L0_xattn_all

    def _L0_ffn_setup():
        import jax, jax.numpy as jnp
        import numpy as np
        B, S, DIM = (2, 512, 256)
        HID = 512
        E, NSH, TOPK = (8, 2, 2)

        def _ffn(x, w1, w2, w3):
            return jax.nn.silu(x @ w1.T) * (x @ w3.T) @ w2.T
        key = jax.random.key(seed)
        ks = jax.random.split(key, 8)
        sc = 0.02
        return {'x': jax.random.normal(ks[0], (B, S, DIM), jnp.float32), 'router_w': jax.random.normal(ks[1], (E, DIM), jnp.float32) * sc, 'expert_bias': jnp.zeros((E,), jnp.float32), 'w1': jax.random.normal(ks[2], (E, HID, DIM), jnp.float32) * sc, 'w3': jax.random.normal(ks[3], (E, HID, DIM), jnp.float32) * sc, 'w2': jax.random.normal(ks[4], (E, DIM, HID), jnp.float32) * sc, 'sw1': jax.random.normal(ks[5], (NSH, HID, DIM), jnp.float32) * sc, 'sw3': jax.random.normal(ks[6], (NSH, HID, DIM), jnp.float32) * sc, 'sw2': jax.random.normal(ks[7], (NSH, DIM, HID), jnp.float32) * sc}
    _L0_ffn_all = _L0_ffn_setup()
    _L0_ffn_in = {k: v for k, v in _L0_ffn_all.items() if k in ('router_w', 'expert_bias', 'w1', 'w3', 'w2', 'sw1', 'sw3', 'sw2')}
    del _L0_ffn_all

    def _L1_xattn_setup():
        import jax, jax.numpy as jnp
        import numpy as np
        H = 256
        B = 8
        L_CHAR = 512
        L_SUB = 256

        def _linear(x, W, b):
            return jnp.einsum('blh,oh->blo', x, W) + b

        def _interp_linear(x, out_len):
            L_in = x.shape[1]
            pos = (jnp.arange(out_len, dtype=x.dtype) + 0.5) * (L_in / out_len) - 0.5
            pos = jnp.clip(pos, 0.0, L_in - 1)
            lo = jnp.floor(pos).astype(jnp.int32)
            hi = jnp.minimum(lo + 1, L_in - 1)
            w = (pos - lo.astype(x.dtype))[None, :, None]
            return x[:, lo] * (1 - w) + x[:, hi] * w
        key = jax.random.key(seed)
        ks = jax.random.split(key, 18)
        s = 0.02
        inp = {'char_emb': jax.random.normal(ks[0], (B, L_CHAR, H), jnp.float32), 'subword_emb': jax.random.normal(ks[1], (B, L_SUB, H), jnp.float32)}
        names = ['Wq_c', 'Wk_s', 'Wv_s', 'Wq_s', 'Wk_c', 'Wv_c']
        for i, n in enumerate(names):
            inp[n] = jax.random.normal(ks[2 + 2 * i], (H, H), jnp.float32) * s
            inp['b' + n[1:]] = jax.random.normal(ks[3 + 2 * i], (H,), jnp.float32) * s
        inp['Wg'] = jax.random.normal(ks[14], (H, 2 * H), jnp.float32) * s
        inp['bg'] = jax.random.normal(ks[15], (H,), jnp.float32) * s
        return inp
    _L1_xattn_all = _L1_xattn_setup()
    _L1_xattn_in = {k: v for k, v in _L1_xattn_all.items() if k in ('Wq_c', 'bq_c', 'Wk_s', 'bk_s', 'Wv_s', 'bv_s', 'Wq_s', 'bq_s', 'Wk_c', 'bk_c', 'Wv_c', 'bv_c', 'Wg', 'bg')}
    del _L1_xattn_all

    def _L1_ffn_setup():
        import jax, jax.numpy as jnp
        import numpy as np
        TOP_P = 0.3
        key = jax.random.key(seed)
        k1, k2, k3, k4 = jax.random.split(key, 4)
        B, S, D, H, E = (4, 1024, 256, 256, 8)
        x = jax.random.normal(k1, (B, S, D), dtype=jnp.float32)
        gate_W = jax.random.normal(k2, (E, D), dtype=jnp.float32) / np.float32(np.sqrt(D))
        expert_W = jax.random.normal(k3, (E, H, D), dtype=jnp.float32) / np.float32(np.sqrt(D))
        out_W = jax.random.normal(k4, (D, H), dtype=jnp.float32) / np.float32(np.sqrt(H))
        return {'x': x, 'gate_W': gate_W, 'expert_W': expert_W, 'out_W': out_W}
    _L1_ffn_all = _L1_ffn_setup()
    _L1_ffn_in = {k: v for k, v in _L1_ffn_all.items() if k in ('gate_W', 'expert_W', 'out_W')}
    del _L1_ffn_all
    return {'x': x, 'ctx_1024': ctx_1024, 'L0_xattn_Wq': _L0_xattn_in['Wq'], 'L0_xattn_Wk': _L0_xattn_in['Wk'], 'L0_xattn_Wv': _L0_xattn_in['Wv'], 'L0_xattn_Wo': _L0_xattn_in['Wo'], 'L0_xattn_bo': _L0_xattn_in['bo'], 'L0_xattn_Wfc': _L0_xattn_in['Wfc'], 'L0_xattn_ln_gamma': _L0_xattn_in['ln_gamma'], 'L0_xattn_ln_beta': _L0_xattn_in['ln_beta'], 'L0_ffn_router_w': _L0_ffn_in['router_w'], 'L0_ffn_expert_bias': _L0_ffn_in['expert_bias'], 'L0_ffn_w1': _L0_ffn_in['w1'], 'L0_ffn_w3': _L0_ffn_in['w3'], 'L0_ffn_w2': _L0_ffn_in['w2'], 'L0_ffn_sw1': _L0_ffn_in['sw1'], 'L0_ffn_sw3': _L0_ffn_in['sw3'], 'L0_ffn_sw2': _L0_ffn_in['sw2'], 'L1_xattn_Wq_c': _L1_xattn_in['Wq_c'], 'L1_xattn_bq_c': _L1_xattn_in['bq_c'], 'L1_xattn_Wk_s': _L1_xattn_in['Wk_s'], 'L1_xattn_bk_s': _L1_xattn_in['bk_s'], 'L1_xattn_Wv_s': _L1_xattn_in['Wv_s'], 'L1_xattn_bv_s': _L1_xattn_in['bv_s'], 'L1_xattn_Wq_s': _L1_xattn_in['Wq_s'], 'L1_xattn_bq_s': _L1_xattn_in['bq_s'], 'L1_xattn_Wk_c': _L1_xattn_in['Wk_c'], 'L1_xattn_bk_c': _L1_xattn_in['bk_c'], 'L1_xattn_Wv_c': _L1_xattn_in['Wv_c'], 'L1_xattn_bv_c': _L1_xattn_in['bv_c'], 'L1_xattn_Wg': _L1_xattn_in['Wg'], 'L1_xattn_bg': _L1_xattn_in['bg'], 'L1_ffn_gate_W': _L1_ffn_in['gate_W'], 'L1_ffn_expert_W': _L1_ffn_in['expert_W'], 'L1_ffn_out_W': _L1_ffn_in['out_W']}

def reference(x, ctx_1024, L0_xattn_Wq, L0_xattn_Wk, L0_xattn_Wv, L0_xattn_Wo, L0_xattn_bo, L0_xattn_Wfc, L0_xattn_ln_gamma, L0_xattn_ln_beta, L0_ffn_router_w, L0_ffn_expert_bias, L0_ffn_w1, L0_ffn_w3, L0_ffn_w2, L0_ffn_sw1, L0_ffn_sw3, L0_ffn_sw2, L1_xattn_Wq_c, L1_xattn_bq_c, L1_xattn_Wk_s, L1_xattn_bk_s, L1_xattn_Wv_s, L1_xattn_bv_s, L1_xattn_Wq_s, L1_xattn_bq_s, L1_xattn_Wk_c, L1_xattn_bk_c, L1_xattn_Wv_c, L1_xattn_bv_c, L1_xattn_Wg, L1_xattn_bg, L1_ffn_gate_W, L1_ffn_expert_W, L1_ffn_out_W):
    import jax
    import jax.numpy as jnp

    def _L0_xattn_ref(q_feat, kv_feat, Wq, Wk, Wv, Wo, bo, Wfc, ln_gamma, ln_beta):
        import jax, jax.numpy as jnp
        import numpy as np
        EMBED = 256
        HIDDEN = 128
        LN_EPS = 1e-05
        Q = jnp.einsum('bse,eh->bsh', q_feat, Wq)
        K = jnp.einsum('bse,eh->bsh', kv_feat, Wk)
        V = jnp.einsum('bse,eh->bsh', kv_feat, Wv)
        scale = 1.0 / jnp.sqrt(jnp.asarray(HIDDEN, Q.dtype))
        scores = jnp.einsum('bqh,bkh->bqk', Q, K) * scale
        attn = jax.nn.softmax(scores, axis=-1)
        ctx = jnp.einsum('bqk,bkh->bqh', attn, V)
        out = jnp.einsum('bqh,he->bqe', ctx, Wo) + bo
        out = out + q_feat
        out = jnp.einsum('bqe,ef->bqf', out, Wfc)
        mu = jnp.mean(out, axis=-1, keepdims=True)
        var = jnp.mean(jnp.square(out - mu), axis=-1, keepdims=True)
        out = (out - mu) * jax.lax.rsqrt(var + LN_EPS) * ln_gamma + ln_beta
        return out

    def _L0_ffn_ref(x, router_w, expert_bias, w1, w3, w2, sw1, sw3, sw2):
        import jax, jax.numpy as jnp
        import numpy as np
        B, S, DIM = (2, 512, 256)
        HID = 512
        E, NSH, TOPK = (8, 2, 2)

        def _ffn(x, w1, w2, w3):
            return jax.nn.silu(x @ w1.T) * (x @ w3.T) @ w2.T
        bs, sl, d = x.shape
        xf = x.reshape(-1, d)
        shared = jnp.zeros_like(xf)
        for i in range(sw1.shape[0]):
            shared = shared + _ffn(xf, sw1[i], sw2[i], sw3[i])
        logits = xf @ router_w.T + expert_bias
        rw, sel = jax.lax.top_k(logits, TOPK)
        rw = jax.nn.softmax(rw.astype(jnp.float32), axis=-1).astype(x.dtype)
        onehot = jax.nn.one_hot(sel, E, dtype=x.dtype)
        combine = jnp.einsum('tk,tke->te', rw, onehot)

        def body(acc, ew):
            e1, e3, e2, cw = ew
            acc = acc + cw[:, None] * _ffn(xf, e1, e2, e3)
            return (acc, None)
        out, _ = jax.lax.scan(body, jnp.zeros_like(xf), (w1, w3, w2, combine.T))
        out = out + shared
        return out.reshape(bs, sl, -1)

    def _L1_xattn_ref(char_emb, subword_emb, Wq_c, bq_c, Wk_s, bk_s, Wv_s, bv_s, Wq_s, bq_s, Wk_c, bk_c, Wv_c, bv_c, Wg, bg):
        import jax, jax.numpy as jnp
        import numpy as np
        H = 256
        B = 8
        L_CHAR = 512
        L_SUB = 256

        def _linear(x, W, b):
            return jnp.einsum('blh,oh->blo', x, W) + b

        def _interp_linear(x, out_len):
            L_in = x.shape[1]
            pos = (jnp.arange(out_len, dtype=x.dtype) + 0.5) * (L_in / out_len) - 0.5
            pos = jnp.clip(pos, 0.0, L_in - 1)
            lo = jnp.floor(pos).astype(jnp.int32)
            hi = jnp.minimum(lo + 1, L_in - 1)
            w = (pos - lo.astype(x.dtype))[None, :, None]
            return x[:, lo] * (1 - w) + x[:, hi] * w
        h = char_emb.shape[-1]
        scale = 1.0 / jnp.sqrt(jnp.asarray(h, char_emb.dtype))
        Q_char = _linear(char_emb, Wq_c, bq_c)
        K_sub = _linear(subword_emb, Wk_s, bk_s)
        V_sub = _linear(subword_emb, Wv_s, bv_s)
        scores = jnp.einsum('bqh,bkh->bqk', Q_char, K_sub) * scale
        char2sub = jnp.einsum('bqk,bkh->bqh', jax.nn.softmax(scores, axis=-1), V_sub)
        Q_sub = _linear(subword_emb, Wq_s, bq_s)
        K_char = _linear(char_emb, Wk_c, bk_c)
        V_char = _linear(char_emb, Wv_c, bv_c)
        scores2 = jnp.einsum('bqh,bkh->bqk', Q_sub, K_char) * scale
        sub2char = jnp.einsum('bqk,bkh->bqh', jax.nn.softmax(scores2, axis=-1), V_char)
        L_char = char_emb.shape[1]
        if sub2char.shape[1] != L_char:
            sub2char = _interp_linear(sub2char, L_char)
        gate_in = jnp.concatenate([char2sub, sub2char], axis=-1)
        gate = jax.nn.sigmoid(jnp.einsum('blh,oh->blo', gate_in, Wg) + bg)
        return gate * char2sub + (1 - gate) * sub2char

    def _L1_ffn_ref(x, gate_W, expert_W, out_W):
        import jax, jax.numpy as jnp
        import numpy as np
        TOP_P = 0.3
        B, S, D = x.shape
        E = gate_W.shape[0]
        N = B * S
        p = jax.nn.softmax(jnp.einsum('bsd,ed->bse', x, gate_W), axis=-1).reshape(N, E)
        tpi = (p > TOP_P).astype(jnp.int32)
        cnt = jnp.sum(tpi[:, :, None] == jnp.arange(E)[None, None, :], axis=1)
        scale = cnt.astype(x.dtype) * p
        x2 = x.reshape(N, D)
        h = jnp.einsum('nd,ehd->neh', x2, expert_W)
        final = jnp.einsum('neh,ne->nh', h, scale)
        out = jnp.einsum('nh,dh->nd', final, out_W).reshape(B, S, D)
        return out
    x = x + _L0_xattn_ref(_layernorm(x, axis=-1), ctx_1024, L0_xattn_Wq, L0_xattn_Wk, L0_xattn_Wv, L0_xattn_Wo, L0_xattn_bo, L0_xattn_Wfc, L0_xattn_ln_gamma, L0_xattn_ln_beta)
    x = x + _L0_ffn_ref(_layernorm(x, axis=-1), L0_ffn_router_w, L0_ffn_expert_bias, L0_ffn_w1, L0_ffn_w3, L0_ffn_w2, L0_ffn_sw1, L0_ffn_sw3, L0_ffn_sw2)
    x = x + _L1_xattn_ref(_layernorm(x, axis=-1), ctx_1024, L1_xattn_Wq_c, L1_xattn_bq_c, L1_xattn_Wk_s, L1_xattn_bk_s, L1_xattn_Wv_s, L1_xattn_bv_s, L1_xattn_Wq_s, L1_xattn_bq_s, L1_xattn_Wk_c, L1_xattn_bk_c, L1_xattn_Wv_c, L1_xattn_bv_c, L1_xattn_Wg, L1_xattn_bg)
    x = x + _L1_ffn_ref(_layernorm(x, axis=-1), L1_ffn_gate_W, L1_ffn_expert_W, L1_ffn_out_W)
    return x

_drawn_inputs = setup_inputs


def setup_inputs(seed=0):
    import zlib

    import numpy as np

    out = dict(_drawn_inputs(seed))
    spreads = {'L0_xattn_bo': (0.0, 0.1),
     'L0_xattn_ln_gamma': (1.0, 0.2),
     'L0_xattn_ln_beta': (0.0, 0.1),
     'L0_ffn_expert_bias': (0.0, 0.8)}
    factors = {'L0_ffn_router_w': 3.951,
     'L0_ffn_w1': 3.518,
     'L0_ffn_w3': 3.363,
     'L0_ffn_w2': 3.603,
     'L1_xattn_Wq_c': 8.0,
     'L1_xattn_bq_c': 31.135,
     'L1_xattn_Wk_s': 8.0,
     'L1_xattn_bk_s': 64.0,
     'L1_xattn_bv_s': 5.262,
     'L1_xattn_Wq_s': 8.0,
     'L1_xattn_bq_s': 33.258,
     'L1_xattn_Wk_c': 8.0,
     'L1_xattn_bk_c': 64.0,
     'L1_xattn_bv_c': 3.956,
     'L1_xattn_Wg': 8.0,
     'L1_xattn_bg': 36.587}
    for name, (base, spread) in spreads.items():
        noise = np.random.default_rng([zlib.crc32(name.encode()), seed]).standard_normal(out[name].shape)
        drawn = base * np.exp(spread * noise) if base else spread * noise
        out[name] = jnp.asarray(drawn.astype(out[name].dtype))
    for name, factor in factors.items():
        out[name] = (out[name] * factor).astype(out[name].dtype)
    return out
```

```python
import concourse.bass as bass
from concourse import mybir
from contextlib import ExitStack

F32 = mybir.dt.float32
F32R = mybir.dt.float32r
I32 = mybir.dt.int32
ALU = mybir.AluOpType
ACT = mybir.ActivationFunctionType
AX = mybir.AxisListType.X
ds = bass.ds

P = 128
D = 256
DC = D // P
S = 2048
NT = S // P
C = 1601
NC = -(-C // P)
CP = NC * P
HA = 128
E = 8
NSH = 2
F = 512
EPS = 1e-5
BIG = 3.0e38


def pairs(eng, n, body):
    main = (n - 2) // 2 * 2
    if main > 0:
        with eng.Fori(0, main // 2) as j:
            body(j * 2, 0, True)
            body(j * 2 + 1, 1, True)
    for i in range(main, n):
        body(i, i % 2, i + 2 < n)


def pairs3(eng, n, body):
    main = (n - 3) // 2 * 2
    with eng.Fori(0, main // 2) as j:
        body(j * 2, 0, 4)
        body(j * 2 + 1, 1, 4)
    for i in range(main, n):
        body(i, i % 2, n - i)


def mm3(pe, out, wh, wl, xh, xl, first, last):
    pe.matmul(out, wh, xh, start=first, stop=False)
    pe.matmul(out, wh, xl, start=False, stop=False)
    return pe.matmul(out, wl, xh, start=False, stop=last)


def build(nc, A, out):
    top = ExitStack()
    with top:
        def sb(ctx, name, shape, dt=F32):
            return ctx.enter_context(nc.sbuf_tensor(name, shape, dt))

        def split_pair(ctx, name, shape):
            return sb(ctx, name + "_hi", shape, F32R), sb(ctx, name + "_lo", shape, F32R)

        banks = [top.enter_context(nc.psum_tensor(f"bank{i}", [P, 512], F32)) for i in range(0, 4)]
        wide = top.enter_context(nc.psum_tensor("wide", [P, 4 * 512], F32))

        X = sb(top, "X", [P, NT * D])
        ident = sb(top, "ident", [P, P])
        MV = sb(top, "MV", [P, 2 * NT])
        RSTD = sb(top, "RSTD", [P, NT])
        mhalf = sb(top, "mhalf", [P, NT])
        stats = sb(top, "stats", [P, 6 * NT])
        rows = sb(top, "rows", [P, 9 * D])
        GAMMA, BETA, BFC, BV_S, BV_C, BG = (rows[:, j * D:(j + 1) * D] for j in range(6))
        BIASE = rows[:, 6 * D:6 * D + E]
        cols = sb(top, "cols", [P, 16])
        BO, BQC, BKS, BQS, BKC = (cols[:, 2 * j:2 * j + 2] for j in range(5))
        CT_hi, CT_lo = split_pair(top, "CT", [P, DC, CP])

        free_sems = [nc.alloc_semaphore(f"signal{i}") for i in range(140)]

        def sems(ctx, names):
            got = [free_sems.pop(0) for _ in names.split()]

            def give_back():
                for s in got:
                    nc.gpsimd.sem_clear(s)
                free_sems.extend(got)
            ctx.callback(give_back)
            return got


        def row_statistics(dve, src, st):
            def one(i, p, more):
                dve.bn_stats(out=stats[:, ds(i * 6, 6)], in_=src[:, ds(i * D, D)]).then_inc(st, 1)
            pairs(dve, NT, one)
            dve.wait_ge(st, NT)
            for i in range(NT):
                dve.bn_aggr(out=MV[:, 2 * i:2 * i + 2], in_=stats[:, 6 * i:6 * i + 6]).then_inc(st, 1)

        def split_phase(tag, items):
            with ExitStack() as ctx:
                loaded = sems(ctx, " ".join(f"{tag}ld{j}" for j in range(len(items))))
                hi_done, lo_done = sems(ctx, f"{tag}hi {tag}lo")
                blk = ctx.enter_context(nc.Block())

                @blk.sync
                def _(sp):
                    for j, (dram, raw, hi, lo) in enumerate(items):
                        sp.dma_start(raw, dram.rearrange("(c p) n -> p c n", p=P)).then_inc(loaded[j], 16)

                @blk.scalar
                def _(act):
                    for j, (dram, raw, hi, lo) in enumerate(items):
                        act.wait_ge(loaded[j], 16)
                        act.activation(hi, raw, ACT.Copy).then_inc(hi_done, 1)

                @blk.vector
                def _(dve):
                    for j, (dram, raw, hi, lo) in enumerate(items):
                        dve.wait_ge(hi_done, j + 1)
                        dve.tensor_tensor(lo, raw, hi.bitcast(F32), ALU.subtract).then_inc(lo_done, 1)

        def weights(ctx, tag, spec):
            total = sum(kc * n for kc, n in spec.values())
            raw = sb(ctx, tag + "raw", [P, total])
            hi, lo = split_pair(ctx, tag, [P, total])
            items, at, off = [], {}, 0
            for name, (kc, n) in spec.items():
                r, h, l = (t[:, off:off + kc * n].rearrange("p (c n) -> p c n", c=kc) for t in (raw, hi, lo))
                items.append((A[name], r, h, l))
                at[name] = (h, l)
                off += kc * n
            split_phase(tag, items)
            return at

        def transpose_pass(tag, n, kc, source, products, evac, prepare=None):
            with ExitStack() as ctx:
                t_in = sb(ctx, tag + "tin", [P, 2, kc, P])
                s_hi, s_lo = split_pair(ctx, tag + "slot", [P, 2, kc, P])
                fi, td, hd, ld, md, de = sems(ctx, " ".join(tag + s for s in "fi td hd ld md de".split()))
                (own,) = sems(ctx, tag + "own")
                blk = ctx.enter_context(nc.Block())

                @blk.vector
                def _(dve):
                    def fill(i, p):
                        parts = source(i)
                        for j, x in enumerate(parts):
                            w = kc // len(parts)
                            dve.tensor_copy(t_in[:, p, j * w:(j + 1) * w, :],
                                            x.rearrange("p (c n) -> p c n", c=w)).then_inc(fi, 1)

                    def low(i, p):
                        dve.wait_ge(hd, i + 1)
                        dve.tensor_tensor(s_lo[:, p, :, :], banks[p][:, 0:kc * P].rearrange("p (c n) -> p c n", c=kc),
                                          s_hi[:, p, :, :].bitcast(F32), ALU.subtract).then_inc(ld, 1)
                    fill(0, 0)
                    fill(1, 1)
                    low(0, 0)
                    fill(2, 0)

                    def step(i, p, left):
                        if left > 1:
                            low(i + 1, 1 - p)
                        if left > 3:
                            fill(i + 3, 1 - p)
                        dve.wait_ge(md, i + 1)
                        evac(dve, i, p, banks[2 + p], own).then_inc(de, 1)
                    pairs3(dve, n, step)

                @blk.scalar
                def _(act):
                    def step(i, p, more):
                        act.wait_ge(td, i + 1)
                        act.activation(s_hi[:, p, :, :], banks[p][:, 0:kc * P].rearrange("p (c n) -> p c n", c=kc),
                                       ACT.Copy).then_inc(hd, 1)
                        if prepare:
                            prepare(act, i, p, own)
                    pairs(act, n, step)

                @blk.tensor
                def _(pe):
                    pe.sem_inc(de, 2)
                    parts = len(source(0))

                    def transposes(i, p):
                        pe.wait_ge(fi, parts * (i + 1))
                        for c in range(kc):
                            t = pe.transpose(banks[p][:, c * P:(c + 1) * P], t_in[:, p, c, :], ident[:, :])
                        t.then_inc(td, 1)
                    transposes(0, 0)
                    transposes(1, 1)

                    def step(i, p, more):
                        pe.wait_ge(ld, i + 1)
                        pe.wait_ge(de, i + 1)
                        products(pe, banks[2 + p], s_hi[:, p, :, :], s_lo[:, p, :, :]).then_inc(md, 1)
                        if more:
                            transposes(i + 2, p)
                    pairs(pe, n, step)

        def experts(tag, n, w_up, w_gate, w_down, CW, ncw, cw_at, XT_hi, XT_lo):
            NB, FC, TB = S // 512, F // P, 4
            W = DC * F * 2 + FC * D
            Q = W // NB
            with ExitStack() as ctx:
                raw = sb(ctx, tag + "raw", [P, W])
                w_hi, w_lo = split_pair(ctx, tag + "w", [P, 2, W])
                sil = sb(ctx, tag + "sil", [P, 2, 512])
                gate = sb(ctx, tag + "gate", [P, 2, 512])
                g_hi, g_lo = split_pair(ctx, tag + "g", [P, FC, 512])
                (ldw, whi, wlo, hd, sd, gd, ghi, glo, yd, yf) = sems(
                    ctx, " ".join(tag + s for s in "ldw whi wlo hd sd gd ghi glo yd yf".split()))
                blk = ctx.enter_context(nc.Block())

                def up(t, par, which, c, m):
                    o = which * DC * F + c * F + m * P
                    return t[:, par, o:o + P]

                def down(t, par, m):
                    o = 2 * DC * F + m * D
                    return t[:, par, o:o + D]

                @blk.sync
                def _(sp):
                    def load(e, wait):
                        if wait:
                            sp.wait_ge(wlo, NB * e)
                        for j, w in enumerate((w_up, w_gate)):
                            sp.dma_start(raw[:, j * DC * F:(j + 1) * DC * F].rearrange("p (c n) -> p c n", c=DC),
                                         w[ds(e, 1), :, :].rearrange("a (c p) n -> p (a c) n", p=P)).then_inc(ldw, 16)
                        sp.dma_start(raw[:, 2 * DC * F:W].rearrange("p (c n) -> p c n", c=FC),
                                     w_down[ds(e, 1), :, :].rearrange("a (c p) n -> p (a c) n", p=P)).then_inc(ldw, 16)
                    load(0, False)
                    with sp.Fori(1, n) as e:
                        load(e, True)

                def whole(eng, body):
                    with eng.Fori(0, n // 2) as j:
                        for par in range(2):
                            body(j * 2 + par, par)

                @blk.scalar
                def _(act):
                    def split(e, par, q, more=True):
                        act.activation(w_hi[:, par, ds(q * Q, Q)], raw[:, ds(q * Q, Q)], ACT.Copy).then_inc(whi, 1)
                    act.wait_ge(ldw, 48)
                    for q in range(NB):
                        split(0, 0, q)

                    def hi(n0, c):
                        act.wait_ge(gd, n0 + 1 + 2)
                        act.activation(g_hi[:, c, :], gate[:, c % 2, :], ACT.Copy).then_inc(ghi, 1)

                    def block(e, par, b, more):
                        for c in range(FC):
                            n0 = (e * NB + b) * FC + c
                            act.wait_ge(hd, n0 + 1)
                            act.activation(sil[:, c % 2, :], banks[2 * (c % 2)][:, :], ACT.Silu).then_inc(sd, 1)
                            if c:
                                hi(n0 - 1, c - 1)
                        if more:
                            act.wait_ge(ldw, 48 * (e + 2))
                            split(e + 1, 1 - par, b)
                        hi((e * NB + b) * FC + FC - 1, FC - 1)

                    def expert(e, par, more=True):
                        with act.Fori(0, NB) as b:
                            block(e, par, b, more)
                    if n > 2:
                        with act.Fori(0, n // 2 - 1) as j:
                            expert(j * 2, 0)
                            expert(j * 2 + 1, 1)
                    expert(n - 2, 0)
                    expert(n - 1, 1, False)

                @blk.vector
                def _(dve):
                    def split(e, par, q):
                        dve.wait_ge(whi, e * NB + q + 1)
                        dve.tensor_tensor(w_lo[:, par, ds(q * Q, Q)], raw[:, ds(q * Q, Q)],
                                          w_hi[:, par, ds(q * Q, Q)].bitcast(F32), ALU.subtract).then_inc(wlo, 1)
                    for q in range(NB):
                        split(0, 0, q)

                    def lo(n0, c):
                        dve.wait_ge(ghi, n0 + 1)
                        dve.tensor_tensor(g_lo[:, c, :], gate[:, c % 2, :], g_hi[:, c, :].bitcast(F32),
                                          ALU.subtract).then_inc(glo, 1)

                    def gather(e, b):
                        dve.wait_ge(yd, e * NB + b + 1)
                        for t in range(TB):
                            x = X[:, ds((b * TB + t) * D, D)]
                            m = dve.scalar_tensor_tensor(out=x, in0=wide[:, 512 * t:512 * t + D],
                                                         scalar=CW[:, ds((b * TB + t) * ncw + (e + cw_at), 1)], in1=x,
                                                         op0=ALU.mult, op1=ALU.add)
                        m.then_inc(yf, 1)

                    def block(e, par, b, more):
                        for c in range(FC):
                            n0 = (e * NB + b) * FC + c
                            dve.wait_ge(glo, n0 + 1)
                            dve.wait_ge(sd, n0 + 1)
                            dve.tensor_tensor(gate[:, c % 2, :], sil[:, c % 2, :], banks[2 * (c % 2) + 1][:, :],
                                              ALU.mult).then_inc(gd, 1)
                            if c:
                                lo(n0 - 1, c - 1)
                        if more:
                            split(e + 1, 1 - par, b)
                        lo((e * NB + b) * FC + FC - 1, FC - 1)
                        gather(e, b)

                    def expert(e, par, more=True):
                        with dve.Fori(0, NB) as b:
                            block(e, par, b, more)
                    if n > 2:
                        with dve.Fori(0, n // 2 - 1) as j:
                            expert(j * 2, 0)
                            expert(j * 2 + 1, 1)
                    expert(n - 2, 0)
                    expert(n - 1, 1, False)

                @blk.tensor
                def _(pe):
                    pe.sem_inc(yf, 1)
                    pe.sem_inc(glo, 2)
                    pe.sem_inc(gd, 2)
                    pe.wait_ge(wlo, NB)

                    def hidden(e, par, b, c):
                        n0 = (e * NB + b) * FC + c
                        pe.wait_ge(gd, n0 + 1)
                        for which in range(2):
                            for k in range(DC):
                                m = mm3(pe, banks[2 * (c % 2) + which][:, :], up(w_hi, par, which, k, c),
                                        up(w_lo, par, which, k, c), XT_hi[:, k, ds(b * 512, 512)],
                                        XT_lo[:, k, ds(b * 512, 512)], k == 0, k == DC - 1)
                        m.then_inc(hd, 1)

                    def result(e, par, b, c):
                        if c == 0:
                            pe.wait_ge(yf, e * NB + b + 1)
                        pe.wait_ge(glo, (e * NB + b) * FC + c + 1 + 2)
                        for t in range(TB):
                            m = mm3(pe, wide[:, 512 * t:512 * t + D], g_hi[:, c, t * P:(t + 1) * P],
                                    g_lo[:, c, t * P:(t + 1) * P], down(w_hi, par, c), down(w_lo, par, c),
                                    c == 0, c == FC - 1)
                        if c == FC - 1:
                            m.then_inc(yd, 1)

                    def block(e, par, b):
                        pe.wait_ge(wlo, (e + 1) * NB)
                        for c in range(FC):
                            hidden(e, par, b, c)
                            if c >= 2:
                                result(e, par, b, c - 2)
                        result(e, par, b, FC - 2)
                        result(e, par, b, FC - 1)

                    def expert(e, par):
                        with pe.Fori(0, NB) as b:
                            block(e, par, b)
                    with pe.Fori(0, n // 2) as j:
                        expert(j * 2, 0)
                        expert(j * 2 + 1, 1)

        def ingest(tag, XT_hi, XT_lo):
            with ExitStack() as ctx:
                xn = sb(ctx, tag + "xn", [P, 2 * D])
                st, ve, rs, xr, td, hd, ld = sems(ctx, " ".join(tag + s for s in "st ve rs xr td hd ld".split()))
                blk = ctx.enter_context(nc.Block())

                @blk.gpsimd
                def _(pool):
                    pool.wait_ge(st, 2 * NT)
                    pool.tensor_scalar(RSTD[:, :], MV[:, 1::2], EPS, None, ALU.add).then_inc(ve, 1)
                    pool.wait_ge(ve, 1)
                    pool.tensor_tensor(RSTD[:, :], RSTD[:, :], mhalf[:, :], ALU.pow).then_inc(rs, 1)

                @blk.vector
                def _(dve):
                    row_statistics(dve, X, st)
                    dve.wait_ge(rs, 1)
                    dve.wait_ge(st, 2 * NT)

                    def normalise(i, p):
                        dve.tensor_scalar(xn[:, p * D:(p + 1) * D], X[:, ds(i * D, D)], MV[:, ds(2 * i, 1)],
                                          RSTD[:, ds(i, 1)], ALU.subtract, ALU.mult).then_inc(xr, 1)
                    normalise(0, 0)
                    normalise(1, 1)

                    def low(i, p, more):
                        dve.wait_ge(hd, i + 1)
                        dve.tensor_tensor(XT_lo[:, :, ds(i * P, P)],
                                          banks[p][:, 0:D].rearrange("p (c n) -> p c n", c=DC),
                                          XT_hi[:, :, ds(i * P, P)].bitcast(F32), ALU.subtract).then_inc(ld, 1)
                        if more:
                            normalise(i + 2, p)
                    pairs(dve, NT, low)

                @blk.tensor
                def _(pe):
                    pe.sem_inc(ld, 2)

                    def step(i, p, more):
                        pe.wait_ge(xr, i + 1)
                        pe.wait_ge(ld, i + 1)
                        for c in range(DC):
                            t = pe.transpose(banks[p][:, c * P:(c + 1) * P],
                                             xn[:, p * D + c * P:p * D + (c + 1) * P], ident[:, :])
                        t.then_inc(td, 1)
                    pairs(pe, NT, step)

                @blk.scalar
                def _(act):
                    def high(i, p, more):
                        act.wait_ge(td, i + 1)
                        act.activation(XT_hi[:, :, ds(i * P, P)],
                                       banks[p][:, 0:D].rearrange("p (c n) -> p c n", c=DC), ACT.Copy).then_inc(hd, 1)
                    pairs(act, NT, high)

        def slot_pass(tag, n, kc, src_hi, src_lo, products, act_evac, dve_evac, after=None, final=None):
            with ExitStack() as ctx:
                s_hi, s_lo = split_pair(ctx, tag + "slot", [P, 2, kc, P])
                sh, sl, md, ae, de = sems(ctx, " ".join(tag + s for s in "sh sl md ae de".split()))
                (own,) = sems(ctx, tag + "own")
                blk = ctx.enter_context(nc.Block())

                @blk.scalar
                def _(act):
                    def fill(i, p):
                        act.activation(s_hi[:, p, :, :], src_hi[:, 0:kc, ds(i * P, P)].bitcast(F32), ACT.Copy).then_inc(sh, 1)
                    fill(0, 0)
                    fill(1, 1)

                    def step(i, p, more):
                        act.wait_ge(md, i + 1)
                        if act_evac:
                            act_evac(act, i, p, banks[p], ae)
                        if more:
                            fill(i + 2, p)
                    pairs(act, n, step)

                @blk.vector
                def _(dve):
                    def fill(i, p):
                        dve.tensor_copy(s_lo[:, p, :, :], src_lo[:, 0:kc, ds(i * P, P)]).then_inc(sl, 1)
                    fill(0, 0)
                    fill(1, 1)

                    def step(i, p, more):
                        if act_evac:
                            dve.wait_ge(ae, i + 1)
                        else:
                            dve.wait_ge(md, i + 1)
                        dve_evac(dve, i, p, banks[p], own).then_inc(de, 1)
                        if more:
                            fill(i + 2, p)
                    pairs(dve, n, step)
                    if final:
                        final(dve, own, de)

                @blk.tensor
                def _(pe):
                    pe.sem_inc(de, 2)

                    def step(i, p, more):
                        pe.wait_ge(sh, i + 1)
                        pe.wait_ge(sl, i + 1)
                        pe.wait_ge(de, i + 1)
                        products(pe, banks[p], s_hi[:, p, :, :], s_lo[:, p, :, :]).then_inc(md, 1)
                    pairs(pe, n, step)

        def attention(tag, nq, Q_hi, Q_lo, Wq_hi, Wq_lo, bq, kc, scale, nk, nk_cols, K_hi, K_lo, V_hi, V_lo, vw,
                      finish_act, finish_dve):
            G = -(-nk // 4)
            widths = [min(512, nk_cols + nk_cols % 2 - 512 * g) for g in range(G)]
            with ExitStack() as ctx:
                prob = sb(ctx, tag + "prob", [P, nk * P])
                pt_hi, pt_lo = split_pair(ctx, tag + "pt", [P, nk * P])
                q_hi, q_lo = split_pair(ctx, tag + "q", [P, kc, P])
                part = sb(ctx, tag + "part", [P, 4])
                top1 = sb(ctx, tag + "top1", [P, 1])
                nmax = sb(ctx, tag + "nmax", [P, 1])
                rsum = sb(ctx, tag + "rsum", [P, nq])
                rinv = sb(ctx, tag + "rinv", [P, nq])
                (s_done, t_done, pv_done, q_done, thi, tlo, qhi, qlo, mx, exp_done, o_free, f_act, chain, inv_done) = sems(
                    ctx, " ".join(tag + s for s in
                                  "s t pv q thi tlo qhi qlo mx ex of fa ch iv".split()))
                tb = [banks[0], banks[1]]
                ob, qb = banks[2], banks[3]
                blk = ctx.enter_context(nc.Block())

                def q_columns(i):
                    return ds(i * P, P)

                @blk.tensor
                def _(pe):
                    pe.sem_inc(tlo, 2)
                    pe.sem_inc(o_free, 1)

                    def project(i):
                        for h in range(kc):
                            for c in range(DC):
                                m = mm3(pe, qb[:, h * P:(h + 1) * P],
                                        Wq_hi[:, c, h * P:(h + 1) * P], Wq_lo[:, c, h * P:(h + 1) * P],
                                        Q_hi[:, c, q_columns(i)], Q_lo[:, c, q_columns(i)], c == 0, c == DC - 1)
                        m.then_inc(q_done, 1)

                    def scores(i, g):
                        for c in range(kc):
                            m = mm3(pe, wide[:, 512 * g:512 * g + widths[g]], q_hi[:, c, :], q_lo[:, c, :],
                                    K_hi[:, c, 512 * g:512 * g + widths[g]], K_lo[:, c, 512 * g:512 * g + widths[g]],
                                    c == 0, c == kc - 1)
                        m.then_inc(s_done, 1)

                    def transposes(i, g):
                        pe.wait_ge(tlo, i * G + g + 1)
                        for k in range(4 * g, min(4 * g + 4, nk)):
                            m = pe.transpose(tb[g % 2][:, (k % 4) * P:(k % 4 + 1) * P], prob[:, k * P:(k + 1) * P],
                                             ident[:, :])
                        m.then_inc(t_done, 1)

                    def weighted(i):
                        pe.wait_ge(o_free, i + 1)
                        for g in range(G):
                            pe.wait_ge(tlo, i * G + g + 1 + 2)
                            for k in range(4 * g, min(4 * g + 4, nk)):
                                m = mm3(pe, ob[:, 0:vw], pt_hi[:, k * P:(k + 1) * P], pt_lo[:, k * P:(k + 1) * P],
                                        V_hi[:, k, :], V_lo[:, k, :], k == 0, k == nk - 1) if vw == D else \
                                    mm3(pe, ob[:, 0:P], V_hi[:, k, :], V_lo[:, k, :],
                                        pt_hi[:, k * P:(k + 1) * P], pt_lo[:, k * P:(k + 1) * P], k == 0, k == nk - 1)
                        m.then_inc(pv_done, 1)

                    def turn(i, more):
                        pe.wait_ge(exp_done, i)
                        pe.wait_ge(qhi, i + 1)
                        pe.wait_ge(qlo, i + 1)
                        for g in range(G):
                            transposes(i - 1, g)
                            scores(i, g)
                        if more:
                            project(i + 1)
                        weighted(i - 1)

                    project(0)
                    pe.wait_ge(qhi, 1)
                    pe.wait_ge(qlo, 1)
                    for g in range(G):
                        scores(0, g)
                    project(1)
                    with pe.Fori(1, nq - 1) as i:
                        turn(i, True)
                    turn(nq - 1, False)
                    pe.wait_ge(exp_done, nq)
                    for g in range(G):
                        transposes(nq - 1, g)
                    weighted(nq - 1)

                @blk.scalar
                def _(act):
                    def query(i):
                        act.wait_ge(q_done, i + 1)
                        for h in range(kc):
                            m = act.activation(q_hi[:, h, :], qb[:, h * P:(h + 1) * P], ACT.Identity,
                                               bias=bq[:, h:h + 1] if bq is not None else 0.0)
                        m.then_inc(qhi, 1)

                    def high(i, g):
                        act.wait_ge(t_done, i * G + g + 1)
                        w = (min(4 * g + 4, nk) - 4 * g) * P
                        act.activation(pt_hi[:, 512 * g:512 * g + w], tb[g % 2][:, 0:w], ACT.Copy).then_inc(thi, 1)

                    def exponent(i):
                        act.wait_ge(mx, i + 1)
                        act.activation(prob[:, 0:nk_cols], wide[:, 0:nk_cols], ACT.Exp, bias=nmax[:, 0:1],
                                       scale=scale, accum_out=rsum[:, ds(i, 1)]).then_inc(exp_done, 1)

                    query(0)
                    exponent(0)
                    query(1)

                    def turn(i, more):
                        for g in range(G):
                            high(i - 1, g)
                        if more:
                            query(i + 1)
                        exponent(i)
                        if finish_act:
                            act.wait_ge(pv_done, i)
                            finish_act(act, i - 1, ob).then_inc(f_act, 1)
                    with act.Fori(1, nq - 1) as i:
                        turn(i, True)
                    turn(nq - 1, False)
                    for g in range(G):
                        high(nq - 1, g)
                    if finish_act:
                        act.wait_ge(pv_done, nq)
                        finish_act(act, nq - 1, ob).then_inc(f_act, 1)

                @blk.vector
                def _(dve):
                    if nk * P > nk_cols:
                        dve.memset(prob[:, nk_cols:nk * P], 0.0).then_inc(chain, 1)
                    else:
                        dve.memset(part[:, :], 0.0).then_inc(chain, 1)
                    dve.wait_ge(chain, 1)

                    def query(i):
                        dve.wait_ge(qhi, i + 1)
                        for h in range(kc):
                            if bq is not None:
                                m = dve.scalar_tensor_tensor(out=q_lo[:, h, :], in0=qb[:, h * P:(h + 1) * P],
                                                             scalar=bq[:, h:h + 1], in1=q_hi[:, h, :].bitcast(F32),
                                                             op0=ALU.add, op1=ALU.subtract)
                            else:
                                m = dve.tensor_tensor(q_lo[:, h, :], qb[:, h * P:(h + 1) * P],
                                                      q_hi[:, h, :].bitcast(F32), ALU.subtract)
                        m.then_inc(qlo, 1)

                    def low(i, g):
                        dve.wait_ge(thi, i * G + g + 1)
                        w = (min(4 * g + 4, nk) - 4 * g) * P
                        dve.tensor_tensor(pt_lo[:, 512 * g:512 * g + w], tb[g % 2][:, 0:w],
                                          pt_hi[:, 512 * g:512 * g + w].bitcast(F32), ALU.subtract).then_inc(tlo, 1)

                    def maximum(i, g):
                        dve.wait_ge(s_done, i * G + g + 1)
                        dve.reduce_max(part[:, g:g + 1], wide[:, 512 * g:512 * g + min(512, nk_cols - 512 * g)],
                                       AX).then_inc(chain, 1)

                    def whole_maximum(i):
                        dve.wait_ge(chain, i * (G + 1) + G + 1)
                        dve.reduce_max(top1[:, :], part[:, 0:G], AX).then_inc(chain, 1)
                        dve.wait_ge(chain, (i + 1) * (G + 1) + 1)
                        dve.tensor_scalar(nmax[:, :], top1[:, :], -scale, None, ALU.mult).then_inc(mx, 1)

                    def finish(i):
                        dve.wait_ge(exp_done, i + 1)
                        dve.reciprocal(rinv[:, ds(i, 1)], rsum[:, ds(i, 1)]).then_inc(inv_done, 1)
                        dve.wait_ge(inv_done, i + 1)
                        if finish_act:
                            dve.wait_ge(f_act, i + 1)
                        else:
                            dve.wait_ge(pv_done, i + 1)
                        finish_dve(dve, i, ob, rinv[:, ds(i, 1)]).then_inc(o_free, 1)

                    query(0)
                    for g in range(G):
                        maximum(0, g)
                    whole_maximum(0)
                    query(1)

                    def turn(i, more):
                        for g in range(G):
                            low(i - 1, g)
                            maximum(i, g)
                        whole_maximum(i)
                        if more:
                            query(i + 1)
                        finish(i - 1)
                    with dve.Fori(1, nq - 1) as i:
                        turn(i, True)
                    turn(nq - 1, False)
                    for g in range(G):
                        low(nq - 1, g)
                    finish(nq - 1)

        def small(ctx, name, shape, dt=F32):
            return sb(ctx, name, shape, dt)

        def moe_phase():
            with ExitStack() as ph:
                XT_hi, XT_lo = split_pair(ph, "XT1", [P, DC, S])
                CW = sb(ph, "CW", [P, NT * (E + NSH)])
                ingest("i1", XT_hi, XT_lo)
                with ExitStack() as ctx:
                    W = weights(ctx, "wr", {"L0_ffn_router_wT": (DC, E)})
                    rh, rl = W["L0_ffn_router_wT"]
                    LG = sb(ctx, "LG", [P, NT, E])

                    def products(pe, bank, sh, sl):
                        for c in range(DC):
                            m = mm3(pe, bank[:, 0:E], sh[:, c, :], sl[:, c, :], rh[:, c, :], rl[:, c, :], c == 0, c == 1)
                        return m

                    def evac(dve, i, p, bank, own):
                        return dve.tensor_tensor(LG[:, ds(i, 1), :], bank[:, 0:E].unsqueeze(1), BIASE.unsqueeze(1), ALU.add)
                    slot_pass("rt", NT, DC, XT_hi, XT_lo, products, None, evac)

                    rank = sb(ctx, "rank", [P, NT, E])
                    ranki = sb(ctx, "ranki", [P, NT, E], I32)
                    t3, LG2, oh1, oh2 = (sb(ctx, n, [P, NT, E]) for n in ("t3", "LG2", "oh1", "oh2"))
                    m1, m2, tm, dd, ex, w1, w2 = (sb(ctx, n, [P, NT]) for n in ("m1", "m2", "tm", "dd", "ex", "w1", "w2"))
                    rk, ch, xp = sems(ctx, "rk rch rxp")
                    blk = ctx.enter_context(nc.Block())

                    def wide3(t):
                        return t[:, :].unsqueeze(2).to_broadcast([P, NT, E])

                    @blk.gpsimd
                    def _(pool):
                        pool.iota(ranki[:, :, :], pattern=[[0, NT], [-1, E]], base=E, channel_multiplier=0).then_inc(rk, 1)

                    @blk.scalar
                    def _(act):
                        act.wait_ge(xp, 1)
                        act.activation(ex[:, :], dd[:, :], ACT.Exp).then_inc(xp, 1)

                    @blk.vector
                    def _(dve):
                        count = [0]

                        def link(ins):
                            count[0] += 1
                            ins.then_inc(ch, 1)
                            dve.wait_ge(ch, count[0])

                        def first_of_largest(logits, m, oh):
                            link(dve.reduce_max(m[:, :], logits, AX))
                            link(dve.tensor_tensor(t3[:, :, :], logits, wide3(m), ALU.is_equal))
                            link(dve.tensor_tensor(t3[:, :, :], t3[:, :, :], rank[:, :, :], ALU.mult))
                            link(dve.reduce_max(tm[:, :], t3[:, :, :], AX))
                            link(dve.tensor_tensor(oh[:, :, :], rank[:, :, :], wide3(tm), ALU.is_equal))
                        dve.wait_ge(rk, 1)
                        link(dve.tensor_copy(rank[:, :, :], ranki[:, :, :]))
                        first_of_largest(LG[:, :, :], m1, oh1)
                        link(dve.scalar_tensor_tensor(out=LG2[:, :, :], in0=oh1[:, :, :], scalar=-BIG, in1=LG[:, :, :],
                                                      op0=ALU.mult, op1=ALU.add))
                        first_of_largest(LG2[:, :, :], m2, oh2)
                        dve.tensor_tensor(dd[:, :], m2[:, :], m1[:, :], ALU.subtract).then_inc(xp, 1)
                        dve.wait_ge(xp, 2)
                        link(dve.tensor_scalar(w1[:, :], ex[:, :], 1.0, None, ALU.add))
                        link(dve.reciprocal(w1[:, :], w1[:, :]))
                        link(dve.tensor_tensor(w2[:, :], ex[:, :], w1[:, :], ALU.mult))
                        link(dve.tensor_tensor(oh1[:, :, :], oh1[:, :, :], wide3(w1), ALU.mult))
                        link(dve.tensor_tensor(oh2[:, :, :], oh2[:, :, :], wide3(w2), ALU.mult))
                        cw = CW[:, :].rearrange("p (i e) -> p i e", e=E + NSH)
                        link(dve.tensor_tensor(cw[:, :, 0:E], oh1[:, :, :], oh2[:, :, :], ALU.add))
                        link(dve.memset(cw[:, :, E:E + NSH], 1.0))
                experts("me", E + NSH, A["w1T"], A["w3T"], A["w2T"], CW, E + NSH, 0, XT_hi, XT_lo)

        def cross_phase():
            with ExitStack() as ph:
                C2S = sb(ph, "C2S", [P, NT * D])
                scratch = nc.dram_tensor("s2c_rows", (1 + CP, D), F32, kind="Internal").ap()
                with ExitStack() as mid:
                    K_hi, K_lo = split_pair(mid, "K1", [P, DC, S])
                    V_hi, V_lo = split_pair(mid, "V1", [P, NT, D])
                    o_s2c = sb(mid, "o_s2c", [P, NC * D])

                    def keys_values(tag, n, src_hi, src_lo, k_name, v_name, bk):
                        with ExitStack() as ctx:
                            W = weights(ctx, tag + "w", {k_name: (DC, D), v_name: (DC, D)})
                            (kh, kl), (vh, vl) = W[k_name], W[v_name]

                            def products(pe, bank, sh, sl):
                                for h in range(DC):
                                    for c in range(DC):
                                        mm3(pe, bank[:, h * P:(h + 1) * P], kh[:, c, h * P:(h + 1) * P],
                                            kl[:, c, h * P:(h + 1) * P], sh[:, c, :], sl[:, c, :], c == 0, c == 1)
                                for c in range(DC):
                                    m = mm3(pe, bank[:, D:2 * D], sh[:, c, :], sl[:, c, :], vh[:, c, :], vl[:, c, :],
                                            c == 0, c == 1)
                                return m

                            def hi(act, i, p, bank, done):
                                for h in range(DC):
                                    act.activation(K_hi[:, h, ds(i * P, P)], bank[:, h * P:(h + 1) * P], ACT.Identity,
                                                   bias=bk[:, h:h + 1])
                                act.activation(V_hi[:, ds(i, 1), :], bank[:, D:2 * D].unsqueeze(1), ACT.Copy).then_inc(done, 1)

                            def lo(dve, i, p, bank, own):
                                for h in range(DC):
                                    k = K_hi[:, h, ds(i * P, P)].bitcast(F32)
                                    dve.scalar_tensor_tensor(out=K_lo[:, h, ds(i * P, P)], in0=bank[:, h * P:(h + 1) * P],
                                                             scalar=bk[:, h:h + 1], in1=k, op0=ALU.add, op1=ALU.subtract)
                                return dve.tensor_tensor(V_lo[:, ds(i, 1), :], bank[:, D:2 * D].unsqueeze(1),
                                                         V_hi[:, ds(i, 1), :].bitcast(F32), ALU.subtract)
                            slot_pass(tag, n, DC, src_hi, src_lo, products, hi, lo)

                    def finish_into(dst, bv):
                        def finish(dve, i, bank, rinv):
                            return dve.scalar_tensor_tensor(out=dst[:, ds(i * D, D)], in0=bank[:, 0:D], scalar=rinv, in1=bv,
                                                            op0=ALU.mult, op1=ALU.add)
                        return finish

                    scale = D ** -0.5
                    with ExitStack() as q1:
                        XT_hi, XT_lo = split_pair(q1, "XT2", [P, DC, S])
                        ingest("i2", XT_hi, XT_lo)
                        keys_values("ks", NC, CT_hi, CT_lo, "L1_xattn_Wk_sT", "L1_xattn_Wv_sT", BKS)
                        with ExitStack() as ctx:
                            W = weights(ctx, "wqc", {"L1_xattn_Wq_cT": (DC, D)})
                            attention("ac", NT, XT_hi, XT_lo, *W["L1_xattn_Wq_cT"], BQC, DC, scale, NC, C, K_hi, K_lo,
                                      V_hi, V_lo, D, None, finish_into(C2S, BV_S))
                        keys_values("kc", NT, XT_hi, XT_lo, "L1_xattn_Wk_cT", "L1_xattn_Wv_cT", BKC)
                    with ExitStack() as ctx:
                        W = weights(ctx, "wqs", {"L1_xattn_Wq_sT": (DC, D)})
                        attention("as", NC, CT_hi, CT_lo, *W["L1_xattn_Wq_sT"], BQS, DC, scale, NT, S, K_hi, K_lo,
                                  V_hi, V_lo, D, None, finish_into(o_s2c, BV_C))
                    with ExitStack() as ctx:
                        zrow = sb(ctx, "zrow", [1, D])
                        (zr, stc) = sems(ctx, "zr stc")
                        blk = ctx.enter_context(nc.Block())

                        @blk.vector
                        def _(dve):
                            dve.memset(zrow[:, :], 0.0).then_inc(zr, 1)

                        @blk.sync
                        def _(sp):
                            sp.dma_start(scratch[1:1 + CP, :].rearrange("(i p) d -> p i d", p=P),
                                         o_s2c[:, :].rearrange("p (i d) -> p i d", d=D)).then_inc(stc, 16)
                            sp.wait_ge(zr, 1)
                            sp.dma_start(scratch[0:1, :], zrow[:, :]).then_inc(stc, 16)
                            sp.wait_ge(stc, 32)

                STEP = P * C // S
                S2CI = sb(ph, "S2CI", [P, NT * D])
                with ExitStack() as ctx:
                    tent = sb(ctx, "tent", [P, NT * P], F32R)
                    with ExitStack() as c2:
                        posi = sb(c2, "posi", [P, S], I32)
                        keyi = sb(c2, "keyi", [P, S], I32)
                        pos = sb(c2, "pos", [P, S])
                        key = sb(c2, "key", [P, S])
                        io, cc, rr = sems(c2, "io icc irr")
                        blk = c2.enter_context(nc.Block())

                        @blk.gpsimd
                        def _(pool):
                            pool.iota(posi[:, :], pattern=[[2 * C, S]], base=C - S, channel_multiplier=0).then_inc(io, 1)
                            pool.iota(keyi[:, :], pattern=[[STEP, NT], [0, P]], base=-1, channel_multiplier=1).then_inc(io, 1)

                        @blk.vector
                        def _(dve):
                            dve.wait_ge(io, 2)
                            dve.tensor_copy(pos[:, :], posi[:, :]).then_inc(cc, 1)
                            dve.tensor_copy(key[:, :], keyi[:, :]).then_inc(cc, 1)
                            dve.wait_ge(cc, 2)
                            dve.tensor_scalar(pos[:, :], pos[:, :], 0.5 / S, 0.0, ALU.mult, ALU.max).then_inc(cc, 1)
                            dve.wait_ge(cc, 3)
                            dve.scalar_tensor_tensor(out=pos[:, :], in0=pos[:, :], scalar=float(C - 1), in1=key[:, :],
                                                     op0=ALU.min, op1=ALU.subtract).then_inc(cc, 1)

                        @blk.scalar
                        def _(act):
                            act.wait_ge(cc, 4)
                            act.activation(key[:, :], pos[:, :], ACT.Abs).then_inc(rr, 1)
                            act.wait_ge(rr, 1)
                            act.activation(tent[:, :], key[:, :], ACT.Relu, bias=1.0, scale=-1.0).then_inc(rr, 1)

                    win = sb(ctx, "win", [P, NT * D])
                    win_hi, win_lo = split_pair(ctx, "win", [P, NT * D])
                    t_slot = sb(ctx, "t_slot", [P, 2 * P], F32R)
                    wl, wh, wo, ts, md, de = sems(ctx, "w_l w_h w_o w_t w_md w_de")
                    blk = ctx.enter_context(nc.Block())

                    @blk.sync
                    def _(sp):
                        with sp.Fori(0, NT) as i:
                            sp.dma_start(win[:, ds(i * D, D)], scratch[ds(i * STEP, P), :]).then_inc(wl, 16)

                    @blk.scalar
                    def _(act):
                        act.wait_ge(wl, 16 * NT)
                        with act.Fori(0, NT) as i:
                            act.activation(win_hi[:, ds(i * D, D)], win[:, ds(i * D, D)], ACT.Copy).then_inc(wh, 1)

                    @blk.vector
                    def _(dve):
                        def fill(i, p):
                            dve.wait_ge(wh, i + 1)
                            dve.tensor_tensor(win_lo[:, ds(i * D, D)], win[:, ds(i * D, D)],
                                              win_hi[:, ds(i * D, D)].bitcast(F32), ALU.subtract)
                            dve.tensor_copy(t_slot[:, p * P:(p + 1) * P], tent[:, ds(i * P, P)]).then_inc(ts, 1)
                        fill(0, 0)
                        fill(1, 1)

                        def step(i, p, more):
                            dve.wait_ge(md, i + 1)
                            dve.tensor_copy(S2CI[:, ds(i * D, D)], banks[p][:, 0:D]).then_inc(de, 1)
                            if more:
                                fill(i + 2, p)
                        pairs(dve, NT, step)

                    @blk.tensor
                    def _(pe):
                        pe.sem_inc(de, 2)

                        def step(i, p, more):
                            pe.wait_ge(ts, i + 1)
                            pe.wait_ge(de, i + 1)
                            t = t_slot[:, p * P:(p + 1) * P]
                            pe.matmul(banks[p][:, 0:D], t, win_hi[:, ds(i * D, D)], start=True, stop=False)
                            pe.matmul(banks[p][:, 0:D], t, win_lo[:, ds(i * D, D)], start=False, stop=True).then_inc(md, 1)
                        pairs(pe, NT, step)

                with ExitStack() as ctx:
                    W = weights(ctx, "wg", {"L1_xattn_WgT": (2 * DC, D)})
                    gh, gl = W["L1_xattn_WgT"]
                    LGT = sb(ctx, "LGT", [P, NT * D])

                    def source(i):
                        return [C2S[:, ds(i * D, D)], S2CI[:, ds(i * D, D)]]

                    def products(pe, bank, sh, sl):
                        for c in range(2 * DC):
                            m = mm3(pe, bank[:, 0:D], sh[:, c, :], sl[:, c, :], gh[:, c, :], gl[:, c, :], c == 0, c == 3)
                        return m

                    def evac(dve, i, p, bank, own):
                        return dve.tensor_tensor(LGT[:, ds(i * D, D)], bank[:, 0:D], BG, ALU.add)
                    transpose_pass("gt", NT, 2 * DC, source, products, evac)

                    th = LGT
                    a, b, c = sems(ctx, "ga gb gc")
                    blk = ctx.enter_context(nc.Block())

                    @blk.scalar
                    def _(act):
                        with act.Fori(0, NT // 4) as i:
                            act.activation(th[:, ds(i * 4 * D, 4 * D)], LGT[:, ds(i * 4 * D, 4 * D)], ACT.Tanh,
                                           scale=0.5).then_inc(a, 1)

                    @blk.vector
                    def _(dve):
                        with dve.Fori(0, NT // 4) as i:
                            sl = ds(i * 4 * D, 4 * D)
                            dve.tensor_tensor(C2S[:, sl], C2S[:, sl], S2CI[:, sl], ALU.subtract).then_inc(b, 1)
                            dve.tensor_tensor(X[:, sl], X[:, sl], S2CI[:, sl], ALU.add).then_inc(b, 1)
                            dve.wait_ge(a, i + 1)
                            dve.wait_ge(b, i * 4 + 1)
                            dve.scalar_tensor_tensor(out=th[:, sl], in0=th[:, sl], scalar=1.0, in1=C2S[:, sl], op0=ALU.add,
                                                     op1=ALU.mult).then_inc(b, 1)
                            dve.wait_ge(b, i * 4 + 3)
                            dve.scalar_tensor_tensor(out=X[:, sl], in0=th[:, sl], scalar=0.5, in1=X[:, sl], op0=ALU.mult,
                                                     op1=ALU.add).then_inc(b, 1)

        def last_phase():
            with ExitStack() as ph:
                XT_hi, XT_lo = split_pair(ph, "XT3", [P, DC, S])
                ingest("i3", XT_hi, XT_lo)
                W = weights(ph, "wl", {"L1_ffn_gate_WT": (DC, E), "expert01T": (DC, 2 * D), "L1_ffn_out_WT": (DC, D)})
                SC = sb(ph, "SC", [P, 2, NT])
                FIN = sb(ph, "FIN", [P, NT * D])
                with ExitStack() as ctx:
                    rh, rl = W["L1_ffn_gate_WT"]
                    LG = sb(ctx, "LG3", [P, NT, E])
                    PR = sb(ctx, "PR3", [P, NT, E])

                    def products(pe, bank, sh, sl):
                        for c in range(DC):
                            m = mm3(pe, bank[:, 0:E], sh[:, c, :], sl[:, c, :], rh[:, c, :], rl[:, c, :], c == 0, c == 1)
                        return m

                    def evac(dve, i, p, bank, own):
                        return dve.tensor_copy(LG[:, ds(i, 1), :], bank[:, 0:E].unsqueeze(1))
                    slot_pass("gg", NT, DC, XT_hi, XT_lo, products, None, evac)
                    m1, sm, cn = (sb(ctx, n, [P, NT]) for n in ("m13", "sm3", "cn3"))
                    ch, xp = sems(ctx, "r3ch r3xp")
                    blk = ctx.enter_context(nc.Block())

                    def wide3(t):
                        return t[:, :].unsqueeze(2).to_broadcast([P, NT, E])

                    @blk.scalar
                    def _(act):
                        act.wait_ge(xp, 1)
                        act.activation(PR[:, :, :], LG[:, :, :], ACT.Exp).then_inc(xp, 1)

                    @blk.vector
                    def _(dve):
                        count = [0]

                        def link(ins):
                            count[0] += 1
                            ins.then_inc(ch, 1)
                            dve.wait_ge(ch, count[0])
                        link(dve.reduce_max(m1[:, :], LG[:, :, :], AX))
                        dve.tensor_tensor(LG[:, :, :], LG[:, :, :], wide3(m1), ALU.subtract).then_inc(xp, 1)
                        dve.wait_ge(xp, 2)
                        link(dve.reduce_sum(sm[:, :], PR[:, :, :], AX))
                        link(dve.reciprocal(sm[:, :], sm[:, :]))
                        link(dve.tensor_tensor(PR[:, :, :], PR[:, :, :], wide3(sm), ALU.mult))
                        link(dve.tensor_scalar(LG[:, :, :], PR[:, :, :], 0.3, None, ALU.is_gt))
                        link(dve.reduce_sum(cn[:, :], LG[:, :, :], AX))
                        link(dve.tensor_tensor(SC[:, 1, :], cn[:, :], PR[:, :, 1], ALU.mult))
                        link(dve.tensor_scalar(cn[:, :], cn[:, :], -1.0, float(E), ALU.mult, ALU.add))
                        link(dve.tensor_tensor(SC[:, 0, :], cn[:, :], PR[:, :, 0], ALU.mult))
                eh, el = W["expert01T"]
                with ExitStack() as ctx:
                    part = sb(ctx, "part3", [P, 2, D])

                    def products(pe, bank, sh, sl):
                        for c in range(DC):
                            m = mm3(pe, bank[:, :], sh[:, c, :], sl[:, c, :], eh[:, c, :], el[:, c, :], c == 0, c == 1)
                        return m

                    def hi(act, i, p, bank, done):
                        act.activation(part[:, p, :], bank[:, D:2 * D], ACT.Copy, scale=SC[:, 1, ds(i, 1)]).then_inc(done, 1)

                    def evac(dve, i, p, bank, own):
                        return dve.scalar_tensor_tensor(out=FIN[:, ds(i * D, D)], in0=bank[:, 0:D],
                                                        scalar=SC[:, 0, ds(i, 1)], in1=part[:, p, :], op0=ALU.mult,
                                                        op1=ALU.add)
                    slot_pass("ee", NT, DC, XT_hi, XT_lo, products, hi, evac)
                oh, ol = W["L1_ffn_out_WT"]

                def products(pe, bank, sh, sl):
                    for c in range(DC):
                        m = mm3(pe, bank[:, 0:D], sh[:, c, :], sl[:, c, :], oh[:, c, :], ol[:, c, :], c == 0, c == 1)
                    return m

                def evac(dve, i, p, bank, own):
                    x = X[:, ds(i * D, D)]
                    return dve.tensor_tensor(x, x, bank[:, 0:D], ALU.add)
                transpose_pass("oo", NT, DC, lambda i: [FIN[:, ds(i * D, D)]], products, evac)

        with ExitStack() as ph:
            XT_hi, XT_lo = split_pair(ph, "XT0", [P, DC, S])
            Wb_hi, Wb_lo = split_pair(ph, "W0", [P, 2064])
            Fx = sb(ph, "Fx", [P, NT * D])

            def part_of(t, off, kc, n):
                return t[:, off:off + kc * n].rearrange("p (c n) -> p c n", c=kc)
            spec0, off = {}, 0
            for name, kc, n in (("L0_xattn_Wq", 2, HA), ("L0_xattn_Wk", 2, HA), ("L0_xattn_Wv", 2, HA),
                                ("L0_xattn_WoT", 2, HA), ("L0_xattn_Wfc", 2, D), ("bo2", 2, P), ("Wof", 1, D)):
                spec0[name] = (off, kc, n)
                off += kc * n
            assert off <= 2064

            def w0(name):
                return part_of(Wb_hi, *spec0[name]), part_of(Wb_lo, *spec0[name])
            with ExitStack() as ctx:
                raw = sb(ctx, "raw0", [P, 2064])
                ctf = sb(ctx, "ctf", [P, DC, CP])
                ldw, ldc, ldx, ldv, hi, lo, z, pd, idn, aa, bb, st = sems(
                    ctx, "p_ldw p_ldc p_ldx p_ldv p_hi p_lo p_z p_pd p_idn p_aa p_bb p_st")
                blk = ctx.enter_context(nc.Block())
                wnames = [n for n in spec0 if n.startswith("L0")]
                nw = spec0["bo2"][0]

                @blk.sync
                def _(sp):
                    for name in wnames:
                        o, kc, n = spec0[name]
                        sp.dma_start(part_of(raw, o, kc, n), A[name].rearrange("(c p) n -> p c n", p=P)).then_inc(ldw, 16)
                    for c in range(DC):
                        sp.dma_start(ctf[:, c, 0:C], A["ctxT"][c * P:(c + 1) * P, :]).then_inc(ldc, 16)
                    sp.wait_ge(ldw, 16 * len(wnames))

                @blk.scalar
                def _(act):
                    for j, (t, name) in enumerate(((BO, "L0_xattn_bo"), (BQC, "L1_xattn_bq_c"), (BKS, "L1_xattn_bk_s"),
                                                   (BQS, "L1_xattn_bq_s"), (BKC, "L1_xattn_bk_c"))):
                        act.dma_start(t, A[name]).then_inc(ldv, 16)
                    for j in range(4):
                        act.dma_start(X[:, j * 4 * D:(j + 1) * 4 * D].rearrange("p (i d) -> p i d", d=D),
                                      A["x"][0, j * 512:(j + 1) * 512, :].rearrange("(i p) d -> p i d", p=P)).then_inc(ldx, 16)
                    for t, name in ((GAMMA, "L0_xattn_ln_gamma"), (BETA, "L0_xattn_ln_beta"), (BV_S, "L1_xattn_bv_s"),
                                    (BV_C, "L1_xattn_bv_c"), (BG, "L1_xattn_bg"), (BIASE, "L0_ffn_expert_bias")):
                        act.dma_start(t, A[name].partition_broadcast(P)).then_inc(ldv, 16)
                    act.wait_ge(ldv, 16 * 11)
                    act.wait_ge(ldx, 64)
                    act.wait_ge(z, 2)
                    act.wait_ge(ldw, 16 * len(wnames))
                    for c in range(DC):
                        act.activation(raw[:, nw + c * P:nw + (c + 1) * P], ident[:, :], ACT.Identity,
                                       bias=BO[:, c:c + 1], scale=0.0).then_inc(z, 1)
                    act.wait_ge(z, 4)
                    act.activation(Wb_hi[:, 0:nw + 2 * P], raw[:, 0:nw + 2 * P], ACT.Copy).then_inc(hi, 1)
                    act.wait_ge(ldc, 32)
                    act.wait_ge(pd, 1)
                    for c in range(DC):
                        act.activation(CT_hi[:, c, :], ctf[:, c, :], ACT.Copy).then_inc(hi, 1)
                    act.wait_ge(aa, 1)
                    o, _, n = spec0["Wof"]
                    act.activation(Wb_hi[:, o:o + n], banks[0][:, 0:D], ACT.Copy).then_inc(hi, 1)

                @blk.gpsimd
                def _(pool):
                    pool.memset(ident[:, :], 0.0).then_inc(idn, 1)
                    pool.memset(mhalf[:, :], -0.5).then_inc(z, 1)
                    pool.wait_ge(idn, 1)
                    pool.affine_select(out=ident[:, :], in_=ident[:, :], compare_op=ALU.not_equal, fill=1.0, base=0,
                                       pattern=[[-1, P]], channel_multiplier=1).then_inc(z, 1)

                @blk.vector
                def _(dve):
                    dve.memset(ctf[:, :, C:CP], 0.0).then_inc(pd, 1)
                    dve.wait_ge(hi, 1)
                    dve.tensor_tensor(Wb_lo[:, 0:nw + 2 * P], raw[:, 0:nw + 2 * P], Wb_hi[:, 0:nw + 2 * P].bitcast(F32),
                                      ALU.subtract).then_inc(lo, 1)
                    for c in range(DC):
                        dve.wait_ge(hi, c + 2)
                        dve.tensor_tensor(CT_lo[:, c, :], ctf[:, c, :], CT_hi[:, c, :].bitcast(F32),
                                          ALU.subtract).then_inc(lo, 1)
                    dve.wait_ge(aa, 2)
                    dve.tensor_copy(BFC, banks[1][:, 0:D]).then_inc(lo, 1)
                    dve.wait_ge(hi, 4)
                    o, _, n = spec0["Wof"]
                    dve.tensor_tensor(Wb_lo[:, o:o + n], banks[0][:, 0:D], Wb_hi[:, o:o + n].bitcast(F32),
                                      ALU.subtract).then_inc(lo, 1)

                @blk.tensor
                def _(pe):
                    pe.wait_ge(hi, 1)
                    pe.wait_ge(lo, 1)
                    (ah, al), (fh, fl), (bh, bl) = w0("L0_xattn_WoT"), w0("L0_xattn_Wfc"), w0("bo2")
                    for c in range(DC):
                        m = mm3(pe, banks[0][:, 0:D], ah[:, c, :], al[:, c, :], fh[:, c, :], fl[:, c, :], c == 0, c == 1)
                    m.then_inc(aa, 1)
                    for c in range(DC):
                        m = mm3(pe, banks[1][:, 0:D], bh[:, c, :], bl[:, c, :], fh[:, c, :], fl[:, c, :], c == 0, c == 1)
                    m.then_inc(aa, 1)

            ingest("i0", XT_hi, XT_lo)

            fch, fcl = w0("L0_xattn_Wfc")

            def fc_products(pe, bank, sh, sl):
                for c in range(DC):
                    m = mm3(pe, bank[:, 0:D], sh[:, c, :], sl[:, c, :], fch[:, c, :], fcl[:, c, :], c == 0, c == 1)
                return m

            def fc_out(dve, i, p, bank, own):
                return dve.tensor_tensor(Fx[:, ds(i * D, D)], bank[:, 0:D], BFC, ALU.add)
            slot_pass("f0", NT, DC, XT_hi, XT_lo, fc_products, None, fc_out)

            with ExitStack() as at:
                K_hi, K_lo = split_pair(at, "K0", [P, 1, CP])
                V_hi, V_lo = split_pair(at, "V0", [P, NC, HA])
                CX_hi, CX_lo = split_pair(at, "CX", [P, 1, S])
                kh, kl = w0("L0_xattn_Wk")
                vh, vl = w0("L0_xattn_Wv")

                def kv_products(pe, bank, sh, sl):
                    for c in range(DC):
                        mm3(pe, bank[:, 0:P], kh[:, c, :], kl[:, c, :], sh[:, c, :], sl[:, c, :], c == 0, c == 1)
                    for c in range(DC):
                        m = mm3(pe, bank[:, P:2 * P], sh[:, c, :], sl[:, c, :], vh[:, c, :], vl[:, c, :], c == 0, c == 1)
                    return m

                def kv_hi(act, i, p, bank, done):
                    act.activation(K_hi[:, 0, ds(i * P, P)], bank[:, 0:P], ACT.Copy)
                    act.activation(V_hi[:, ds(i, 1), :], bank[:, P:2 * P].unsqueeze(1), ACT.Copy).then_inc(done, 1)

                def kv_lo(dve, i, p, bank, own):
                    dve.tensor_tensor(K_lo[:, 0, ds(i * P, P)], bank[:, 0:P], K_hi[:, 0, ds(i * P, P)].bitcast(F32),
                                      ALU.subtract)
                    return dve.tensor_tensor(V_lo[:, ds(i, 1), :], bank[:, P:2 * P].unsqueeze(1),
                                             V_hi[:, ds(i, 1), :].bitcast(F32), ALU.subtract)
                slot_pass("kv0", NC, DC, CT_hi, CT_lo, kv_products, kv_hi, kv_lo)

                RI = sb(at, "RI", [P, NT])

                def ctx_hi(act, i, bank):
                    return act.activation(CX_hi[:, 0, ds(i * P, P)], bank[:, 0:P], ACT.Copy)

                def ctx_lo(dve, i, bank, rinv):
                    dve.tensor_copy(RI[:, ds(i, 1)], rinv)
                    return dve.tensor_tensor(CX_lo[:, 0, ds(i * P, P)], bank[:, 0:P],
                                             CX_hi[:, 0, ds(i * P, P)].bitcast(F32), ALU.subtract)
                attention("a0", NT, XT_hi, XT_lo, *w0("L0_xattn_Wq"), None, 1, HA ** -0.5, NC, C, K_hi, K_lo, V_hi, V_lo,
                          HA, ctx_hi, ctx_lo)

                wofh, wofl = w0("Wof")

                def of_products(pe, bank, sh, sl):
                    return mm3(pe, bank[:, 0:D], sh[:, 0, :], sl[:, 0, :], wofh[:, 0, :], wofl[:, 0, :], True, True)

                def of_out(dve, i, p, bank, own):
                    z = Fx[:, ds(i * D, D)]
                    return dve.scalar_tensor_tensor(out=z, in0=bank[:, 0:D], scalar=RI[:, ds(i, 1)], in1=z,
                                                    op0=ALU.mult, op1=ALU.add)
                slot_pass("of", NT, 1, CX_hi, CX_lo, of_products, None, of_out)

            with ExitStack() as ctx:
                zn = sb(ctx, "zn", [P, 2 * D])
                a, b, c, d, e = sems(ctx, "ya yb yc yd ye")
                blk = ctx.enter_context(nc.Block())

                @blk.gpsimd
                def _(pool):
                    pool.wait_ge(c, 2 * NT)
                    pool.tensor_scalar(RSTD[:, :], MV[:, 1::2], EPS, None, ALU.add).then_inc(a, 1)
                    pool.wait_ge(a, 1)
                    pool.tensor_tensor(RSTD[:, :], RSTD[:, :], mhalf[:, :], ALU.pow).then_inc(a, 1)

                @blk.vector
                def _(dve):
                    row_statistics(dve, Fx, c)
                    dve.wait_ge(a, 2)
                    dve.wait_ge(c, 2 * NT)

                    def step(i, p, more):
                        z = zn[:, p * D:(p + 1) * D]
                        x = X[:, ds(i * D, D)]
                        dve.tensor_scalar(z, Fx[:, ds(i * D, D)], MV[:, ds(2 * i, 1)], RSTD[:, ds(i, 1)], ALU.subtract,
                                          ALU.mult).then_inc(b, 1)
                        dve.tensor_tensor(x, x, BETA, ALU.add).then_inc(b, 1)
                        dve.wait_ge(b, i * 4 + 1)
                        dve.tensor_tensor(z, z, GAMMA, ALU.mult).then_inc(b, 1)
                        dve.wait_ge(b, i * 4 + 3)
                        dve.tensor_tensor(x, x, z, ALU.add).then_inc(b, 1)
                    pairs(dve, NT, step)

        moe_phase()
        cross_phase()
        last_phase()

        with ExitStack() as ctx:
            (stored,) = sems(ctx, "stored")
            blk = ctx.enter_context(nc.Block())

            @blk.sync
            def _(sp):
                for j in range(4):
                    sp.dma_start(out[0, j * 512:(j + 1) * 512, :].rearrange("(i p) d -> p i d", p=P),
                                 X[:, j * 4 * D:(j + 1) * 4 * D].rearrange("p (i d) -> p i d", d=D)).then_inc(stored, 16)
                sp.wait_ge(stored, 64)


_HOST_TRANSPOSED = {"L0_xattn_WoT": "L0_xattn_Wo", **{n + "T": n for n in (
    "L0_ffn_router_w", "L1_xattn_Wq_c", "L1_xattn_Wk_s", "L1_xattn_Wv_s", "L1_xattn_Wq_s", "L1_xattn_Wk_c",
    "L1_xattn_Wv_c", "L1_xattn_Wg", "L1_ffn_gate_W", "L1_ffn_out_W")}}
_IN_COLUMNS = ("L0_xattn_bo", "L1_xattn_bq_c", "L1_xattn_bk_s", "L1_xattn_bq_s", "L1_xattn_bk_c")


def kernel(**inputs):
    import numpy as _np
    import concourse.bacc as _bacc
    from concourse import mybir as _mybir
    from concourse.bass_utils import run_bass_kernel_spmd as _run

    nc = _bacc.Bacc("TRN2", target_bir_lowering=False, num_devices=1)
    laid_out = {k: _np.asarray(v) for k, v in inputs.items()}
    laid_out["ctxT"] = laid_out.pop("ctx_1024")[0].T
    for new, old in _HOST_TRANSPOSED.items():
        laid_out[new] = _np.swapaxes(laid_out.pop(old), -1, -2)
    for name in _IN_COLUMNS:
        laid_out[name] = laid_out[name].reshape(D // P, P).T
    for new, old in (("w1T", "w1"), ("w3T", "w3"), ("w2T", "w2")):
        laid_out[new] = _np.swapaxes(_np.concatenate(
            (laid_out.pop("L0_ffn_" + old), laid_out.pop("L0_ffn_s" + old))), -1, -2)
    laid_out["expert01T"] = laid_out.pop("L1_ffn_expert_W")[:2].reshape(2 * D, D).T
    arrays, aps = {}, {}
    for name, a in laid_out.items():
        arrays[name] = _np.ascontiguousarray(a)
        aps[name] = nc.dram_tensor(name, a.shape, _mybir.dt.from_np(a.dtype), kind="ExternalInput").ap()
    out = nc.dram_tensor("out", (1, S, D), _mybir.dt.float32, kind="ExternalOutput").ap()
    build(nc, aps, out)
    r = _run(nc, [arrays], core_ids=[0])
    return r.results[0]["out"]
```

```python
import concourse.bass as bass
from concourse import mybir
from contextlib import ExitStack

F32 = mybir.dt.float32
F32R = mybir.dt.float32r
I32 = mybir.dt.int32
ALU = mybir.AluOpType
ACT = mybir.ActivationFunctionType
AX = mybir.AxisListType.X
ds = bass.ds

P = 128
D = 256
DC = D // P
S = 2048
NT = S // P
C = 1601
NC = -(-C // P)
CP = NC * P
HA = 128
E = 8
NSH = 2
F = 512
EPS = 1e-5
BIG = 3.0e38
RT = 256
NR = (2 * S + E * (RT - 1)) // RT


def pairs(eng, n, body):
    main = (n - 2) // 2 * 2
    if main > 0:
        with eng.Fori(0, main // 2) as j:
            body(j * 2, 0, True)
            body(j * 2 + 1, 1, True)
    for i in range(main, n):
        body(i, i % 2, i + 2 < n)


def pairs3(eng, n, body):
    main = (n - 3) // 2 * 2
    with eng.Fori(0, main // 2) as j:
        body(j * 2, 0, 4)
        body(j * 2 + 1, 1, 4)
    for i in range(main, n):
        body(i, i % 2, n - i)


def mm3(pe, out, wh, wl, xh, xl, first, last):
    pe.matmul(out, wh, xh, start=first, stop=False)
    pe.matmul(out, wh, xl, start=False, stop=False)
    return pe.matmul(out, wl, xh, start=False, stop=last)


def build(nc, A, out):
    top = ExitStack()
    with top:
        def sb(ctx, name, shape, dt=F32):
            return ctx.enter_context(nc.sbuf_tensor(name, shape, dt))

        def split_pair(ctx, name, shape):
            return sb(ctx, name + "_hi", shape, F32R), sb(ctx, name + "_lo", shape, F32R)

        banks = [top.enter_context(nc.psum_tensor(f"bank{i}", [P, 512], F32)) for i in range(0, 4)]
        wide = top.enter_context(nc.psum_tensor("wide", [P, 4 * 512], F32))

        X = sb(top, "X", [P, NT * D])
        ident = sb(top, "ident", [P, P])
        MV = sb(top, "MV", [P, 2 * NT])
        RSTD = sb(top, "RSTD", [P, NT])
        mhalf = sb(top, "mhalf", [P, NT])
        stats = sb(top, "stats", [P, 6 * NT])
        rows = sb(top, "rows", [P, 9 * D])
        GAMMA, BETA, BFC, BV_S, BV_C, BG = (rows[:, j * D:(j + 1) * D] for j in range(6))
        BIASE = rows[:, 6 * D:6 * D + E]
        cols = sb(top, "cols", [P, 16])
        BO, BQC, BKS, BQS, BKC = (cols[:, 2 * j:2 * j + 2] for j in range(5))
        CT_hi, CT_lo = split_pair(top, "CT", [P, DC, CP])

        free_sems = [nc.alloc_semaphore(f"signal{i}") for i in range(140)]

        def sems(ctx, names):
            got = [free_sems.pop(0) for _ in names.split()]

            def give_back():
                for s in got:
                    nc.gpsimd.sem_clear(s)
                free_sems.extend(got)
            ctx.callback(give_back)
            return got


        def row_statistics(dve, src, st):
            def one(i, p, more):
                dve.bn_stats(out=stats[:, ds(i * 6, 6)], in_=src[:, ds(i * D, D)]).then_inc(st, 1)
            pairs(dve, NT, one)
            dve.wait_ge(st, NT)
            for i in range(NT):
                dve.bn_aggr(out=MV[:, 2 * i:2 * i + 2], in_=stats[:, 6 * i:6 * i + 6]).then_inc(st, 1)

        def split_phase(tag, items):
            with ExitStack() as ctx:
                loaded = sems(ctx, " ".join(f"{tag}ld{j}" for j in range(len(items))))
                hi_done, lo_done = sems(ctx, f"{tag}hi {tag}lo")
                blk = ctx.enter_context(nc.Block())

                @blk.sync
                def _(sp):
                    for j, (dram, raw, hi, lo) in enumerate(items):
                        sp.dma_start(raw, dram.rearrange("(c p) n -> p c n", p=P)).then_inc(loaded[j], 16)

                @blk.scalar
                def _(act):
                    for j, (dram, raw, hi, lo) in enumerate(items):
                        act.wait_ge(loaded[j], 16)
                        act.activation(hi, raw, ACT.Copy).then_inc(hi_done, 1)

                @blk.vector
                def _(dve):
                    for j, (dram, raw, hi, lo) in enumerate(items):
                        dve.wait_ge(hi_done, j + 1)
                        dve.tensor_tensor(lo, raw, hi.bitcast(F32), ALU.subtract).then_inc(lo_done, 1)

        def weights(ctx, tag, spec):
            total = sum(kc * n for kc, n in spec.values())
            raw = sb(ctx, tag + "raw", [P, total])
            hi, lo = split_pair(ctx, tag, [P, total])
            items, at, off = [], {}, 0
            for name, (kc, n) in spec.items():
                r, h, l = (t[:, off:off + kc * n].rearrange("p (c n) -> p c n", c=kc) for t in (raw, hi, lo))
                items.append((A[name], r, h, l))
                at[name] = (h, l)
                off += kc * n
            split_phase(tag, items)
            return at

        def transpose_pass(tag, n, kc, source, products, evac, prepare=None):
            with ExitStack() as ctx:
                t_in = sb(ctx, tag + "tin", [P, 2, kc, P])
                s_hi, s_lo = split_pair(ctx, tag + "slot", [P, 2, kc, P])
                fi, td, hd, ld, md, de = sems(ctx, " ".join(tag + s for s in "fi td hd ld md de".split()))
                (own,) = sems(ctx, tag + "own")
                blk = ctx.enter_context(nc.Block())

                @blk.vector
                def _(dve):
                    def fill(i, p):
                        parts = source(i)
                        for j, x in enumerate(parts):
                            w = kc // len(parts)
                            dve.tensor_copy(t_in[:, p, j * w:(j + 1) * w, :],
                                            x.rearrange("p (c n) -> p c n", c=w)).then_inc(fi, 1)

                    def low(i, p):
                        dve.wait_ge(hd, i + 1)
                        dve.tensor_tensor(s_lo[:, p, :, :], banks[p][:, 0:kc * P].rearrange("p (c n) -> p c n", c=kc),
                                          s_hi[:, p, :, :].bitcast(F32), ALU.subtract).then_inc(ld, 1)
                    fill(0, 0)
                    fill(1, 1)
                    low(0, 0)
                    fill(2, 0)

                    def step(i, p, left):
                        if left > 1:
                            low(i + 1, 1 - p)
                        if left > 3:
                            fill(i + 3, 1 - p)
                        dve.wait_ge(md, i + 1)
                        evac(dve, i, p, banks[2 + p], own).then_inc(de, 1)
                    pairs3(dve, n, step)

                @blk.scalar
                def _(act):
                    def step(i, p, more):
                        act.wait_ge(td, i + 1)
                        act.activation(s_hi[:, p, :, :], banks[p][:, 0:kc * P].rearrange("p (c n) -> p c n", c=kc),
                                       ACT.Copy).then_inc(hd, 1)
                        if prepare:
                            prepare(act, i, p, own)
                    pairs(act, n, step)

                @blk.tensor
                def _(pe):
                    pe.sem_inc(de, 2)
                    parts = len(source(0))

                    def transposes(i, p):
                        pe.wait_ge(fi, parts * (i + 1))
                        for c in range(kc):
                            t = pe.transpose(banks[p][:, c * P:(c + 1) * P], t_in[:, p, c, :], ident[:, :])
                        t.then_inc(td, 1)
                    transposes(0, 0)
                    transposes(1, 1)

                    def step(i, p, more):
                        pe.wait_ge(ld, i + 1)
                        pe.wait_ge(de, i + 1)
                        products(pe, banks[2 + p], s_hi[:, p, :, :], s_lo[:, p, :, :]).then_inc(md, 1)
                        if more:
                            transposes(i + 2, p)
                    pairs(pe, n, step)

        def shared_expert(tag, e, XT_hi, XT_lo, on_pool=None, after=None):
            NB, FC, TB = S // 512, F // P, 4
            W = DC * F * 2 + FC * D
            with ExitStack() as ctx:
                raw = sb(ctx, tag + "raw", [P, W])
                w_hi, w_lo = split_pair(ctx, tag + "w", [P, W])
                sil = sb(ctx, tag + "sil", [P, 2, 512])
                gate = sb(ctx, tag + "gate", [P, 2, 512])
                g_hi, g_lo = split_pair(ctx, tag + "g", [P, FC, 512])
                (ld1, ld3, ld2, whi, wlo, hd, sd, gd, ghi, glo, yd, yf) = sems(
                    ctx, " ".join(tag + s for s in "ld1 ld3 ld2 whi wlo hd sd gd ghi glo yd yf".split()))
                blk = ctx.enter_context(nc.Block())
                loads = (ld1, ld3, ld2)

                def up(t, which, c, m):
                    o = which * DC * F + c * F + m * P
                    return t[:, o:o + P]

                def down(t, m):
                    o = 2 * DC * F + m * D
                    return t[:, o:o + D]

                def piece(t, k):
                    return t[:, k * DC * F:(k + 1) * DC * F]

                @blk.sync
                def _(sp):
                    for k, w in enumerate(("w1T", "w3T", "w2T")):
                        sp.dma_start(piece(raw, k).rearrange("p (c n) -> p c n", n=F if k < 2 else D),
                                     A[w][e].rearrange("(c p) n -> p c n", p=P)).then_inc(loads[k], 16)

                if on_pool:
                    blk.gpsimd(on_pool)

                @blk.scalar
                def _(act):
                    for k in range(3):
                        act.wait_ge(loads[k], 16)
                        act.activation(piece(w_hi, k), piece(raw, k), ACT.Copy).then_inc(whi, 1)

                    def hi(n0, c):
                        act.wait_ge(gd, n0 + 1 + 2)
                        act.activation(g_hi[:, c, :], gate[:, c % 2, :], ACT.Copy).then_inc(ghi, 1)

                    with act.Fori(0, NB) as b:
                        for c in range(FC):
                            n0 = b * FC + c
                            act.wait_ge(hd, n0 + 1)
                            act.activation(sil[:, c % 2, :], banks[2 * (c % 2)][:, :], ACT.Silu).then_inc(sd, 1)
                            if c:
                                hi(n0 - 1, c - 1)
                        hi(b * FC + FC - 1, FC - 1)

                @blk.vector
                def _(dve):
                    for k in range(3):
                        dve.wait_ge(whi, k + 1)
                        dve.tensor_tensor(piece(w_lo, k), piece(raw, k), piece(w_hi, k).bitcast(F32),
                                          ALU.subtract).then_inc(wlo, 1)

                    def lo(n0, c):
                        dve.wait_ge(ghi, n0 + 1)
                        dve.tensor_tensor(g_lo[:, c, :], gate[:, c % 2, :], g_hi[:, c, :].bitcast(F32),
                                          ALU.subtract).then_inc(glo, 1)

                    with dve.Fori(0, NB) as b:
                        for c in range(FC):
                            n0 = b * FC + c
                            dve.wait_ge(glo, n0 + 1)
                            dve.wait_ge(sd, n0 + 1)
                            dve.tensor_tensor(gate[:, c % 2, :], sil[:, c % 2, :], banks[2 * (c % 2) + 1][:, :],
                                              ALU.mult).then_inc(gd, 1)
                            if c:
                                lo(n0 - 1, c - 1)
                        lo(b * FC + FC - 1, FC - 1)
                        dve.wait_ge(yd, b + 1)
                        for t in range(TB):
                            x = X[:, ds((b * TB + t) * D, D)]
                            m = dve.tensor_tensor(x, x, wide[:, 512 * t:512 * t + D], ALU.add)
                        m.then_inc(yf, 1)
                    if after:
                        after(dve, yf, NB + 1)

                @blk.tensor
                def _(pe):
                    pe.sem_inc(yf, 1)
                    pe.sem_inc(glo, 2)
                    pe.sem_inc(gd, 2)
                    pe.wait_ge(wlo, 3)

                    def hidden(b, c):
                        pe.wait_ge(gd, b * FC + c + 1)
                        for which in range(2):
                            for k in range(DC):
                                m = mm3(pe, banks[2 * (c % 2) + which][:, :], up(w_hi, which, k, c),
                                        up(w_lo, which, k, c), XT_hi[:, k, ds(b * 512, 512)],
                                        XT_lo[:, k, ds(b * 512, 512)], k == 0, k == DC - 1)
                        m.then_inc(hd, 1)

                    def result(b, c):
                        if c == 0:
                            pe.wait_ge(yf, b + 1)
                        pe.wait_ge(glo, b * FC + c + 1 + 2)
                        for t in range(TB):
                            m = mm3(pe, wide[:, 512 * t:512 * t + D], g_hi[:, c, t * P:(t + 1) * P],
                                    g_lo[:, c, t * P:(t + 1) * P], down(w_hi, c), down(w_lo, c),
                                    c == 0, c == FC - 1)
                        if c == FC - 1:
                            m.then_inc(yd, 1)

                    with pe.Fori(0, NB) as b:
                        for c in range(FC):
                            hidden(b, c)
                            if c >= 2:
                                result(b, c - 2)
                        result(b, FC - 2)
                        result(b, FC - 1)

        def routed_experts(table, rows_in, rows_out):
            FC, TB = F // P, RT // P
            NP = (NR - 1) // 2
            assert NR == 2 * NP + 1
            W = DC * F * 2 + FC * D
            with ExitStack() as ctx:
                raw = sb(ctx, "rraw", [P, W])
                w_hi, w_lo = split_pair(ctx, "rw", [P, 2, W])
                xr = sb(ctx, "rxr", [P, 2, TB, D])
                x_hi, x_lo = split_pair(ctx, "rx", [P, 2, DC, RT])
                sil = sb(ctx, "rsil", [P, 2, RT])
                gate = sb(ctx, "rgate", [P, 2, RT])
                g_hi, g_lo = split_pair(ctx, "rg", [P, FC, RT])
                ys = sb(ctx, "rys", [P, 2, TB * D])
                (l0, l1, l2, xl0, xl1, td, xhi, xlo, whi, w0, w1, w2, hd, sd, gd, ghi, glo, yd, ye, stored, ysf) = sems(
                    ctx, " ".join(f"r{i}" for i in range(21)))
                loaded, split_done, rows_in_done = (l0, l1, l2), (w0, w1, w2), (xl0, xl1)
                blk = ctx.enter_context(nc.Block())
                tbank = banks[2]

                def up(t, par, which, c, m):
                    o = which * DC * F + c * F + m * P
                    return t[:, par, o:o + P]

                def down(t, par, m):
                    o = 2 * DC * F + m * D
                    return t[:, par, o:o + D]

                def over_tiles(eng, body):
                    body(0, 0, 0, True)
                    with eng.Fori(0, NP) as k:
                        body(k * 2 + 1, 1, k, False)
                        body(k * 2 + 2, 0, k + 1, False)

                @blk.sync
                def _(sp):
                    def load(j, par, first):
                        e = sp.value_load(table[0:1, ds(j, 1)] if not first else table[0:1, j:j + 1], min_val=0, max_val=E - 1)
                        sp.wait_ge(td, j + 1)
                        sp.dma_start(xr[:, par, :, :], rows_in[ds(j * RT, RT), :].rearrange("(t p) d -> p t d", p=P))\
                          .then_inc(rows_in_done[par], 16)
                        for k, w in enumerate(("w1T", "w3T", "w2T")):
                            if not first:
                                sp.wait_ge(split_done[k], j)
                            sp.dma_start(raw[:, k * DC * F:(k + 1) * DC * F].rearrange("p (c n) -> p c n", n=F if k < 2 else D),
                                         A[w][ds(e, 1), :, :].rearrange("a (c p) n -> p (a c) n", p=P))\
                              .then_inc(loaded[k], 16)
                    load(0, 0, True)
                    with sp.Fori(0, NP) as k:
                        load(k * 2 + 1, 1, False)
                        load(k * 2 + 2, 0, False)
                    load(NR, 1, False)

                @blk.gpsimd
                def _(pool):
                    pool.sem_inc(ysf, 2)

                    def store(j, par, half, first):
                        pool.wait_ge(ye, j + 1 + 1)
                        pool.wait_ge(yd, 1)
                        pool.dma_start(rows_out[ds(j * RT, RT), :].rearrange("(t p) d -> p t d", p=P),
                                       ys[:, par, :].rearrange("p (t d) -> p t d", d=D)).then_inc(stored, 16)
                        pool.wait_ge(stored, 16 * (j + 1))
                        pool.sem_inc(ysf, 1)
                    over_tiles(pool, store)

                @blk.scalar
                def _(act):
                    def split(j, par, k):
                        act.wait_ge(loaded[k], 16 * (j + 1))
                        act.activation(w_hi[:, par, k * DC * F:(k + 1) * DC * F], raw[:, k * DC * F:(k + 1) * DC * F],
                                       ACT.Copy).then_inc(whi, 1)

                    def rows(j, par):
                        act.wait_ge(td, j + 1 + 2)
                        act.activation(x_hi[:, par, :, :], tbank[:, :].rearrange("p (c n) -> p c n", c=DC),
                                       ACT.Copy).then_inc(xhi, 1)

                    def silu(j, c):
                        act.wait_ge(hd, j * FC + c + 1)
                        act.activation(sil[:, c % 2, :], banks[c % 2][:, 0:RT], ACT.Silu).then_inc(sd, 1)

                    def hi(j, c):
                        act.wait_ge(gd, j * FC + c + 1 + 2)
                        act.activation(g_hi[:, c, :], gate[:, c % 2, :], ACT.Copy).then_inc(ghi, 1)
                    rows(0, 0)
                    for k in range(3):
                        split(0, 0, k)

                    def tile(j, par, half, first):
                        silu(j, 0)
                        split(j + 1, 1 - par, 0)
                        silu(j, 1)
                        hi(j, 0)
                        split(j + 1, 1 - par, 1)
                        silu(j, 2)
                        hi(j, 1)
                        rows(j + 1, 1 - par)
                        silu(j, 3)
                        hi(j, 2)
                        if not first:
                            act.wait_ge(yd, j)
                        split(j + 1, 1 - par, 2)
                        hi(j, 3)
                    over_tiles(act, tile)

                @blk.vector
                def _(dve):
                    def split(j, par, k):
                        dve.wait_ge(whi, j * 3 + k + 1)
                        dve.tensor_tensor(w_lo[:, par, k * DC * F:(k + 1) * DC * F], raw[:, k * DC * F:(k + 1) * DC * F],
                                          w_hi[:, par, k * DC * F:(k + 1) * DC * F].bitcast(F32),
                                          ALU.subtract).then_inc(split_done[k], 1)

                    def rows(j, par):
                        dve.wait_ge(xhi, j + 1)
                        dve.tensor_tensor(x_lo[:, par, :, :], tbank[:, :].rearrange("p (c n) -> p c n", c=DC),
                                          x_hi[:, par, :, :].bitcast(F32), ALU.subtract).then_inc(xlo, 1)

                    def gated(j, c):
                        dve.wait_ge(glo, j * FC + c + 1)
                        dve.wait_ge(sd, j * FC + c + 1)
                        dve.tensor_tensor(gate[:, c % 2, :], sil[:, c % 2, :], banks[c % 2][:, RT:2 * RT],
                                          ALU.mult).then_inc(gd, 1)

                    def lo(j, c):
                        dve.wait_ge(ghi, j * FC + c + 1)
                        dve.tensor_tensor(g_lo[:, c, :], gate[:, c % 2, :], g_hi[:, c, :].bitcast(F32),
                                          ALU.subtract).then_inc(glo, 1)

                    def results(j, par, half):
                        dve.wait_ge(yd, j + 1)
                        dve.wait_ge(ysf, j + 1)
                        dve.tensor_copy(ys[:, par, :].rearrange("p (t d) -> p t d", d=D),
                                        wide[:, 0:512 * TB].rearrange("p (t n) -> p t n", n=512)[:, :, 0:D]).then_inc(ye, 1)
                    rows(0, 0)
                    for k in range(3):
                        split(0, 0, k)

                    def tile(j, par, half, first):
                        gated(j, 0)
                        split(j + 1, 1 - par, 0)
                        gated(j, 1)
                        lo(j, 0)
                        split(j + 1, 1 - par, 1)
                        if not first:
                            results(j - 1, 1 - par, half - 1 if par == 0 else half)
                        gated(j, 2)
                        lo(j, 1)
                        rows(j + 1, 1 - par)
                        gated(j, 3)
                        lo(j, 2)
                        split(j + 1, 1 - par, 2)
                        lo(j, 3)
                    over_tiles(dve, tile)
                    results(NR - 1, 0, NP)

                @blk.tensor
                def _(pe):
                    pe.sem_inc(td, 2)
                    pe.sem_inc(glo, 2)
                    pe.sem_inc(gd, 2)
                    pe.sem_inc(ye, 1)

                    def transposes(j, par, half):
                        pe.wait_ge(rows_in_done[par], 16 * (half + 1))
                        for c in range(DC):
                            for t in range(TB):
                                o = c * RT + t * P
                                m = pe.transpose(tbank[:, o:o + P], xr[:, par, t, c * P:(c + 1) * P], ident[:, :])
                        m.then_inc(td, 1)

                    def hidden(j, par, c):
                        pe.wait_ge(gd, j * FC + c + 1)
                        for which in range(2):
                            for k in range(DC):
                                m = mm3(pe, banks[c % 2][:, which * RT:(which + 1) * RT], up(w_hi, par, which, k, c),
                                        up(w_lo, par, which, k, c), x_hi[:, par, k, :], x_lo[:, par, k, :],
                                        k == 0, k == DC - 1)
                        m.then_inc(hd, 1)

                    def result(j, par, c):
                        if c == 0:
                            pe.wait_ge(w2, j + 1)
                            pe.wait_ge(ye, j + 1)
                        pe.wait_ge(glo, j * FC + c + 1 + 2)
                        for t in range(TB):
                            m = mm3(pe, wide[:, 512 * t:512 * t + D], g_hi[:, c, t * P:(t + 1) * P],
                                    g_lo[:, c, t * P:(t + 1) * P], down(w_hi, par, c), down(w_lo, par, c),
                                    c == 0, c == FC - 1)
                        if c == FC - 1:
                            m.then_inc(yd, 1)

                    transposes(0, 0, 0)

                    def tile(j, par, half, first):
                        pe.wait_ge(xlo, j + 1)
                        pe.wait_ge(w0, j + 1)
                        pe.wait_ge(w1, j + 1)
                        hidden(j, par, 0)
                        if not first:
                            result(j - 1, 1 - par, FC - 2)
                        hidden(j, par, 1)
                        if not first:
                            result(j - 1, 1 - par, FC - 1)
                        transposes(j + 1, 1 - par, half if par == 0 else half + 1)
                        hidden(j, par, 2)
                        result(j, par, 0)
                        hidden(j, par, 3)
                        result(j, par, 1)
                    over_tiles(pe, tile)
                    result(NR - 1, 0, FC - 2)
                    result(NR - 1, 0, FC - 1)

        def ingest(tag, XT_hi, XT_lo, keep=None):
            with ExitStack() as ctx:
                xn = sb(ctx, tag + "xn", [P, 2 * D])
                st, ve, rs, xr, td, hd, ld, kd = sems(ctx, " ".join(tag + s for s in "st ve rs xr td hd ld kd".split()))
                blk = ctx.enter_context(nc.Block())

                @blk.gpsimd
                def _(pool):
                    pool.wait_ge(st, 2 * NT)
                    pool.tensor_scalar(RSTD[:, :], MV[:, 1::2], EPS, None, ALU.add).then_inc(ve, 1)
                    pool.wait_ge(ve, 1)
                    pool.tensor_tensor(RSTD[:, :], RSTD[:, :], mhalf[:, :], ALU.pow).then_inc(rs, 1)

                @blk.vector
                def _(dve):
                    row_statistics(dve, X, st)
                    dve.wait_ge(rs, 1)
                    dve.wait_ge(st, 2 * NT)

                    def normalise(i, p):
                        dve.tensor_scalar(xn[:, p * D:(p + 1) * D], X[:, ds(i * D, D)], MV[:, ds(2 * i, 1)],
                                          RSTD[:, ds(i, 1)], ALU.subtract, ALU.mult).then_inc(xr, 1)
                    normalise(0, 0)
                    normalise(1, 1)

                    def low(i, p, more):
                        dve.wait_ge(hd, i + 1)
                        dve.tensor_tensor(XT_lo[:, :, ds(i * P, P)],
                                          banks[p][:, 0:D].rearrange("p (c n) -> p c n", c=DC),
                                          XT_hi[:, :, ds(i * P, P)].bitcast(F32), ALU.subtract).then_inc(ld, 1)
                        if keep is not None:
                            dve.tensor_copy(keep[:, ds(i * D, D)], xn[:, p * D:(p + 1) * D]).then_inc(kd, 1)
                            dve.wait_ge(kd, i + 1)
                        if more:
                            normalise(i + 2, p)
                    pairs(dve, NT, low)

                @blk.tensor
                def _(pe):
                    pe.sem_inc(ld, 2)

                    def step(i, p, more):
                        pe.wait_ge(xr, i + 1)
                        pe.wait_ge(ld, i + 1)
                        for c in range(DC):
                            t = pe.transpose(banks[p][:, c * P:(c + 1) * P],
                                             xn[:, p * D + c * P:p * D + (c + 1) * P], ident[:, :])
                        t.then_inc(td, 1)
                    pairs(pe, NT, step)

                @blk.scalar
                def _(act):
                    def high(i, p, more):
                        act.wait_ge(td, i + 1)
                        act.activation(XT_hi[:, :, ds(i * P, P)],
                                       banks[p][:, 0:D].rearrange("p (c n) -> p c n", c=DC), ACT.Copy).then_inc(hd, 1)
                    pairs(act, NT, high)

        def slot_pass(tag, n, kc, src_hi, src_lo, products, act_evac, dve_evac, after=None, final=None):
            with ExitStack() as ctx:
                s_hi, s_lo = split_pair(ctx, tag + "slot", [P, 2, kc, P])
                sh, sl, md, ae, de = sems(ctx, " ".join(tag + s for s in "sh sl md ae de".split()))
                (own,) = sems(ctx, tag + "own")
                blk = ctx.enter_context(nc.Block())

                @blk.scalar
                def _(act):
                    def fill(i, p):
                        act.activation(s_hi[:, p, :, :], src_hi[:, 0:kc, ds(i * P, P)].bitcast(F32), ACT.Copy).then_inc(sh, 1)
                    fill(0, 0)
                    fill(1, 1)

                    def step(i, p, more):
                        act.wait_ge(md, i + 1)
                        if act_evac:
                            act_evac(act, i, p, banks[p], ae)
                        if more:
                            fill(i + 2, p)
                    pairs(act, n, step)

                @blk.vector
                def _(dve):
                    def fill(i, p):
                        dve.tensor_copy(s_lo[:, p, :, :], src_lo[:, 0:kc, ds(i * P, P)]).then_inc(sl, 1)
                    fill(0, 0)
                    fill(1, 1)

                    def step(i, p, more):
                        if act_evac:
                            dve.wait_ge(ae, i + 1)
                        else:
                            dve.wait_ge(md, i + 1)
                        dve_evac(dve, i, p, banks[p], own).then_inc(de, 1)
                        if more:
                            fill(i + 2, p)
                    pairs(dve, n, step)
                    if final:
                        final(dve, own, de)

                @blk.tensor
                def _(pe):
                    pe.sem_inc(de, 2)

                    def step(i, p, more):
                        pe.wait_ge(sh, i + 1)
                        pe.wait_ge(sl, i + 1)
                        pe.wait_ge(de, i + 1)
                        products(pe, banks[p], s_hi[:, p, :, :], s_lo[:, p, :, :]).then_inc(md, 1)
                    pairs(pe, n, step)

        def attention(tag, nq, Q_hi, Q_lo, Wq_hi, Wq_lo, bq, kc, scale, nk, nk_cols, K_hi, K_lo, V_hi, V_lo, vw,
                      finish_act, finish_dve, on_sync=None):
            G = -(-nk // 4)
            widths = [min(512, nk_cols + nk_cols % 2 - 512 * g) for g in range(G)]
            with ExitStack() as ctx:
                prob = sb(ctx, tag + "prob", [P, nk * P])
                pt_hi, pt_lo = split_pair(ctx, tag + "pt", [P, nk * P])
                q_hi, q_lo = split_pair(ctx, tag + "q", [P, kc, P])
                part = sb(ctx, tag + "part", [P, 4])
                top1 = sb(ctx, tag + "top1", [P, 1])
                nmax = sb(ctx, tag + "nmax", [P, 1])
                rsum = sb(ctx, tag + "rsum", [P, nq])
                rinv = sb(ctx, tag + "rinv", [P, nq])
                (s_done, t_done, pv_done, q_done, thi, tlo, qhi, qlo, mx, exp_done, o_free, f_act, chain, inv_done) = sems(
                    ctx, " ".join(tag + s for s in
                                  "s t pv q thi tlo qhi qlo mx ex of fa ch iv".split()))
                tb = [banks[0], banks[1]]
                ob, qb = banks[2], banks[3]
                blk = ctx.enter_context(nc.Block())
                if on_sync:
                    blk.sync(on_sync)

                def q_columns(i):
                    return ds(i * P, P)

                @blk.tensor
                def _(pe):
                    pe.sem_inc(tlo, 2)
                    pe.sem_inc(o_free, 1)

                    def project(i):
                        for h in range(kc):
                            for c in range(DC):
                                m = mm3(pe, qb[:, h * P:(h + 1) * P],
                                        Wq_hi[:, c, h * P:(h + 1) * P], Wq_lo[:, c, h * P:(h + 1) * P],
                                        Q_hi[:, c, q_columns(i)], Q_lo[:, c, q_columns(i)], c == 0, c == DC - 1)
                        m.then_inc(q_done, 1)

                    def scores(i, g):
                        for c in range(kc):
                            m = mm3(pe, wide[:, 512 * g:512 * g + widths[g]], q_hi[:, c, :], q_lo[:, c, :],
                                    K_hi[:, c, 512 * g:512 * g + widths[g]], K_lo[:, c, 512 * g:512 * g + widths[g]],
                                    c == 0, c == kc - 1)
                        m.then_inc(s_done, 1)

                    def transposes(i, g):
                        pe.wait_ge(tlo, i * G + g + 1)
                        for k in range(4 * g, min(4 * g + 4, nk)):
                            m = pe.transpose(tb[g % 2][:, (k % 4) * P:(k % 4 + 1) * P], prob[:, k * P:(k + 1) * P],
                                             ident[:, :])
                        m.then_inc(t_done, 1)

                    def weighted(i):
                        pe.wait_ge(o_free, i + 1)
                        for g in range(G):
                            pe.wait_ge(tlo, i * G + g + 1 + 2)
                            for k in range(4 * g, min(4 * g + 4, nk)):
                                m = mm3(pe, ob[:, 0:vw], pt_hi[:, k * P:(k + 1) * P], pt_lo[:, k * P:(k + 1) * P],
                                        V_hi[:, k, :], V_lo[:, k, :], k == 0, k == nk - 1) if vw == D else \
                                    mm3(pe, ob[:, 0:P], V_hi[:, k, :], V_lo[:, k, :],
                                        pt_hi[:, k * P:(k + 1) * P], pt_lo[:, k * P:(k + 1) * P], k == 0, k == nk - 1)
                        m.then_inc(pv_done, 1)

                    def turn(i, more):
                        pe.wait_ge(exp_done, i)
                        pe.wait_ge(qhi, i + 1)
                        pe.wait_ge(qlo, i + 1)
                        for g in range(G):
                            transposes(i - 1, g)
                            scores(i, g)
                        if more:
                            project(i + 1)
                        weighted(i - 1)

                    project(0)
                    pe.wait_ge(qhi, 1)
                    pe.wait_ge(qlo, 1)
                    for g in range(G):
                        scores(0, g)
                    project(1)
                    with pe.Fori(1, nq - 1) as i:
                        turn(i, True)
                    turn(nq - 1, False)
                    pe.wait_ge(exp_done, nq)
                    for g in range(G):
                        transposes(nq - 1, g)
                    weighted(nq - 1)

                @blk.scalar
                def _(act):
                    def query(i):
                        act.wait_ge(q_done, i + 1)
                        for h in range(kc):
                            m = act.activation(q_hi[:, h, :], qb[:, h * P:(h + 1) * P], ACT.Identity,
                                               bias=bq[:, h:h + 1] if bq is not None else 0.0)
                        m.then_inc(qhi, 1)

                    def high(i, g):
                        act.wait_ge(t_done, i * G + g + 1)
                        w = (min(4 * g + 4, nk) - 4 * g) * P
                        act.activation(pt_hi[:, 512 * g:512 * g + w], tb[g % 2][:, 0:w], ACT.Copy).then_inc(thi, 1)

                    def exponent(i):
                        act.wait_ge(mx, i + 1)
                        act.activation(prob[:, 0:nk_cols], wide[:, 0:nk_cols], ACT.Exp, bias=nmax[:, 0:1],
                                       scale=scale, accum_out=rsum[:, ds(i, 1)]).then_inc(exp_done, 1)

                    query(0)
                    exponent(0)
                    query(1)

                    def turn(i, more):
                        for g in range(G):
                            high(i - 1, g)
                        if more:
                            query(i + 1)
                        exponent(i)
                        if finish_act:
                            act.wait_ge(pv_done, i)
                            finish_act(act, i - 1, ob).then_inc(f_act, 1)
                    with act.Fori(1, nq - 1) as i:
                        turn(i, True)
                    turn(nq - 1, False)
                    for g in range(G):
                        high(nq - 1, g)
                    if finish_act:
                        act.wait_ge(pv_done, nq)
                        finish_act(act, nq - 1, ob).then_inc(f_act, 1)

                @blk.vector
                def _(dve):
                    if nk * P > nk_cols:
                        dve.memset(prob[:, nk_cols:nk * P], 0.0).then_inc(chain, 1)
                    else:
                        dve.memset(part[:, :], 0.0).then_inc(chain, 1)
                    dve.wait_ge(chain, 1)

                    def query(i):
                        dve.wait_ge(qhi, i + 1)
                        for h in range(kc):
                            if bq is not None:
                                m = dve.scalar_tensor_tensor(out=q_lo[:, h, :], in0=qb[:, h * P:(h + 1) * P],
                                                             scalar=bq[:, h:h + 1], in1=q_hi[:, h, :].bitcast(F32),
                                                             op0=ALU.add, op1=ALU.subtract)
                            else:
                                m = dve.tensor_tensor(q_lo[:, h, :], qb[:, h * P:(h + 1) * P],
                                                      q_hi[:, h, :].bitcast(F32), ALU.subtract)
                        m.then_inc(qlo, 1)

                    def low(i, g):
                        dve.wait_ge(thi, i * G + g + 1)
                        w = (min(4 * g + 4, nk) - 4 * g) * P
                        dve.tensor_tensor(pt_lo[:, 512 * g:512 * g + w], tb[g % 2][:, 0:w],
                                          pt_hi[:, 512 * g:512 * g + w].bitcast(F32), ALU.subtract).then_inc(tlo, 1)

                    def maximum(i, g):
                        dve.wait_ge(s_done, i * G + g + 1)
                        dve.reduce_max(part[:, g:g + 1], wide[:, 512 * g:512 * g + min(512, nk_cols - 512 * g)],
                                       AX).then_inc(chain, 1)

                    def whole_maximum(i):
                        dve.wait_ge(chain, i * (G + 1) + G + 1)
                        dve.reduce_max(top1[:, :], part[:, 0:G], AX).then_inc(chain, 1)
                        dve.wait_ge(chain, (i + 1) * (G + 1) + 1)
                        dve.tensor_scalar(nmax[:, :], top1[:, :], -scale, None, ALU.mult).then_inc(mx, 1)

                    def finish(i):
                        dve.wait_ge(exp_done, i + 1)
                        dve.reciprocal(rinv[:, ds(i, 1)], rsum[:, ds(i, 1)]).then_inc(inv_done, 1)
                        dve.wait_ge(inv_done, i + 1)
                        if finish_act:
                            dve.wait_ge(f_act, i + 1)
                        else:
                            dve.wait_ge(pv_done, i + 1)
                        finish_dve(dve, i, ob, rinv[:, ds(i, 1)]).then_inc(o_free, 1)

                    query(0)
                    for g in range(G):
                        maximum(0, g)
                    whole_maximum(0)
                    query(1)

                    def turn(i, more):
                        for g in range(G):
                            low(i - 1, g)
                            maximum(i, g)
                        whole_maximum(i)
                        if more:
                            query(i + 1)
                        finish(i - 1)
                    with dve.Fori(1, nq - 1) as i:
                        turn(i, True)
                    turn(nq - 1, False)
                    for g in range(G):
                        low(nq - 1, g)
                    finish(nq - 1)

        def small(ctx, name, shape, dt=F32):
            return sb(ctx, name, shape, dt)

        def moe_phase():
            rows_out = nc.dram_tensor("routed_results", (NR * RT, D), F32, kind="Internal").ap()
            with ExitStack() as ph:
                w12 = sb(ph, "w12", [P, 2, NT])
                pos = sb(ph, "pos", [P, 2, NT], mybir.dt.uint32)
                table = sb(ph, "table", [P, NR + 1], I32)
                XT_hi, XT_lo = split_pair(ph, "XT1", [P, DC, S])
                s_ex = ph.enter_context(ExitStack())
                XN = sb(s_ex, "XN", [P, NT * D])
                ingest("i1", XT_hi, XT_lo, XN)
                with ExitStack() as ctx:
                    W = weights(ctx, "wr", {"L0_ffn_router_wT": (DC, E)})
                    rh, rl = W["L0_ffn_router_wT"]
                    LG = sb(ctx, "LG", [P, NT, E])

                    def products(pe, bank, sh, sl):
                        for c in range(DC):
                            m = mm3(pe, bank[:, 0:E], sh[:, c, :], sl[:, c, :], rh[:, c, :], rl[:, c, :], c == 0, c == 1)
                        return m

                    def evac(dve, i, p, bank, own):
                        return dve.tensor_tensor(LG[:, ds(i, 1), :], bank[:, 0:E].unsqueeze(1), BIASE.unsqueeze(1), ALU.add)
                    slot_pass("rt", NT, DC, XT_hi, XT_lo, products, None, evac)

                    rank = sb(ctx, "rank", [P, NT, E])
                    ranki = sb(ctx, "ranki", [P, NT, E], I32)
                    t3, LG2, oh1, oh2, before, slot = (sb(ctx, n, [P, NT, E]) for n in
                                                       ("t3", "LG2", "oh1", "oh2", "before", "slot"))
                    chosen = sb(ctx, "chosen", [P, NT, E], F32R)
                    m1, m2, tm, dd, ex = (sb(ctx, n, [P, NT]) for n in ("m1", "m2", "tm", "dd", "ex"))
                    count_e, tiles_e, first_e, end_e = (sb(ctx, n, [P, E]) for n in ("cnt", "tls", "fst", "end"))
                    lim = sb(ctx, "lim", [P, E, E])
                    limi = sb(ctx, "limi", [P, E, E], I32)
                    tl = sb(ctx, "tl", [P, NR + 1, E])
                    tli = sb(ctx, "tli", [P, NR + 1, E], I32)
                    cmp8 = sb(ctx, "cmp8", [P, E, E])
                    te = sb(ctx, "te", [P, NR + 1])
                    ones = sb(ctx, "ones", [P, P])
                    ones_r = sb(ctx, "ones_r", [P, P], F32R)
                    below = sb(ctx, "below", [P, P], F32R)
                    rk, ch, xp, pm = sems(ctx, "rk rch rxp rpm")
                    blk = ctx.enter_context(nc.Block())

                    def wide3(t, n=NT):
                        return t.unsqueeze(2).to_broadcast([P, n, E])

                    @blk.gpsimd
                    def _(pool):
                        pool.iota(ranki[:, :, :], pattern=[[0, NT], [-1, E]], base=E, channel_multiplier=0).then_inc(rk, 1)
                        pool.iota(limi[:, :, :], pattern=[[0, E], [RT, E]], base=0, channel_multiplier=0).then_inc(rk, 1)
                        pool.iota(tli[:, :, :], pattern=[[1, NR + 1], [0, E]], base=0, channel_multiplier=0).then_inc(rk, 1)
                        pool.memset(ones[:, :], 1.0).then_inc(rk, 1)
                        pool.wait_ge(rk, 4)
                        pool.affine_select(out=below[:, :], in_=ones[:, :], compare_op=ALU.is_gt, fill=0.0, base=0,
                                           pattern=[[1, P]], channel_multiplier=-1).then_inc(rk, 1)

                    @blk.scalar
                    def _(act):
                        act.wait_ge(rk, 4)
                        act.activation(ones_r[:, :], ones[:, :], ACT.Copy).then_inc(pm, 1)
                        act.wait_ge(xp, 1)
                        act.activation(ex[:, :], dd[:, :], ACT.Exp).then_inc(xp, 1)

                    @blk.tensor
                    def _(pe):
                        pe.wait_ge(rk, 5)
                        pe.wait_ge(pm, 2)
                        m = chosen[:, :, :].rearrange("p i e -> p (i e)")
                        pe.matmul(banks[0][:, 0:NT * E], below[:, :], m, start=True, stop=True)
                        pe.matmul(banks[1][:, 0:NT * E], ones_r[:, :], m, start=True, stop=True).then_inc(pm, 1)

                    @blk.vector
                    def _(dve):
                        count = [0]

                        def link(ins):
                            count[0] += 1
                            ins.then_inc(ch, 1)
                            dve.wait_ge(ch, count[0])

                        def first_of_largest(logits, m, oh):
                            link(dve.reduce_max(m[:, :], logits, AX))
                            link(dve.tensor_tensor(t3[:, :, :], logits, wide3(m[:, :]), ALU.is_equal))
                            link(dve.tensor_tensor(t3[:, :, :], t3[:, :, :], rank[:, :, :], ALU.mult))
                            link(dve.reduce_max(tm[:, :], t3[:, :, :], AX))
                            link(dve.tensor_tensor(oh[:, :, :], rank[:, :, :], wide3(tm[:, :]), ALU.is_equal))
                        dve.wait_ge(rk, 5)
                        link(dve.tensor_copy(rank[:, :, :], ranki[:, :, :]))
                        link(dve.tensor_copy(lim[:, :, :], limi[:, :, :]))
                        link(dve.tensor_copy(tl[:, :, :], tli[:, :, :]))
                        first_of_largest(LG[:, :, :], m1, oh1)
                        link(dve.scalar_tensor_tensor(out=LG2[:, :, :], in0=oh1[:, :, :], scalar=-BIG, in1=LG[:, :, :],
                                                      op0=ALU.mult, op1=ALU.add))
                        first_of_largest(LG2[:, :, :], m2, oh2)
                        dve.tensor_tensor(dd[:, :], m2[:, :], m1[:, :], ALU.subtract).then_inc(xp, 1)
                        dve.wait_ge(pm, 1)
                        dve.tensor_tensor(chosen[:, :, :], oh1[:, :, :], oh2[:, :, :], ALU.add).then_inc(pm, 1)
                        dve.wait_ge(xp, 2)
                        link(dve.tensor_scalar(tm[:, :], ex[:, :], 1.0, None, ALU.add))
                        link(dve.reciprocal(w12[:, 0, :], tm[:, :]))
                        link(dve.tensor_tensor(w12[:, 1, :], ex[:, :], w12[:, 0, :], ALU.mult))
                        dve.wait_ge(pm, 3)
                        link(dve.memset(before[:, 0, :], 0.0))
                        for i in range(1, NT):
                            link(dve.tensor_tensor(before[:, i, :], before[:, i - 1, :], banks[1][:, (i - 1) * E:i * E],
                                                   ALU.add))
                        link(dve.tensor_tensor(count_e[:, :], before[:, NT - 1, :], banks[1][:, (NT - 1) * E:NT * E], ALU.add))
                        link(dve.tensor_tensor(cmp8[:, :, :], wide3(count_e[:, :], E), lim[:, :, :], ALU.is_gt))
                        link(dve.reduce_sum(tiles_e[:, :], cmp8[:, :, :], AX))
                        link(dve.memset(first_e[:, 0:1], 0.0))
                        for e in range(1, E):
                            link(dve.tensor_tensor(first_e[:, e:e + 1], first_e[:, e - 1:e], tiles_e[:, e - 1:e], ALU.add))
                        link(dve.tensor_tensor(end_e[:, :], first_e[:, :], tiles_e[:, :], ALU.add))
                        link(dve.tensor_tensor(before[:, :, :], before[:, :, :],
                                               banks[0][:, 0:NT * E].rearrange("p (i e) -> p i e", e=E), ALU.add))
                        link(dve.scalar_tensor_tensor(out=slot[:, :, :], in0=first_e[:, :].unsqueeze(1).to_broadcast([P, NT, E]),
                                                      scalar=float(RT), in1=before[:, :, :], op0=ALU.mult, op1=ALU.add))
                        for k, oh in enumerate((oh1, oh2)):
                            link(dve.tensor_tensor(t3[:, :, :], oh[:, :, :], slot[:, :, :], ALU.mult))
                            link(dve.reduce_sum(tm[:, :], t3[:, :, :], AX))
                            link(dve.tensor_copy(pos[:, k, :], tm[:, :]))
                        link(dve.tensor_tensor(tl[:, :, :], end_e[:, :].unsqueeze(1).to_broadcast([P, NR + 1, E]),
                                               tl[:, :, :], ALU.is_le))
                        link(dve.reduce_sum(te[:, :], tl[:, :, :], AX))
                        link(dve.tensor_scalar(te[:, :], te[:, :], float(E - 1), None, ALU.min))
                        link(dve.tensor_copy(table[:, :], te[:, :]))

                scattered, gathered = sems(ph, "scattered gathered")

                def scatter(pool):
                    for k in range(2):
                        for i in range(NT):
                            pool.indirect_dma_start(rows_in[:, :], bass.IndirectOffsetOnAxis(ap=pos[:, k, i:i + 1], axis=0),
                                                    XN[:, i * D:(i + 1) * D], None).then_inc(scattered, 16)
                    pool.wait_ge(scattered, 16 * 2 * NT)
                shared_expert("s0", E, XT_hi, XT_lo, on_pool=scatter)
                s_ex.close()
                routed_experts(table, rows_in, rows_out)
                with ExitStack() as s_ex:
                    back = sb(s_ex, "back", [P, 2, NT, D])

                    def gather(pool):
                        for i in range(NT):
                            for k in range(2):
                                pool.indirect_dma_start(back[:, k, i, :], None, rows_out[:, :],
                                                        bass.IndirectOffsetOnAxis(ap=pos[:, k, i:i + 1], axis=0))\
                                    .then_inc(gathered, 16)

                    def combine(dve, done, n):
                        dve.wait_ge(gathered, 16 * 2 * NT)
                        dve.wait_ge(done, n)
                        for k in range(2):
                            for i in range(NT):
                                x = X[:, i * D:(i + 1) * D]
                                m = dve.scalar_tensor_tensor(out=x, in0=back[:, k, i, :], scalar=w12[:, k, i:i + 1], in1=x,
                                                             op0=ALU.mult, op1=ALU.add)
                            m.then_inc(done, 1)
                            dve.wait_ge(done, n + k + 1)
                    shared_expert("s1", E + 1, XT_hi, XT_lo, on_pool=gather, after=combine)

        def cross_phase():
            with ExitStack() as ph:
                C2S = sb(ph, "C2S", [P, NT * D])
                scratch = nc.dram_tensor("s2c_rows", (1 + CP, D), F32, kind="Internal").ap()
                with ExitStack() as mid:
                    K_hi, K_lo = split_pair(mid, "K1", [P, DC, S])
                    V_hi, V_lo = split_pair(mid, "V1", [P, NT, D])
                    o_s2c = sb(mid, "o_s2c", [P, NC * D])

                    def keys_values(tag, n, src_hi, src_lo, k_name, v_name, bk):
                        with ExitStack() as ctx:
                            W = weights(ctx, tag + "w", {k_name: (DC, D), v_name: (DC, D)})
                            (kh, kl), (vh, vl) = W[k_name], W[v_name]

                            def products(pe, bank, sh, sl):
                                for h in range(DC):
                                    for c in range(DC):
                                        mm3(pe, bank[:, h * P:(h + 1) * P], kh[:, c, h * P:(h + 1) * P],
                                            kl[:, c, h * P:(h + 1) * P], sh[:, c, :], sl[:, c, :], c == 0, c == 1)
                                for c in range(DC):
                                    m = mm3(pe, bank[:, D:2 * D], sh[:, c, :], sl[:, c, :], vh[:, c, :], vl[:, c, :],
                                            c == 0, c == 1)
                                return m

                            def hi(act, i, p, bank, done):
                                for h in range(DC):
                                    act.activation(K_hi[:, h, ds(i * P, P)], bank[:, h * P:(h + 1) * P], ACT.Identity,
                                                   bias=bk[:, h:h + 1])
                                act.activation(V_hi[:, ds(i, 1), :], bank[:, D:2 * D].unsqueeze(1), ACT.Copy).then_inc(done, 1)

                            def lo(dve, i, p, bank, own):
                                for h in range(DC):
                                    k = K_hi[:, h, ds(i * P, P)].bitcast(F32)
                                    dve.scalar_tensor_tensor(out=K_lo[:, h, ds(i * P, P)], in0=bank[:, h * P:(h + 1) * P],
                                                             scalar=bk[:, h:h + 1], in1=k, op0=ALU.add, op1=ALU.subtract)
                                return dve.tensor_tensor(V_lo[:, ds(i, 1), :], bank[:, D:2 * D].unsqueeze(1),
                                                         V_hi[:, ds(i, 1), :].bitcast(F32), ALU.subtract)
                            slot_pass(tag, n, DC, src_hi, src_lo, products, hi, lo)

                    def finish_into(dst, bv):
                        def finish(dve, i, bank, rinv):
                            return dve.scalar_tensor_tensor(out=dst[:, ds(i * D, D)], in0=bank[:, 0:D], scalar=rinv, in1=bv,
                                                            op0=ALU.mult, op1=ALU.add)
                        return finish

                    scale = D ** -0.5
                    with ExitStack() as q1:
                        XT_hi, XT_lo = split_pair(q1, "XT2", [P, DC, S])
                        ingest("i2", XT_hi, XT_lo)
                        keys_values("ks", NC, CT_hi, CT_lo, "L1_xattn_Wk_sT", "L1_xattn_Wv_sT", BKS)
                        with ExitStack() as ctx:
                            W = weights(ctx, "wqc", {"L1_xattn_Wq_cT": (DC, D)})
                            attention("ac", NT, XT_hi, XT_lo, *W["L1_xattn_Wq_cT"], BQC, DC, scale, NC, C, K_hi, K_lo,
                                      V_hi, V_lo, D, None, finish_into(C2S, BV_S))
                        keys_values("kc", NT, XT_hi, XT_lo, "L1_xattn_Wk_cT", "L1_xattn_Wv_cT", BKC)
                    with ExitStack() as ctx:
                        W = weights(ctx, "wqs", {"L1_xattn_Wq_sT": (DC, D)})
                        attention("as", NC, CT_hi, CT_lo, *W["L1_xattn_Wq_sT"], BQS, DC, scale, NT, S, K_hi, K_lo,
                                  V_hi, V_lo, D, None, finish_into(o_s2c, BV_C))
                    with ExitStack() as ctx:
                        zrow = sb(ctx, "zrow", [1, D])
                        (zr, stc) = sems(ctx, "zr stc")
                        blk = ctx.enter_context(nc.Block())

                        @blk.vector
                        def _(dve):
                            dve.memset(zrow[:, :], 0.0).then_inc(zr, 1)

                        @blk.sync
                        def _(sp):
                            sp.dma_start(scratch[1:1 + CP, :].rearrange("(i p) d -> p i d", p=P),
                                         o_s2c[:, :].rearrange("p (i d) -> p i d", d=D)).then_inc(stc, 16)
                            sp.wait_ge(zr, 1)
                            sp.dma_start(scratch[0:1, :], zrow[:, :]).then_inc(stc, 16)
                            sp.wait_ge(stc, 32)

                STEP = P * C // S
                S2CI = sb(ph, "S2CI", [P, NT * D])
                with ExitStack() as ctx:
                    tent = sb(ctx, "tent", [P, NT * P], F32R)
                    with ExitStack() as c2:
                        posi = sb(c2, "posi", [P, S], I32)
                        keyi = sb(c2, "keyi", [P, S], I32)
                        pos = sb(c2, "ipos", [P, S])
                        key = sb(c2, "ikey", [P, S])
                        io, cc, rr = sems(c2, "io icc irr")
                        blk = c2.enter_context(nc.Block())

                        @blk.gpsimd
                        def _(pool):
                            pool.iota(posi[:, :], pattern=[[2 * C, S]], base=C - S, channel_multiplier=0).then_inc(io, 1)
                            pool.iota(keyi[:, :], pattern=[[STEP, NT], [0, P]], base=-1, channel_multiplier=1).then_inc(io, 1)

                        @blk.vector
                        def _(dve):
                            dve.wait_ge(io, 2)
                            dve.tensor_copy(pos[:, :], posi[:, :]).then_inc(cc, 1)
                            dve.tensor_copy(key[:, :], keyi[:, :]).then_inc(cc, 1)
                            dve.wait_ge(cc, 2)
                            dve.tensor_scalar(pos[:, :], pos[:, :], 0.5 / S, 0.0, ALU.mult, ALU.max).then_inc(cc, 1)
                            dve.wait_ge(cc, 3)
                            dve.scalar_tensor_tensor(out=pos[:, :], in0=pos[:, :], scalar=float(C - 1), in1=key[:, :],
                                                     op0=ALU.min, op1=ALU.subtract).then_inc(cc, 1)

                        @blk.scalar
                        def _(act):
                            act.wait_ge(cc, 4)
                            act.activation(key[:, :], pos[:, :], ACT.Abs).then_inc(rr, 1)
                            act.wait_ge(rr, 1)
                            act.activation(tent[:, :], key[:, :], ACT.Relu, bias=1.0, scale=-1.0).then_inc(rr, 1)

                    win = sb(ctx, "win", [P, NT * D])
                    win_hi, win_lo = split_pair(ctx, "win", [P, NT * D])
                    t_slot = sb(ctx, "t_slot", [P, 2 * P], F32R)
                    wl, wh, wo, ts, md, de = sems(ctx, "w_l w_h w_o w_t w_md w_de")
                    blk = ctx.enter_context(nc.Block())

                    @blk.sync
                    def _(sp):
                        with sp.Fori(0, NT) as i:
                            sp.dma_start(win[:, ds(i * D, D)], scratch[ds(i * STEP, P), :]).then_inc(wl, 16)

                    @blk.scalar
                    def _(act):
                        act.wait_ge(wl, 16 * NT)
                        with act.Fori(0, NT) as i:
                            act.activation(win_hi[:, ds(i * D, D)], win[:, ds(i * D, D)], ACT.Copy).then_inc(wh, 1)

                    @blk.vector
                    def _(dve):
                        def fill(i, p):
                            dve.wait_ge(wh, i + 1)
                            dve.tensor_tensor(win_lo[:, ds(i * D, D)], win[:, ds(i * D, D)],
                                              win_hi[:, ds(i * D, D)].bitcast(F32), ALU.subtract)
                            dve.tensor_copy(t_slot[:, p * P:(p + 1) * P], tent[:, ds(i * P, P)]).then_inc(ts, 1)
                        fill(0, 0)
                        fill(1, 1)

                        def step(i, p, more):
                            dve.wait_ge(md, i + 1)
                            dve.tensor_copy(S2CI[:, ds(i * D, D)], banks[p][:, 0:D]).then_inc(de, 1)
                            if more:
                                fill(i + 2, p)
                        pairs(dve, NT, step)

                    @blk.tensor
                    def _(pe):
                        pe.sem_inc(de, 2)

                        def step(i, p, more):
                            pe.wait_ge(ts, i + 1)
                            pe.wait_ge(de, i + 1)
                            t = t_slot[:, p * P:(p + 1) * P]
                            pe.matmul(banks[p][:, 0:D], t, win_hi[:, ds(i * D, D)], start=True, stop=False)
                            pe.matmul(banks[p][:, 0:D], t, win_lo[:, ds(i * D, D)], start=False, stop=True).then_inc(md, 1)
                        pairs(pe, NT, step)

                with ExitStack() as ctx:
                    W = weights(ctx, "wg", {"L1_xattn_WgT": (2 * DC, D)})
                    gh, gl = W["L1_xattn_WgT"]
                    LGT = sb(ctx, "LGT", [P, NT * D])

                    def source(i):
                        return [C2S[:, ds(i * D, D)], S2CI[:, ds(i * D, D)]]

                    def products(pe, bank, sh, sl):
                        for c in range(2 * DC):
                            m = mm3(pe, bank[:, 0:D], sh[:, c, :], sl[:, c, :], gh[:, c, :], gl[:, c, :], c == 0, c == 3)
                        return m

                    def evac(dve, i, p, bank, own):
                        return dve.tensor_tensor(LGT[:, ds(i * D, D)], bank[:, 0:D], BG, ALU.add)
                    transpose_pass("gt", NT, 2 * DC, source, products, evac)

                    th = LGT
                    a, b, c = sems(ctx, "ga gb gc")
                    blk = ctx.enter_context(nc.Block())

                    @blk.scalar
                    def _(act):
                        with act.Fori(0, NT // 4) as i:
                            act.activation(th[:, ds(i * 4 * D, 4 * D)], LGT[:, ds(i * 4 * D, 4 * D)], ACT.Tanh,
                                           scale=0.5).then_inc(a, 1)

                    @blk.vector
                    def _(dve):
                        with dve.Fori(0, NT // 4) as i:
                            sl = ds(i * 4 * D, 4 * D)
                            dve.tensor_tensor(C2S[:, sl], C2S[:, sl], S2CI[:, sl], ALU.subtract).then_inc(b, 1)
                            dve.tensor_tensor(X[:, sl], X[:, sl], S2CI[:, sl], ALU.add).then_inc(b, 1)
                            dve.wait_ge(a, i + 1)
                            dve.wait_ge(b, i * 4 + 1)
                            dve.scalar_tensor_tensor(out=th[:, sl], in0=th[:, sl], scalar=1.0, in1=C2S[:, sl], op0=ALU.add,
                                                     op1=ALU.mult).then_inc(b, 1)
                            dve.wait_ge(b, i * 4 + 3)
                            dve.scalar_tensor_tensor(out=X[:, sl], in0=th[:, sl], scalar=0.5, in1=X[:, sl], op0=ALU.mult,
                                                     op1=ALU.add).then_inc(b, 1)

        def last_phase():
            with ExitStack() as ph:
                XT_hi, XT_lo = split_pair(ph, "XT3", [P, DC, S])
                ingest("i3", XT_hi, XT_lo)
                W = weights(ph, "wl", {"L1_ffn_gate_WT": (DC, E), "expert01T": (DC, 2 * D), "L1_ffn_out_WT": (DC, D)})
                SC = sb(ph, "SC", [P, 2, NT])
                FIN = sb(ph, "FIN", [P, NT * D])
                with ExitStack() as ctx:
                    rh, rl = W["L1_ffn_gate_WT"]
                    LG = sb(ctx, "LG3", [P, NT, E])
                    PR = sb(ctx, "PR3", [P, NT, E])

                    def products(pe, bank, sh, sl):
                        for c in range(DC):
                            m = mm3(pe, bank[:, 0:E], sh[:, c, :], sl[:, c, :], rh[:, c, :], rl[:, c, :], c == 0, c == 1)
                        return m

                    def evac(dve, i, p, bank, own):
                        return dve.tensor_copy(LG[:, ds(i, 1), :], bank[:, 0:E].unsqueeze(1))
                    slot_pass("gg", NT, DC, XT_hi, XT_lo, products, None, evac)
                    m1, sm, cn = (sb(ctx, n, [P, NT]) for n in ("m13", "sm3", "cn3"))
                    ch, xp = sems(ctx, "r3ch r3xp")
                    blk = ctx.enter_context(nc.Block())

                    def wide3(t):
                        return t[:, :].unsqueeze(2).to_broadcast([P, NT, E])

                    @blk.scalar
                    def _(act):
                        act.wait_ge(xp, 1)
                        act.activation(PR[:, :, :], LG[:, :, :], ACT.Exp).then_inc(xp, 1)

                    @blk.vector
                    def _(dve):
                        count = [0]

                        def link(ins):
                            count[0] += 1
                            ins.then_inc(ch, 1)
                            dve.wait_ge(ch, count[0])
                        link(dve.reduce_max(m1[:, :], LG[:, :, :], AX))
                        dve.tensor_tensor(LG[:, :, :], LG[:, :, :], wide3(m1), ALU.subtract).then_inc(xp, 1)
                        dve.wait_ge(xp, 2)
                        link(dve.reduce_sum(sm[:, :], PR[:, :, :], AX))
                        link(dve.reciprocal(sm[:, :], sm[:, :]))
                        link(dve.tensor_tensor(PR[:, :, :], PR[:, :, :], wide3(sm), ALU.mult))
                        link(dve.tensor_scalar(LG[:, :, :], PR[:, :, :], 0.3, None, ALU.is_gt))
                        link(dve.reduce_sum(cn[:, :], LG[:, :, :], AX))
                        link(dve.tensor_tensor(SC[:, 1, :], cn[:, :], PR[:, :, 1], ALU.mult))
                        link(dve.tensor_scalar(cn[:, :], cn[:, :], -1.0, float(E), ALU.mult, ALU.add))
                        link(dve.tensor_tensor(SC[:, 0, :], cn[:, :], PR[:, :, 0], ALU.mult))
                eh, el = W["expert01T"]
                with ExitStack() as ctx:
                    part = sb(ctx, "part3", [P, 2, D])

                    def products(pe, bank, sh, sl):
                        for c in range(DC):
                            m = mm3(pe, bank[:, :], sh[:, c, :], sl[:, c, :], eh[:, c, :], el[:, c, :], c == 0, c == 1)
                        return m

                    def hi(act, i, p, bank, done):
                        act.activation(part[:, p, :], bank[:, D:2 * D], ACT.Copy, scale=SC[:, 1, ds(i, 1)]).then_inc(done, 1)

                    def evac(dve, i, p, bank, own):
                        return dve.scalar_tensor_tensor(out=FIN[:, ds(i * D, D)], in0=bank[:, 0:D],
                                                        scalar=SC[:, 0, ds(i, 1)], in1=part[:, p, :], op0=ALU.mult,
                                                        op1=ALU.add)
                    slot_pass("ee", NT, DC, XT_hi, XT_lo, products, hi, evac)
                oh, ol = W["L1_ffn_out_WT"]

                def products(pe, bank, sh, sl):
                    for c in range(DC):
                        m = mm3(pe, bank[:, 0:D], sh[:, c, :], sl[:, c, :], oh[:, c, :], ol[:, c, :], c == 0, c == 1)
                    return m

                def evac(dve, i, p, bank, own):
                    x = X[:, ds(i * D, D)]
                    return dve.tensor_tensor(x, x, bank[:, 0:D], ALU.add)
                transpose_pass("oo", NT, DC, lambda i: [FIN[:, ds(i * D, D)]], products, evac)

        rows_in = nc.dram_tensor("routed_rows", ((NR + 1) * RT, D), F32, kind="Internal").ap()

        with ExitStack() as ph:
            XT_hi, XT_lo = split_pair(ph, "XT0", [P, DC, S])
            Wb_hi, Wb_lo = split_pair(ph, "W0", [P, 2064])
            Fx = sb(ph, "Fx", [P, NT * D])
            zeros = sb(ph, "zeros", [P, 4 * D])

            def part_of(t, off, kc, n):
                return t[:, off:off + kc * n].rearrange("p (c n) -> p c n", c=kc)
            spec0, off = {}, 0
            for name, kc, n in (("L0_xattn_Wq", 2, HA), ("L0_xattn_Wk", 2, HA), ("L0_xattn_Wv", 2, HA),
                                ("L0_xattn_WoT", 2, HA), ("L0_xattn_Wfc", 2, D), ("bo2", 2, P), ("Wof", 1, D)):
                spec0[name] = (off, kc, n)
                off += kc * n
            assert off <= 2064

            def w0(name):
                return part_of(Wb_hi, *spec0[name]), part_of(Wb_lo, *spec0[name])
            with ExitStack() as ctx:
                raw = sb(ctx, "raw0", [P, 2064])
                ctf = sb(ctx, "ctf", [P, DC, CP])
                ldw, ldc, ldx, ldv, hi, lo, z, pd, idn, aa, bb, st = sems(
                    ctx, "p_ldw p_ldc p_ldx p_ldv p_hi p_lo p_z p_pd p_idn p_aa p_bb p_st")
                blk = ctx.enter_context(nc.Block())
                wnames = [n for n in spec0 if n.startswith("L0")]
                nw = spec0["bo2"][0]

                @blk.sync
                def _(sp):
                    for name in wnames:
                        o, kc, n = spec0[name]
                        sp.dma_start(part_of(raw, o, kc, n), A[name].rearrange("(c p) n -> p c n", p=P)).then_inc(ldw, 16)
                    for c in range(DC):
                        sp.dma_start(ctf[:, c, 0:C], A["ctxT"][c * P:(c + 1) * P, :]).then_inc(ldc, 16)
                    sp.wait_ge(ldw, 16 * len(wnames))

                @blk.scalar
                def _(act):
                    for j, (t, name) in enumerate(((BO, "L0_xattn_bo"), (BQC, "L1_xattn_bq_c"), (BKS, "L1_xattn_bk_s"),
                                                   (BQS, "L1_xattn_bq_s"), (BKC, "L1_xattn_bk_c"))):
                        act.dma_start(t, A[name]).then_inc(ldv, 16)
                    for j in range(4):
                        act.dma_start(X[:, j * 4 * D:(j + 1) * 4 * D].rearrange("p (i d) -> p i d", d=D),
                                      A["x"][0, j * 512:(j + 1) * 512, :].rearrange("(i p) d -> p i d", p=P)).then_inc(ldx, 16)
                    for t, name in ((GAMMA, "L0_xattn_ln_gamma"), (BETA, "L0_xattn_ln_beta"), (BV_S, "L1_xattn_bv_s"),
                                    (BV_C, "L1_xattn_bv_c"), (BG, "L1_xattn_bg"), (BIASE, "L0_ffn_expert_bias")):
                        act.dma_start(t, A[name].partition_broadcast(P)).then_inc(ldv, 16)
                    act.wait_ge(ldv, 16 * 11)
                    act.wait_ge(ldx, 64)
                    act.wait_ge(z, 2)
                    act.wait_ge(ldw, 16 * len(wnames))
                    for c in range(DC):
                        act.activation(raw[:, nw + c * P:nw + (c + 1) * P], ident[:, :], ACT.Identity,
                                       bias=BO[:, c:c + 1], scale=0.0).then_inc(z, 1)
                    act.wait_ge(z, 4)
                    act.activation(Wb_hi[:, 0:nw + 2 * P], raw[:, 0:nw + 2 * P], ACT.Copy).then_inc(hi, 1)
                    act.wait_ge(ldc, 32)
                    act.wait_ge(pd, 1)
                    for c in range(DC):
                        act.activation(CT_hi[:, c, :], ctf[:, c, :], ACT.Copy).then_inc(hi, 1)
                    act.wait_ge(aa, 1)
                    o, _, n = spec0["Wof"]
                    act.activation(Wb_hi[:, o:o + n], banks[0][:, 0:D], ACT.Copy).then_inc(hi, 1)

                @blk.gpsimd
                def _(pool):
                    pool.memset(ident[:, :], 0.0).then_inc(idn, 1)
                    pool.memset(mhalf[:, :], -0.5).then_inc(z, 1)
                    pool.wait_ge(idn, 1)
                    pool.affine_select(out=ident[:, :], in_=ident[:, :], compare_op=ALU.not_equal, fill=1.0, base=0,
                                       pattern=[[-1, P]], channel_multiplier=1).then_inc(z, 1)

                @blk.vector
                def _(dve):
                    dve.memset(zeros[:, :], 0.0)
                    dve.memset(ctf[:, :, C:CP], 0.0).then_inc(pd, 1)
                    dve.wait_ge(hi, 1)
                    dve.tensor_tensor(Wb_lo[:, 0:nw + 2 * P], raw[:, 0:nw + 2 * P], Wb_hi[:, 0:nw + 2 * P].bitcast(F32),
                                      ALU.subtract).then_inc(lo, 1)
                    for c in range(DC):
                        dve.wait_ge(hi, c + 2)
                        dve.tensor_tensor(CT_lo[:, c, :], ctf[:, c, :], CT_hi[:, c, :].bitcast(F32),
                                          ALU.subtract).then_inc(lo, 1)
                    dve.wait_ge(aa, 2)
                    dve.tensor_copy(BFC, banks[1][:, 0:D]).then_inc(lo, 1)
                    dve.wait_ge(hi, 4)
                    o, _, n = spec0["Wof"]
                    dve.tensor_tensor(Wb_lo[:, o:o + n], banks[0][:, 0:D], Wb_hi[:, o:o + n].bitcast(F32),
                                      ALU.subtract).then_inc(lo, 1)

                @blk.tensor
                def _(pe):
                    pe.wait_ge(hi, 1)
                    pe.wait_ge(lo, 1)
                    (ah, al), (fh, fl), (bh, bl) = w0("L0_xattn_WoT"), w0("L0_xattn_Wfc"), w0("bo2")
                    for c in range(DC):
                        m = mm3(pe, banks[0][:, 0:D], ah[:, c, :], al[:, c, :], fh[:, c, :], fl[:, c, :], c == 0, c == 1)
                    m.then_inc(aa, 1)
                    for c in range(DC):
                        m = mm3(pe, banks[1][:, 0:D], bh[:, c, :], bl[:, c, :], fh[:, c, :], fl[:, c, :], c == 0, c == 1)
                    m.then_inc(aa, 1)

            ingest("i0", XT_hi, XT_lo)

            fch, fcl = w0("L0_xattn_Wfc")

            def fc_products(pe, bank, sh, sl):
                for c in range(DC):
                    m = mm3(pe, bank[:, 0:D], sh[:, c, :], sl[:, c, :], fch[:, c, :], fcl[:, c, :], c == 0, c == 1)
                return m

            def fc_out(dve, i, p, bank, own):
                return dve.tensor_tensor(Fx[:, ds(i * D, D)], bank[:, 0:D], BFC, ALU.add)
            slot_pass("f0", NT, DC, XT_hi, XT_lo, fc_products, None, fc_out)

            with ExitStack() as at:
                K_hi, K_lo = split_pair(at, "K0", [P, 1, CP])
                V_hi, V_lo = split_pair(at, "V0", [P, NC, HA])
                CX_hi, CX_lo = split_pair(at, "CX", [P, 1, S])
                kh, kl = w0("L0_xattn_Wk")
                vh, vl = w0("L0_xattn_Wv")

                def kv_products(pe, bank, sh, sl):
                    for c in range(DC):
                        mm3(pe, bank[:, 0:P], kh[:, c, :], kl[:, c, :], sh[:, c, :], sl[:, c, :], c == 0, c == 1)
                    for c in range(DC):
                        m = mm3(pe, bank[:, P:2 * P], sh[:, c, :], sl[:, c, :], vh[:, c, :], vl[:, c, :], c == 0, c == 1)
                    return m

                def kv_hi(act, i, p, bank, done):
                    act.activation(K_hi[:, 0, ds(i * P, P)], bank[:, 0:P], ACT.Copy)
                    act.activation(V_hi[:, ds(i, 1), :], bank[:, P:2 * P].unsqueeze(1), ACT.Copy).then_inc(done, 1)

                def kv_lo(dve, i, p, bank, own):
                    dve.tensor_tensor(K_lo[:, 0, ds(i * P, P)], bank[:, 0:P], K_hi[:, 0, ds(i * P, P)].bitcast(F32),
                                      ALU.subtract)
                    return dve.tensor_tensor(V_lo[:, ds(i, 1), :], bank[:, P:2 * P].unsqueeze(1),
                                             V_hi[:, ds(i, 1), :].bitcast(F32), ALU.subtract)
                slot_pass("kv0", NC, DC, CT_hi, CT_lo, kv_products, kv_hi, kv_lo)

                RI = sb(at, "RI", [P, NT])

                def ctx_hi(act, i, bank):
                    return act.activation(CX_hi[:, 0, ds(i * P, P)], bank[:, 0:P], ACT.Copy)

                def ctx_lo(dve, i, bank, rinv):
                    dve.tensor_copy(RI[:, ds(i, 1)], rinv)
                    return dve.tensor_tensor(CX_lo[:, 0, ds(i * P, P)], bank[:, 0:P],
                                             CX_hi[:, 0, ds(i * P, P)].bitcast(F32), ALU.subtract)

                FR = 4
                (cleared,) = sems(at, "cleared")

                def clear_table(sp):
                    n = (NR + 1) * RT // (P * FR)
                    for j in range(n):
                        sp.dma_start(rows_in[j * P * FR:(j + 1) * P * FR, :].rearrange("(p r) d -> p (r d)", p=P),
                                     zeros[:, :]).then_inc(cleared, 16)
                    sp.wait_ge(cleared, 16 * n)
                attention("a0", NT, XT_hi, XT_lo, *w0("L0_xattn_Wq"), None, 1, HA ** -0.5, NC, C, K_hi, K_lo, V_hi, V_lo,
                          HA, ctx_hi, ctx_lo, on_sync=clear_table)

                wofh, wofl = w0("Wof")

                def of_products(pe, bank, sh, sl):
                    return mm3(pe, bank[:, 0:D], sh[:, 0, :], sl[:, 0, :], wofh[:, 0, :], wofl[:, 0, :], True, True)

                def of_out(dve, i, p, bank, own):
                    z = Fx[:, ds(i * D, D)]
                    return dve.scalar_tensor_tensor(out=z, in0=bank[:, 0:D], scalar=RI[:, ds(i, 1)], in1=z,
                                                    op0=ALU.mult, op1=ALU.add)
                slot_pass("of", NT, 1, CX_hi, CX_lo, of_products, None, of_out)

            with ExitStack() as ctx:
                zn = sb(ctx, "zn", [P, 2 * D])
                a, b, c, d, e = sems(ctx, "ya yb yc yd ye")
                blk = ctx.enter_context(nc.Block())

                @blk.gpsimd
                def _(pool):
                    pool.wait_ge(c, 2 * NT)
                    pool.tensor_scalar(RSTD[:, :], MV[:, 1::2], EPS, None, ALU.add).then_inc(a, 1)
                    pool.wait_ge(a, 1)
                    pool.tensor_tensor(RSTD[:, :], RSTD[:, :], mhalf[:, :], ALU.pow).then_inc(a, 1)

                @blk.vector
                def _(dve):
                    row_statistics(dve, Fx, c)
                    dve.wait_ge(a, 2)
                    dve.wait_ge(c, 2 * NT)

                    def step(i, p, more):
                        z = zn[:, p * D:(p + 1) * D]
                        x = X[:, ds(i * D, D)]
                        dve.tensor_scalar(z, Fx[:, ds(i * D, D)], MV[:, ds(2 * i, 1)], RSTD[:, ds(i, 1)], ALU.subtract,
                                          ALU.mult).then_inc(b, 1)
                        dve.tensor_tensor(x, x, BETA, ALU.add).then_inc(b, 1)
                        dve.wait_ge(b, i * 4 + 1)
                        dve.tensor_tensor(z, z, GAMMA, ALU.mult).then_inc(b, 1)
                        dve.wait_ge(b, i * 4 + 3)
                        dve.tensor_tensor(x, x, z, ALU.add).then_inc(b, 1)
                    pairs(dve, NT, step)

        moe_phase()
        cross_phase()
        last_phase()

        with ExitStack() as ctx:
            (stored,) = sems(ctx, "stored")
            blk = ctx.enter_context(nc.Block())

            @blk.sync
            def _(sp):
                for j in range(4):
                    sp.dma_start(out[0, j * 512:(j + 1) * 512, :].rearrange("(i p) d -> p i d", p=P),
                                 X[:, j * 4 * D:(j + 1) * 4 * D].rearrange("p (i d) -> p i d", d=D)).then_inc(stored, 16)
                sp.wait_ge(stored, 64)


_HOST_TRANSPOSED = {"L0_xattn_WoT": "L0_xattn_Wo", **{n + "T": n for n in (
    "L0_ffn_router_w", "L1_xattn_Wq_c", "L1_xattn_Wk_s", "L1_xattn_Wv_s", "L1_xattn_Wq_s", "L1_xattn_Wk_c",
    "L1_xattn_Wv_c", "L1_xattn_Wg", "L1_ffn_gate_W", "L1_ffn_out_W")}}
_IN_COLUMNS = ("L0_xattn_bo", "L1_xattn_bq_c", "L1_xattn_bk_s", "L1_xattn_bq_s", "L1_xattn_bk_c")


def kernel(**inputs):
    import numpy as _np
    import concourse.bacc as _bacc
    from concourse import mybir as _mybir
    from concourse.bass_utils import run_bass_kernel_spmd as _run

    nc = _bacc.Bacc("TRN2", target_bir_lowering=False, num_devices=1)
    laid_out = {k: _np.asarray(v) for k, v in inputs.items()}
    laid_out["ctxT"] = laid_out.pop("ctx_1024")[0].T
    for new, old in _HOST_TRANSPOSED.items():
        laid_out[new] = _np.swapaxes(laid_out.pop(old), -1, -2)
    for name in _IN_COLUMNS:
        laid_out[name] = laid_out[name].reshape(D // P, P).T
    for new, old in (("w1T", "w1"), ("w3T", "w3"), ("w2T", "w2")):
        laid_out[new] = _np.swapaxes(_np.concatenate(
            (laid_out.pop("L0_ffn_" + old), laid_out.pop("L0_ffn_s" + old))), -1, -2)
    laid_out["expert01T"] = laid_out.pop("L1_ffn_expert_W")[:2].reshape(2 * D, D).T
    arrays, aps = {}, {}
    for name, a in laid_out.items():
        arrays[name] = _np.ascontiguousarray(a)
        aps[name] = nc.dram_tensor(name, a.shape, _mybir.dt.from_np(a.dtype), kind="ExternalInput").ap()
    out = nc.dram_tensor("out", (1, S, D), _mybir.dt.float32, kind="ExternalOutput").ap()
    build(nc, aps, out)
    r = _run(nc, [arrays], core_ids=[0])
    return r.results[0]["out"]
```

```python
import concourse.bass as bass
from concourse import mybir
from contextlib import ExitStack

F32 = mybir.dt.float32
F32R = mybir.dt.float32r
I32 = mybir.dt.int32
ALU = mybir.AluOpType
ACT = mybir.ActivationFunctionType
AX = mybir.AxisListType.X
ds = bass.ds

P = 128
D = 256
DC = D // P
S = 2048
NT = S // P
C = 1601
NC = -(-C // P)
CP = NC * P
HA = 128
E = 8
NSH = 2
F = 512
EPS = 1e-5
BIG = 3.0e38
RT = 256
NR = (2 * S + E * (RT - 1)) // RT


def pairs(eng, n, body):
    main = (n - 2) // 2 * 2
    if main > 0:
        with eng.Fori(0, main // 2) as j:
            body(j * 2, 0, True)
            body(j * 2 + 1, 1, True)
    for i in range(main, n):
        body(i, i % 2, i + 2 < n)


def fours(eng, n, body):
    with eng.Fori(0, n // 4 - 1) as j:
        for q in range(4):
            body(j * 4 + q, q, True)
    for q in range(4):
        body(n - 4 + q, q, False)


def pairs3(eng, n, body):
    main = (n - 3) // 2 * 2
    with eng.Fori(0, main // 2) as j:
        body(j * 2, 0, 4)
        body(j * 2 + 1, 1, 4)
    for i in range(main, n):
        body(i, i % 2, n - i)


def turns(eng, n, body):
    main = (n - 4) // 2
    with eng.Fori(0, main) as j:
        body(j * 2 + 2, 0, True)
        body(j * 2 + 3, 1, True)
    for i in range(2 * main + 2, n):
        body(i, i % 2, i < n - 1)


def mm3(pe, out, wh, wl, xh, xl, first, last):
    pe.matmul(out, wh, xh, start=first, stop=False)
    pe.matmul(out, wh, xl, start=False, stop=False)
    return pe.matmul(out, wl, xh, start=False, stop=last)


def build(nc, A, out):
    top = ExitStack()
    with top:
        def sb(ctx, name, shape, dt=F32):
            return ctx.enter_context(nc.sbuf_tensor(name, shape, dt))

        def split_pair(ctx, name, shape):
            return sb(ctx, name + "_hi", shape, F32R), sb(ctx, name + "_lo", shape, F32R)

        banks = [top.enter_context(nc.psum_tensor(f"bank{i}", [P, 512], F32)) for i in range(0, 4)]
        wide = top.enter_context(nc.psum_tensor("wide", [P, 4 * 512], F32))

        X = sb(top, "X", [P, NT * D])
        ident = sb(top, "ident", [P, P])
        MV = sb(top, "MV", [P, 2 * NT])
        RSTD = sb(top, "RSTD", [P, NT])
        SHIFT = sb(top, "SHIFT", [P, NT])
        mhalf = sb(top, "mhalf", [P, NT])
        stats = sb(top, "stats", [P, 6 * NT])
        rows = sb(top, "rows", [P, 9 * D])
        GAMMA, BETA, BFC, BV_S, BV_C, BG = (rows[:, j * D:(j + 1) * D] for j in range(6))
        BIASE = rows[:, 6 * D:6 * D + E]
        cols = sb(top, "cols", [P, 16])
        BO, BQC, BKS, BQS, BKC = (cols[:, 2 * j:2 * j + 2] for j in range(5))
        CT_hi, CT_lo = split_pair(top, "CT", [P, DC, CP])

        free_sems = [nc.alloc_semaphore(f"signal{i}") for i in range(140)]

        scattered, gathered, stored_results = (nc.alloc_semaphore(n) for n in ("scattered", "gathered", "stored_results"))

        def sems(ctx, names):
            got = [free_sems.pop(0) for _ in names.split()]

            def give_back():
                for s in got:
                    nc.gpsimd.sem_clear(s)
                free_sems.extend(got)
            ctx.callback(give_back)
            return got

        waiting_loads = []

        def start_loads(sp):
            for dst, dram, sem in waiting_loads:
                sp.dma_start(dst, dram.rearrange("(c p) n -> p c n", p=P)).then_inc(sem, 16)
            waiting_loads.clear()

        def blk_loads(blk, then=None):
            if waiting_loads or then:
                @blk.sync
                def _(sp):
                    start_loads(sp)
                    if then:
                        then(sp)


        def row_statistics(dve, src, st):
            def partial(g):
                for i in range(4 * g, 4 * g + 4):
                    dve.bn_stats(out=stats[:, 6 * i:6 * i + 6], in_=src[:, D * i:D * i + D]).then_inc(st, 1)
            partial(0)
            for g in range(NT // 4):
                if g + 1 < NT // 4:
                    partial(g + 1)
                dve.wait_ge(st, 8 * g + 4)
                for i in range(4 * g, 4 * g + 4):
                    dve.bn_aggr(out=MV[:, 2 * i:2 * i + 2], in_=stats[:, 6 * i:6 * i + 6]).then_inc(st, 1)

        def inverse_deviations(pool, st, ve, rs):
            for g in range(NT // 4):
                four = RSTD[:, 4 * g:4 * g + 4]
                pool.wait_ge(st, min(8 * g + 12, 2 * NT))
                pool.tensor_scalar(four, MV[:, 8 * g + 1:8 * g + 8:2], EPS, None, ALU.add).then_inc(ve, 1)
                pool.wait_ge(ve, g + 1)
                pool.tensor_tensor(four, four, mhalf[:, 0:4], ALU.pow).then_inc(rs, 1)

        def shifts(dve):
            return dve.scalar_tensor_tensor(out=SHIFT[:, :], in0=MV[:, 0::2], scalar=-1.0, in1=RSTD[:, :], op0=ALU.mult,
                                            op1=ALU.mult)

        def request(ctx, tag, spec, until_split=None):
            total = sum(kc * n for kc, n in spec.values())
            if until_split is None:
                raw = sb(ctx, tag + "raw", [P, total])
            hi, lo = split_pair(ctx, tag, [P, total])
            if until_split is not None:
                raw = sb(until_split, tag + "raw", [P, total])
            loaded = sems(ctx, " ".join(f"{tag}ld{j}" for j in range(len(spec))))
            at, off = {}, 0
            for (name, (kc, n)), sem in zip(spec.items(), loaded):
                r, h, l = (t[:, off:off + kc * n].rearrange("p (c n) -> p c n", c=kc) for t in (raw, hi, lo))
                waiting_loads.append((r, A[name], sem))
                at[name] = (h, l, r, sem)
                off += kc * n
            return at

        def split_now(tag, *groups):
            with ExitStack() as ctx:
                hi_done, lo_done = sems(ctx, f"{tag}hi {tag}lo")
                blk = ctx.enter_context(nc.Block())
                items = [m for g in groups for m in g.values()]
                blk_loads(blk)

                @blk.scalar
                def _(act):
                    for j, (hi, lo, raw, loaded) in enumerate(items):
                        act.wait_ge(loaded, 16)
                        act.activation(hi, raw, ACT.Copy).then_inc(hi_done, 1)

                @blk.vector
                def _(dve):
                    for j, (hi, lo, raw, loaded) in enumerate(items):
                        dve.wait_ge(hi_done, j + 1)
                        dve.tensor_tensor(lo, raw, hi.bitcast(F32), ALU.subtract).then_inc(lo_done, 1)

        def transpose_pass(tag, n, kc, source, products, evac, on_pool=None):
            with ExitStack() as ctx:
                t_in = sb(ctx, tag + "tin", [P, 2, kc, P])
                s_hi, s_lo = split_pair(ctx, tag + "slot", [P, 2, kc, P])
                fi, td, hd, ld, md, de = sems(ctx, " ".join(tag + s for s in "fi td hd ld md de".split()))
                blk = ctx.enter_context(nc.Block())
                blk_loads(blk)
                if on_pool:
                    blk.gpsimd(on_pool)

                @blk.vector
                def _(dve):
                    def fill(i, p):
                        parts = source(i)
                        for j, x in enumerate(parts):
                            w = kc // len(parts)
                            dve.tensor_copy(t_in[:, p, j * w:(j + 1) * w, :],
                                            x.rearrange("p (c n) -> p c n", c=w)).then_inc(fi, 1)

                    def low(i, p):
                        dve.wait_ge(hd, i + 1)
                        dve.tensor_tensor(s_lo[:, p, :, :], banks[p][:, 0:kc * P].rearrange("p (c n) -> p c n", c=kc),
                                          s_hi[:, p, :, :].bitcast(F32), ALU.subtract).then_inc(ld, 1)
                    fill(0, 0)
                    fill(1, 1)
                    low(0, 0)
                    fill(2, 0)

                    def step(i, p, left):
                        if left > 1:
                            low(i + 1, 1 - p)
                        if left > 3:
                            fill(i + 3, 1 - p)
                        dve.wait_ge(md, i + 1)
                        evac(dve, i, p, banks[2 + p]).then_inc(de, 1)
                    pairs3(dve, n, step)

                @blk.scalar
                def _(act):
                    def step(i, p, more):
                        act.wait_ge(td, i + 1)
                        act.activation(s_hi[:, p, :, :], banks[p][:, 0:kc * P].rearrange("p (c n) -> p c n", c=kc),
                                       ACT.Copy).then_inc(hd, 1)
                    pairs(act, n, step)

                @blk.tensor
                def _(pe):
                    pe.sem_inc(de, 2)
                    parts = len(source(0))

                    def transposes(i, p):
                        pe.wait_ge(fi, parts * (i + 1))
                        for c in range(kc):
                            t = pe.transpose(banks[p][:, c * P:(c + 1) * P], t_in[:, p, c, :], ident[:, :])
                        t.then_inc(td, 1)
                    transposes(0, 0)
                    transposes(1, 1)

                    def step(i, p, more):
                        pe.wait_ge(ld, i + 1)
                        pe.wait_ge(de, i + 1)
                        products(pe, banks[2 + p], s_hi[:, p, :, :], s_lo[:, p, :, :]).then_inc(md, 1)
                        if more:
                            transposes(i + 2, p)
                    pairs(pe, n, step)

        def request_shared(ctx, tag, e, raw):
            loaded = sems(ctx, f"{tag}ld1 {tag}ld3 {tag}ld2")
            for k, w in enumerate(("w1T", "w3T", "w2T")):
                waiting_loads.append((raw[:, k * DC * F:(k + 1) * DC * F].rearrange("p (c n) -> p c n", n=F if k < 2 else D),
                                      A[w][e], loaded[k]))
            return loaded

        def shared_expert(tag, raw, loads, XT_hi, XT_lo, on_pool=None, after=None):
            NB, FC, TB = S // 512, F // P, 4
            W = DC * F * 2 + FC * D
            with ExitStack() as ctx:
                w_hi, w_lo = split_pair(ctx, tag + "w", [P, W])
                sil = sb(ctx, tag + "sil", [P, 2, 512])
                gate = sb(ctx, tag + "gate", [P, 2, 512])
                g_hi, g_lo = split_pair(ctx, tag + "g", [P, FC, 512])
                (whi, wlo, hd, sd, gd, ghi, glo, yd, yf) = sems(
                    ctx, " ".join(tag + s for s in "whi wlo hd sd gd ghi glo yd yf".split()))
                blk = ctx.enter_context(nc.Block())

                def up(t, which, c, m):
                    o = which * DC * F + c * F + m * P
                    return t[:, o:o + P]

                def down(t, m):
                    o = 2 * DC * F + m * D
                    return t[:, o:o + D]

                def piece(t, k):
                    return t[:, k * DC * F:(k + 1) * DC * F]

                if on_pool:
                    blk.gpsimd(on_pool)

                @blk.scalar
                def _(act):
                    for k in range(3):
                        act.wait_ge(loads[k], 16)
                        act.activation(piece(w_hi, k), piece(raw, k), ACT.Copy).then_inc(whi, 1)

                    def hi(n0, c):
                        act.wait_ge(gd, n0 + 1 + 2)
                        act.activation(g_hi[:, c, :], gate[:, c % 2, :], ACT.Copy).then_inc(ghi, 1)

                    def block(b, first):
                        for c in range(FC):
                            n0 = b * FC + c
                            act.wait_ge(hd, n0 + 1)
                            act.activation(sil[:, c % 2, :], banks[2 * (c % 2)][:, :], ACT.Silu).then_inc(sd, 1)
                            if c or not first:
                                hi(n0 - 1, (c - 1) % FC)
                    block(0, True)
                    with act.Fori(1, NB) as b:
                        block(b, False)
                    hi(NB * FC - 1, FC - 1)

                @blk.vector
                def _(dve):
                    for k in range(3):
                        dve.wait_ge(whi, k + 1)
                        dve.tensor_tensor(piece(w_lo, k), piece(raw, k), piece(w_hi, k).bitcast(F32),
                                          ALU.subtract).then_inc(wlo, 1)

                    def lo(n0, c):
                        dve.wait_ge(ghi, n0 + 1)
                        dve.tensor_tensor(g_lo[:, c, :], gate[:, c % 2, :], g_hi[:, c, :].bitcast(F32),
                                          ALU.subtract).then_inc(glo, 1)

                    def add(b):
                        dve.wait_ge(yd, b + 1)
                        for t in range(TB):
                            x = X[:, ds((b * TB + t) * D, D)]
                            m = dve.tensor_tensor(x, x, wide[:, 512 * t:512 * t + D], ALU.add)
                        m.then_inc(yf, 1)

                    def block(b, first):
                        for c in range(FC):
                            n0 = b * FC + c
                            dve.wait_ge(glo, n0 + 1)
                            dve.wait_ge(sd, n0 + 1)
                            dve.tensor_tensor(gate[:, c % 2, :], sil[:, c % 2, :], banks[2 * (c % 2) + 1][:, :],
                                              ALU.mult).then_inc(gd, 1)
                            if c or not first:
                                lo(n0 - 1, (c - 1) % FC)
                            if c == 1 and not first:
                                add(b - 1)
                    block(0, True)
                    with dve.Fori(1, NB) as b:
                        block(b, False)
                    lo(NB * FC - 1, FC - 1)
                    add(NB - 1)
                    if after:
                        after(dve, yf, NB + 1)

                @blk.tensor
                def _(pe):
                    pe.sem_inc(yf, 1)
                    pe.sem_inc(glo, 2)
                    pe.sem_inc(gd, 2)
                    pe.wait_ge(wlo, 2)

                    def hidden(b, c):
                        pe.wait_ge(gd, b * FC + c + 1)
                        for which in range(2):
                            for k in range(DC):
                                m = mm3(pe, banks[2 * (c % 2) + which][:, :], up(w_hi, which, k, c),
                                        up(w_lo, which, k, c), XT_hi[:, k, ds(b * 512, 512)],
                                        XT_lo[:, k, ds(b * 512, 512)], k == 0, k == DC - 1)
                        m.then_inc(hd, 1)

                    def result(b, c):
                        if c == 0:
                            pe.wait_ge(yf, b + 1)
                        pe.wait_ge(glo, b * FC + c + 1 + 2)
                        for t in range(TB):
                            m = mm3(pe, wide[:, 512 * t:512 * t + D], g_hi[:, c, t * P:(t + 1) * P],
                                    g_lo[:, c, t * P:(t + 1) * P], down(w_hi, c), down(w_lo, c),
                                    c == 0, c == FC - 1)
                        if c == FC - 1:
                            m.then_inc(yd, 1)

                    def block(b, first):
                        for c in range(FC):
                            hidden(b, c)
                            if first and c == 2:
                                pe.wait_ge(wlo, 3)
                            if c >= 2:
                                result(b, c - 2)
                            elif not first:
                                result(b - 1, FC - 2 + c)
                    block(0, True)
                    with pe.Fori(1, NB) as b:
                        block(b, False)
                    result(NB - 1, FC - 2)
                    result(NB - 1, FC - 1)

        def routed_experts(table, rows_in, rows_out):
            FC, TB = F // P, RT // P
            NP = (NR - 1) // 2
            assert NR == 2 * NP + 1
            W = DC * F * 2 + FC * D
            with ExitStack() as ctx:
                raw = sb(ctx, "rraw", [P, W])
                w_hi, w_lo = split_pair(ctx, "rw", [P, 2, W])
                xr = sb(ctx, "rxr", [P, 2, TB, D])
                x_hi, x_lo = split_pair(ctx, "rx", [P, 2, DC, RT])
                sil = sb(ctx, "rsil", [P, 2, RT])
                gate = sb(ctx, "rgate", [P, 2, RT])
                g_hi, g_lo = split_pair(ctx, "rg", [P, FC, RT])
                ys = sb(ctx, "rys", [P, 2, TB * D])
                (l0, l1, l2, xl0, xl1, td, xhi, xlo, whi, w0, w1, w2, hd, sd, gd, ghi, glo, yd, ye, ysf) = sems(
                    ctx, " ".join(f"r{i}" for i in range(20)))
                loaded, split_done, rows_in_done = (l0, l1, l2), (w0, w1, w2), (xl0, xl1)
                blk = ctx.enter_context(nc.Block())
                tbank = banks[2]

                def up(t, par, which, c, m):
                    o = which * DC * F + c * F + m * P
                    return t[:, par, o:o + P]

                def down(t, par, m):
                    o = 2 * DC * F + m * D
                    return t[:, par, o:o + D]

                def over_tiles(eng, body):
                    body(0, 0, 0, True)
                    with eng.Fori(0, NP) as k:
                        body(k * 2 + 1, 1, k, False)
                        body(k * 2 + 2, 0, k + 1, False)

                @blk.sync
                def _(sp):
                    start_loads(sp)

                    def load(j, par, first):
                        e = sp.value_load(table[0:1, ds(j, 1)] if not first else table[0:1, j:j + 1], min_val=0, max_val=E - 1)
                        sp.wait_ge(td, j + 1)
                        sp.dma_start(xr[:, par, :, :], rows_in[ds(j * RT, RT), :].rearrange("(t p) d -> p t d", p=P))\
                          .then_inc(rows_in_done[par], 16)
                        for k, w in enumerate(("w1T", "w3T", "w2T")):
                            if not first:
                                sp.wait_ge(split_done[k], j)
                            sp.dma_start(raw[:, k * DC * F:(k + 1) * DC * F].rearrange("p (c n) -> p c n", n=F if k < 2 else D),
                                         A[w][ds(e, 1), :, :].rearrange("a (c p) n -> p (a c) n", p=P))\
                              .then_inc(loaded[k], 16)
                    load(0, 0, True)
                    with sp.Fori(0, NP) as k:
                        load(k * 2 + 1, 1, False)
                        load(k * 2 + 2, 0, False)
                    load(NR, 1, False)

                @blk.gpsimd
                def _(pool):
                    pool.sem_inc(ysf, 2)

                    def store(j, par, half, first):
                        pool.wait_ge(ye, j + 1 + 1)
                        pool.wait_ge(yd, 1)
                        pool.dma_start(rows_out[ds(j * RT, RT), :].rearrange("(t p) d -> p t d", p=P),
                                       ys[:, par, :].rearrange("p (t d) -> p t d", d=D)).then_inc(stored_results, 16)
                        pool.wait_ge(stored_results, 16 * (j + 1))
                        pool.sem_inc(ysf, 1)
                    over_tiles(pool, store)

                @blk.scalar
                def _(act):
                    def split(j, par, k):
                        act.wait_ge(loaded[k], 16 * (j + 1))
                        act.activation(w_hi[:, par, k * DC * F:(k + 1) * DC * F], raw[:, k * DC * F:(k + 1) * DC * F],
                                       ACT.Copy).then_inc(whi, 1)

                    def rows(j, par):
                        act.wait_ge(td, j + 1 + 2)
                        act.activation(x_hi[:, par, :, :], tbank[:, :].rearrange("p (c n) -> p c n", c=DC),
                                       ACT.Copy).then_inc(xhi, 1)

                    def silu(j, c):
                        act.wait_ge(hd, j * FC + c + 1)
                        act.activation(sil[:, c % 2, :], banks[c % 2][:, 0:RT], ACT.Silu).then_inc(sd, 1)

                    def hi(j, c):
                        act.wait_ge(gd, j * FC + c + 1 + 2)
                        act.activation(g_hi[:, c, :], gate[:, c % 2, :], ACT.Copy).then_inc(ghi, 1)
                    rows(0, 0)
                    for k in range(3):
                        split(0, 0, k)

                    def tile(j, par, half, first):
                        silu(j, 0)
                        split(j + 1, 1 - par, 0)
                        silu(j, 1)
                        hi(j, 0)
                        split(j + 1, 1 - par, 1)
                        silu(j, 2)
                        hi(j, 1)
                        rows(j + 1, 1 - par)
                        silu(j, 3)
                        hi(j, 2)
                        if not first:
                            act.wait_ge(yd, j)
                        split(j + 1, 1 - par, 2)
                        hi(j, 3)
                    over_tiles(act, tile)

                @blk.vector
                def _(dve):
                    def split(j, par, k):
                        dve.wait_ge(whi, j * 3 + k + 1)
                        dve.tensor_tensor(w_lo[:, par, k * DC * F:(k + 1) * DC * F], raw[:, k * DC * F:(k + 1) * DC * F],
                                          w_hi[:, par, k * DC * F:(k + 1) * DC * F].bitcast(F32),
                                          ALU.subtract).then_inc(split_done[k], 1)

                    def rows(j, par):
                        dve.wait_ge(xhi, j + 1)
                        dve.tensor_tensor(x_lo[:, par, :, :], tbank[:, :].rearrange("p (c n) -> p c n", c=DC),
                                          x_hi[:, par, :, :].bitcast(F32), ALU.subtract).then_inc(xlo, 1)

                    def gated(j, c):
                        dve.wait_ge(glo, j * FC + c + 1)
                        dve.wait_ge(sd, j * FC + c + 1)
                        dve.tensor_tensor(gate[:, c % 2, :], sil[:, c % 2, :], banks[c % 2][:, RT:2 * RT],
                                          ALU.mult).then_inc(gd, 1)

                    def lo(j, c):
                        dve.wait_ge(ghi, j * FC + c + 1)
                        dve.tensor_tensor(g_lo[:, c, :], gate[:, c % 2, :], g_hi[:, c, :].bitcast(F32),
                                          ALU.subtract).then_inc(glo, 1)

                    def results(j, par, half):
                        dve.wait_ge(yd, j + 1)
                        dve.wait_ge(ysf, j + 1)
                        dve.tensor_copy(ys[:, par, :].rearrange("p (t d) -> p t d", d=D),
                                        wide[:, 0:512 * TB].rearrange("p (t n) -> p t n", n=512)[:, :, 0:D]).then_inc(ye, 1)
                    rows(0, 0)
                    for k in range(3):
                        split(0, 0, k)

                    def tile(j, par, half, first):
                        gated(j, 0)
                        split(j + 1, 1 - par, 0)
                        gated(j, 1)
                        lo(j, 0)
                        if not first:
                            results(j - 1, 1 - par, half - 1 if par == 0 else half)
                        split(j + 1, 1 - par, 1)
                        gated(j, 2)
                        lo(j, 1)
                        rows(j + 1, 1 - par)
                        gated(j, 3)
                        lo(j, 2)
                        split(j + 1, 1 - par, 2)
                        lo(j, 3)
                    over_tiles(dve, tile)
                    results(NR - 1, 0, NP)

                @blk.tensor
                def _(pe):
                    pe.sem_inc(td, 2)
                    pe.sem_inc(glo, 2)
                    pe.sem_inc(gd, 2)
                    pe.sem_inc(ye, 1)

                    def transposes(j, par, half):
                        pe.wait_ge(rows_in_done[par], 16 * (half + 1))
                        for c in range(DC):
                            for t in range(TB):
                                o = c * RT + t * P
                                m = pe.transpose(tbank[:, o:o + P], xr[:, par, t, c * P:(c + 1) * P], ident[:, :])
                        m.then_inc(td, 1)

                    def hidden(j, par, c):
                        pe.wait_ge(gd, j * FC + c + 1)
                        for which in range(2):
                            for k in range(DC):
                                m = mm3(pe, banks[c % 2][:, which * RT:(which + 1) * RT], up(w_hi, par, which, k, c),
                                        up(w_lo, par, which, k, c), x_hi[:, par, k, :], x_lo[:, par, k, :],
                                        k == 0, k == DC - 1)
                        m.then_inc(hd, 1)

                    def result(j, par, c):
                        if c == 0:
                            pe.wait_ge(w2, j + 1)
                            pe.wait_ge(ye, j + 1)
                        pe.wait_ge(glo, j * FC + c + 1 + 2)
                        for t in range(TB):
                            m = mm3(pe, wide[:, 512 * t:512 * t + D], g_hi[:, c, t * P:(t + 1) * P],
                                    g_lo[:, c, t * P:(t + 1) * P], down(w_hi, par, c), down(w_lo, par, c),
                                    c == 0, c == FC - 1)
                        if c == FC - 1:
                            m.then_inc(yd, 1)

                    transposes(0, 0, 0)

                    def tile(j, par, half, first):
                        pe.wait_ge(xlo, j + 1)
                        pe.wait_ge(w0, j + 1)
                        pe.wait_ge(w1, j + 1)
                        hidden(j, par, 0)
                        if not first:
                            result(j - 1, 1 - par, FC - 2)
                        hidden(j, par, 1)
                        if not first:
                            result(j - 1, 1 - par, FC - 1)
                        transposes(j + 1, 1 - par, half if par == 0 else half + 1)
                        hidden(j, par, 2)
                        result(j, par, 0)
                        hidden(j, par, 3)
                        result(j, par, 1)
                    over_tiles(pe, tile)
                    result(NR - 1, 0, FC - 2)
                    result(NR - 1, 0, FC - 1)

        def ingest(tag, XT_hi, XT_lo, keep=None, statistics=True):
            with ExitStack() as ctx:
                xn = keep if keep is not None else sb(ctx, tag + "xn", [P, 4 * D])
                t_in = sb(ctx, tag + "tin", [P, 4 * D]) if keep is not None else xn
                st, ve, rs, ns, xe, xo, td, hd, ld, kd = sems(
                    ctx, " ".join(tag + s for s in "st ve rs ns xe xo td hd ld kd".split()))
                normalised = (xe, xo)
                blk = ctx.enter_context(nc.Block())
                blk_loads(blk)

                @blk.gpsimd
                def _(pool):
                    if statistics:
                        inverse_deviations(pool, st, ve, rs)
                    if keep is not None:
                        with pool.Fori(0, NT // 4) as j:
                            for q in range(4):
                                pool.wait_ge(normalised[q % 2], j * 4 + q + 1)
                                pool.tensor_copy(keep[:, ds((j * 4 + q) * D, D)], t_in[:, q * D:(q + 1) * D]).then_inc(kd, 1)

                @blk.vector
                def _(dve):
                    if statistics:
                        row_statistics(dve, X, st)
                        dve.wait_ge(rs, NT // 4)
                        dve.wait_ge(st, 2 * NT)
                    shifts(dve).then_inc(ns, 1)

                    def normalise(i, q):
                        dve.tensor_scalar(t_in[:, q * D:(q + 1) * D], X[:, ds(i * D, D)], MV[:, ds(2 * i, 1)],
                                          RSTD[:, ds(i, 1)], ALU.subtract, ALU.mult).then_inc(xe, 2)
                    normalise(0, 0)
                    normalise(2, 2)

                    def low(i, q, more):
                        dve.wait_ge(hd, i + 1)
                        dve.tensor_tensor(XT_lo[:, :, ds(i * P, P)],
                                          banks[q][:, 0:D].rearrange("p (c n) -> p c n", c=DC),
                                          XT_hi[:, :, ds(i * P, P)].bitcast(F32), ALU.subtract).then_inc(ld, 1)
                        if more and q % 2 == 0:
                            if keep is not None:
                                dve.wait_ge(kd, i + 1)
                            normalise(i + 4, q)
                    fours(dve, NT, low)

                @blk.tensor
                def _(pe):
                    pe.sem_inc(ld, 4)

                    def step(i, q, more):
                        pe.wait_ge(normalised[q % 2], i + 1)
                        pe.wait_ge(ld, i + 1)
                        for c in range(DC):
                            t = pe.transpose(banks[q][:, c * P:(c + 1) * P],
                                             t_in[:, q * D + c * P:q * D + (c + 1) * P], ident[:, :])
                        t.then_inc(td, 1)
                    fours(pe, NT, step)

                @blk.scalar
                def _(act):
                    def normalise(i, q):
                        act.activation(t_in[:, q * D:(q + 1) * D], X[:, ds(i * D, D)], ACT.Identity,
                                       bias=SHIFT[:, ds(i, 1)], scale=RSTD[:, ds(i, 1)]).then_inc(xo, 2)
                    act.wait_ge(ns, 1)
                    normalise(1, 1)
                    normalise(3, 3)

                    def high(i, q, more):
                        act.wait_ge(td, i + 1)
                        act.activation(XT_hi[:, :, ds(i * P, P)],
                                       banks[q][:, 0:D].rearrange("p (c n) -> p c n", c=DC), ACT.Copy).then_inc(hd, 1)
                        if more and q % 2:
                            if keep is not None:
                                act.wait_ge(kd, i + 1)
                            normalise(i + 4, q)
                    fours(act, NT, high)

        def slot_pass(tag, n, kc, src_hi, src_lo, stages, by_pairs=None, on_sync=None):
            with ExitStack() as ctx:
                s_hi, s_lo = split_pair(ctx, tag + "slot", [P, 2, kc, P])
                sh, sl = sems(ctx, f"{tag}sh {tag}sl")
                md, ae, de = (sems(ctx, " ".join(f"{tag}{x}{k}" for k in range(len(stages)))) for x in ("md", "ae", "de"))
                last = len(stages) - 1
                pmd, pae, pde = sems(ctx, f"{tag}pmd {tag}pae {tag}pde")
                assert len(stages) == 1 or by_pairs is None

                def width(i):
                    return 1 if isinstance(i, int) and i == n - 1 else 2
                blk = ctx.enter_context(nc.Block())
                blk_loads(blk, (lambda sp: on_sync(sp, de[last])) if on_sync else None)

                @blk.scalar
                def _(act):
                    def fill(i, p):
                        x = src_hi[:, 0:kc, ds(i * P, P)]
                        act.activation(s_hi[:, p, :, :], x if src_lo is None else x.bitcast(F32), ACT.Copy).then_inc(sh, 1)
                    fill(0, 0)
                    fill(1, 1)

                    def step(i, p, more):
                        if by_pairs and p == 0:
                            act.wait_ge(pmd, i + 2)
                            by_pairs[1](act, i, width(i), banks[2:4]).then_inc(pae, 2)
                        for k, (_, act_evac, _) in enumerate(stages):
                            if act_evac or (k == last and more):
                                act.wait_ge(md[k], i + 1)
                            if k == last and more:
                                fill(i + 2, p)
                            if act_evac:
                                act_evac(act, i, p, banks[2 * k + p]).then_inc(ae[k], 1)
                    pairs(act, n, step)

                @blk.vector
                def _(dve):
                    def fill(i, p):
                        if src_lo is None:
                            dve.wait_ge(sh, i + 1)
                            dve.tensor_tensor(s_lo[:, p, :, :], src_hi[:, 0:kc, ds(i * P, P)],
                                              s_hi[:, p, :, :].bitcast(F32), ALU.subtract).then_inc(sl, 1)
                        else:
                            dve.tensor_copy(s_lo[:, p, :, :], src_lo[:, 0:kc, ds(i * P, P)]).then_inc(sl, 1)
                    fill(0, 0)
                    fill(1, 1)

                    def step(i, p, more):
                        if by_pairs and p == 0:
                            dve.wait_ge(pae, i + 2)
                            by_pairs[2](dve, i, width(i), banks[2:4]).then_inc(pde, 2)
                        for k, (_, act_evac, dve_evac) in enumerate(stages):
                            if k == last and more:
                                dve.wait_ge(md[k], i + 1)
                                fill(i + 2, p)
                            dve.wait_ge(ae[k] if act_evac else md[k], i + 1)
                            dve_evac(dve, i, p, banks[2 * k + p]).then_inc(de[k], 1)
                    pairs(dve, n, step)

                @blk.tensor
                def _(pe):
                    for k in range(len(stages)):
                        pe.sem_inc(de[k], 2)
                    if by_pairs:
                        pe.sem_inc(pde, 2)

                    def step(i, p, more):
                        if by_pairs and p == 0:
                            pe.wait_ge(pde, i + 2)
                            by_pairs[0](pe, i, width(i), banks[2:4]).then_inc(pmd, 2)
                        pe.wait_ge(sh, i + 1)
                        pe.wait_ge(sl, i + 1)
                        for k, (products, _, _) in enumerate(stages):
                            pe.wait_ge(de[k], i + 1)
                            products(pe, banks[2 * k + p], s_hi[:, p, :, :], s_lo[:, p, :, :]).then_inc(md[k], 1)
                    pairs(pe, n, step)

        def attention(tag, nq, Q_hi, Q_lo, Wq_hi, Wq_lo, bq, kc, scale, nk, nk_cols, K_hi, K_lo, V_hi, V_lo, vw,
                      finish_act, finish_dve, on_sync=None):
            G = -(-nk // 4)
            assert G == 4
            widths = [min(512, nk_cols + nk_cols % 2 - 512 * g) for g in range(G)]
            with ExitStack() as ctx:
                prob = sb(ctx, tag + "prob", [P, 2, nk * P])
                pt = sb(ctx, tag + "pt", [P, nk, 2, P], F32R)
                q_hi, q_lo = split_pair(ctx, tag + "q", [P, 2, kc, P])
                part = sb(ctx, tag + "part", [P, 4])
                top1 = sb(ctx, tag + "top1", [P, 1])
                nmax = sb(ctx, tag + "nmax", [P, 1])
                rsum = sb(ctx, tag + "rsum", [P, 2, nq])
                total = sb(ctx, tag + "total", [P, 1])
                inverse = sb(ctx, tag + "inverse", [P, 1])
                (s_done, t_done, pv_done, q_done, thi, tlo, qhi, qlo, mx, exp_done, o_free, f_act, chain, inv_done) = sems(
                    ctx, " ".join(tag + s for s in
                                  "s t pv q thi tlo qhi qlo mx ex of fa ch iv".split()))
                tb = [banks[0], banks[1]]
                ob, qb = banks[2], banks[3]
                blk = ctx.enter_context(nc.Block())
                if on_sync:
                    blk.sync(lambda sp: on_sync(sp, o_free))

                def weights(g, part):
                    return pt[:, 4 * g:min(4 * g + 4, nk), part, :]

                def transposed(g):
                    return tb[g % 2][:, 0:(min(4 * g + 4, nk) - 4 * g) * P].rearrange("p (k n) -> p k n", n=P)

                def pair_width(i):
                    return 1 if isinstance(i, int) and i == nq - 1 else 2

                def queries(t, h, w):
                    return t[:, 0:w, h, :]

                def projected(h, w):
                    return qb[:, h * 2 * P:h * 2 * P + w * P].rearrange("p (t n) -> p t n", n=P)

                @blk.tensor
                def _(pe):
                    pe.sem_inc(tlo, 2)
                    pe.sem_inc(o_free, 1)

                    def project(i):
                        w = pair_width(i)
                        for h in range(kc):
                            for c in range(DC):
                                m = mm3(pe, qb[:, h * 2 * P:h * 2 * P + w * P],
                                        Wq_hi[:, c, h * P:(h + 1) * P], Wq_lo[:, c, h * P:(h + 1) * P],
                                        Q_hi[:, c, ds(i * P, w * P)], Q_lo[:, c, ds(i * P, w * P)], c == 0, c == DC - 1)
                        m.then_inc(q_done, 2)

                    def scores(i, p, g):
                        for c in range(kc):
                            m = mm3(pe, wide[:, 512 * g:512 * g + widths[g]], q_hi[:, p, c, :], q_lo[:, p, c, :],
                                    K_hi[:, c, 512 * g:512 * g + widths[g]], K_lo[:, c, 512 * g:512 * g + widths[g]],
                                    c == 0, c == kc - 1)
                        m.then_inc(s_done, 1)

                    def transposes(i, p, g):
                        pe.wait_ge(tlo, i * G + g + 1)
                        for k in range(4 * g, min(4 * g + 4, nk)):
                            m = pe.transpose(tb[g % 2][:, (k % 4) * P:(k % 4 + 1) * P], prob[:, p, k * P:(k + 1) * P],
                                             ident[:, :])
                        m.then_inc(t_done, 1)

                    def weighted(i, g):
                        if g == 0:
                            pe.wait_ge(o_free, i + 1)
                        pe.wait_ge(tlo, i * G + g + 1 + 2)
                        for k in range(4 * g, min(4 * g + 4, nk)):
                            hi, lo = pt[:, k, 0, :], pt[:, k, 1, :]
                            if vw == D:
                                m = mm3(pe, ob[:, 0:D], hi, lo, V_hi[:, k, :], V_lo[:, k, :], k == 0, k == nk - 1)
                            else:
                                both = pt[:, k, :, :].rearrange("p h n -> p (h n)")
                                pe.matmul(ob[:, 0:2 * P], V_hi[:, k, :], both, start=k == 0, stop=False)
                                m = pe.matmul(ob[:, 0:2 * P], V_lo[:, k, :], both, start=False, stop=k == nk - 1)
                        if g == G - 1:
                            m.then_inc(pv_done, 1)

                    def turn(i, p, more):
                        pe.wait_ge(exp_done, i)
                        pe.wait_ge(qhi, i + 1)
                        pe.wait_ge(qlo, i + 1)
                        for g in range(G):
                            scores(i, p, g)
                        if more and p:
                            project(i + 1)
                        for g in range(G):
                            weighted(i - 2, g)
                            transposes(i - 1, 1 - p, g)

                    project(0)
                    pe.wait_ge(qhi, 1)
                    pe.wait_ge(qlo, 1)
                    for g in range(G):
                        scores(0, 0, g)
                    pe.wait_ge(exp_done, 1)
                    for g in range(G):
                        scores(1, 1, g)
                    project(2)
                    for g in range(G):
                        transposes(0, 0, g)
                    turns(pe, nq, turn)
                    pe.wait_ge(exp_done, nq)
                    for g in range(G):
                        weighted(nq - 2, g)
                        transposes(nq - 1, (nq - 1) % 2, g)
                    for g in range(G):
                        weighted(nq - 1, g)

                @blk.scalar
                def _(act):
                    def query(i):
                        act.wait_ge(q_done, i + 1)
                        w = pair_width(i)
                        for h in range(kc):
                            m = act.activation(queries(q_hi, h, w), projected(h, w), ACT.Identity,
                                               bias=bq[:, h:h + 1] if bq is not None else 0.0)
                        m.then_inc(qhi, 2)

                    def high(i, g):
                        act.wait_ge(t_done, i * G + g + 1)
                        act.activation(weights(g, 0), transposed(g), ACT.Copy).then_inc(thi, 1)

                    def exponent(i, p, half):
                        if half == 0:
                            act.wait_ge(mx, i + 1)
                        keys = slice(0, 1024) if half == 0 else slice(1024, nk_cols)
                        m = act.activation(prob[:, p, keys], wide[:, keys], ACT.Exp, bias=nmax[:, 0:1],
                                           scale=scale, accum_out=rsum[:, half, ds(i, 1)])
                        if half == 1:
                            m.then_inc(exp_done, 1)

                    def finish(i):
                        if finish_act:
                            act.wait_ge(pv_done, i + 1)
                            finish_act(act, i, ob).then_inc(f_act, 1)

                    def turn(i, p, more):
                        if more and p:
                            query(i + 1)
                        high(i - 1, 0)
                        exponent(i, p, 0)
                        high(i - 1, 1)
                        exponent(i, p, 1)
                        high(i - 1, 2)
                        finish(i - 2)
                        high(i - 1, 3)

                    query(0)
                    exponent(0, 0, 0)
                    exponent(0, 0, 1)
                    query(2)
                    exponent(1, 1, 0)
                    exponent(1, 1, 1)
                    for g in range(G):
                        high(0, g)
                    turns(act, nq, turn)
                    for g in range(3):
                        high(nq - 1, g)
                    finish(nq - 2)
                    high(nq - 1, 3)
                    finish(nq - 1)

                @blk.vector
                def _(dve):
                    if nk * P > nk_cols:
                        dve.memset(prob[:, :, nk_cols:nk * P], 0.0).then_inc(chain, 1)
                    else:
                        dve.memset(part[:, :], 0.0).then_inc(chain, 1)
                    dve.wait_ge(chain, 1)

                    def query(i):
                        dve.wait_ge(qhi, i + 1)
                        w = pair_width(i)
                        for h in range(kc):
                            if bq is not None:
                                m = dve.scalar_tensor_tensor(out=queries(q_lo, h, w), in0=projected(h, w),
                                                             scalar=bq[:, h:h + 1], in1=queries(q_hi, h, w).bitcast(F32),
                                                             op0=ALU.add, op1=ALU.subtract)
                            else:
                                m = dve.tensor_tensor(queries(q_lo, h, w), projected(h, w),
                                                      queries(q_hi, h, w).bitcast(F32), ALU.subtract)
                        m.then_inc(qlo, 2)

                    def low(i, g):
                        dve.wait_ge(thi, i * G + g + 1)
                        dve.tensor_tensor(weights(g, 1), transposed(g), weights(g, 0).bitcast(F32),
                                          ALU.subtract).then_inc(tlo, 1)

                    def maximum(i, g):
                        dve.wait_ge(s_done, i * G + g + 1)
                        dve.reduce_max(part[:, g:g + 1], wide[:, 512 * g:512 * g + min(512, nk_cols - 512 * g)],
                                       AX).then_inc(chain, 1)

                    def whole_maximum(i):
                        dve.wait_ge(chain, i * (G + 1) + G + 1)
                        dve.reduce_max(top1[:, :], part[:, 0:G], AX).then_inc(chain, 1)
                        dve.wait_ge(chain, (i + 1) * (G + 1) + 1)
                        dve.tensor_scalar(nmax[:, :], top1[:, :], -scale, None, ALU.mult).then_inc(mx, 1)

                    def finish(i):
                        dve.wait_ge(exp_done, i + 1)
                        dve.tensor_tensor(total[:, :], rsum[:, 0, ds(i, 1)], rsum[:, 1, ds(i, 1)], ALU.add)\
                           .then_inc(inv_done, 1)
                        dve.wait_ge(inv_done, 2 * i + 1)
                        dve.reciprocal(inverse[:, :], total[:, :]).then_inc(inv_done, 1)
                        dve.wait_ge(inv_done, 2 * i + 2)
                        if finish_act:
                            dve.wait_ge(f_act, i + 1)
                        else:
                            dve.wait_ge(pv_done, i + 1)
                        finish_dve(dve, i, ob, inverse[:, :]).then_inc(o_free, 1)

                    def scored(i, more):
                        for g in range(G):
                            maximum(i, g)
                        whole_maximum(i)
                        if more:
                            query(i + 1)

                    def turn(i, p, more):
                        scored(i, more and p)
                        for g in range(3):
                            low(i - 1, g)
                        finish(i - 2)
                        low(i - 1, 3)

                    query(0)
                    scored(0, False)
                    scored(1, True)
                    for g in range(G):
                        low(0, g)
                    turns(dve, nq, turn)
                    for g in range(3):
                        low(nq - 1, g)
                    finish(nq - 2)
                    low(nq - 1, 3)
                    finish(nq - 1)

        def row_logits(tag, W, XT_hi, XT_lo, LG, bias):
            wh, wl, raw, loaded = W
            NB = S // 512
            with ExitStack() as ctx:
                by_expert = sb(ctx, tag + "by_expert", [E, S])
                wd, lgd, cpd, tpd = sems(ctx, " ".join(tag + s for s in "wd lgd cpd tpd".split()))
                blk = ctx.enter_context(nc.Block())

                @blk.scalar
                def _(act):
                    act.wait_ge(loaded, 16)
                    act.activation(wh, raw, ACT.Copy).then_inc(wd, 1)
                    for b in range(NB):
                        act.wait_ge(lgd, b + 1)
                        act.activation(by_expert[:, 512 * b:512 * b + 512], banks[b][0:E, :], ACT.Copy).then_inc(cpd, 1)

                @blk.vector
                def _(dve):
                    dve.wait_ge(wd, 1)
                    dve.tensor_tensor(wl, raw, wh.bitcast(F32), ALU.subtract).then_inc(wd, 1)
                    dve.wait_ge(tpd, 1)
                    got = wide[:, 0:NT * E].rearrange("p (i e) -> p i e", e=E)
                    if bias is None:
                        dve.tensor_copy(LG[:, :, :], got)
                    else:
                        dve.tensor_tensor(LG[:, :, :], got, bias.unsqueeze(1).to_broadcast([P, NT, E]), ALU.add)

                @blk.tensor
                def _(pe):
                    pe.wait_ge(wd, 2)
                    for b in range(NB):
                        for c in range(DC):
                            x = slice(512 * b, 512 * b + 512)
                            m = mm3(pe, banks[b][0:E, :], wh[:, c, :], wl[:, c, :], XT_hi[:, c, x], XT_lo[:, c, x],
                                    c == 0, c == 1)
                        m.then_inc(lgd, 1)
                    for i in range(NT):
                        if i % 4 == 0:
                            pe.wait_ge(cpd, i // 4 + 1)
                        m = pe.transpose(wide[:, i * E:(i + 1) * E], by_expert[:, i * P:(i + 1) * P], ident[0:E, 0:E])
                    m.then_inc(tpd, 1)

        def moe_phase():
            rows_out = nc.dram_tensor("routed_results", (NR * RT, D), F32, kind="Internal").ap()
            with ExitStack() as ph:
                w12 = sb(ph, "w12", [P, 2, NT])
                pos = sb(ph, "pos", [P, 2, NT], mybir.dt.uint32)
                table = sb(ph, "table", [P, NR + 1], I32)
                XT_hi, XT_lo = split_pair(ph, "XT1", [P, DC, S])
                W = request(ph, "wr", {"L0_ffn_router_wT": (DC, E)})
                raw = sb(ph, "sraw", [P, 2 * DC * F + F // P * D])
                loaded = request_shared(ph, "s0", E, raw)
                s_ex = ph.enter_context(ExitStack())
                XN = sb(s_ex, "XN", [P, NT * D])
                ingest("i1", XT_hi, XT_lo, XN)
                with ExitStack() as ctx:
                    LG = sb(ctx, "LG", [P, NT, E])
                    row_logits("rl", W["L0_ffn_router_wT"], XT_hi, XT_lo, LG, BIASE)

                    rank = sb(ctx, "rank", [P, NT, E])
                    ranki = sb(ctx, "ranki", [P, NT, E], I32)
                    t3, LG2, oh1, oh2, before, slot = (sb(ctx, n, [P, NT, E]) for n in
                                                       ("t3", "LG2", "oh1", "oh2", "before", "slot"))
                    chosen = sb(ctx, "chosen", [P, NT, E], F32R)
                    m1, m2, tm, dd, ex = (sb(ctx, n, [P, NT]) for n in ("m1", "m2", "tm", "dd", "ex"))
                    count_e, tiles_e, first_e, end_e = (sb(ctx, n, [P, E]) for n in ("cnt", "tls", "fst", "end"))
                    lim = sb(ctx, "lim", [P, E, E])
                    limi = sb(ctx, "limi", [P, E, E], I32)
                    tl = sb(ctx, "tl", [P, NR + 1, E])
                    tli = sb(ctx, "tli", [P, NR + 1, E], I32)
                    cmp8 = sb(ctx, "cmp8", [P, E, E])
                    te = sb(ctx, "te", [P, NR + 1])
                    ones = sb(ctx, "ones", [P, P])
                    ones_r = sb(ctx, "ones_r", [P, P], F32R)
                    below = sb(ctx, "below", [P, P], F32R)
                    rk, ch, xp, pm = sems(ctx, "rk rch rxp rpm")
                    blk = ctx.enter_context(nc.Block())

                    def wide3(t, n=NT):
                        return t.unsqueeze(2).to_broadcast([P, n, E])

                    @blk.gpsimd
                    def _(pool):
                        pool.iota(ranki[:, :, :], pattern=[[0, NT], [-1, E]], base=E, channel_multiplier=0).then_inc(rk, 1)
                        pool.iota(limi[:, :, :], pattern=[[0, E], [RT, E]], base=0, channel_multiplier=0).then_inc(rk, 1)
                        pool.iota(tli[:, :, :], pattern=[[1, NR + 1], [0, E]], base=0, channel_multiplier=0).then_inc(rk, 1)
                        pool.memset(ones[:, :], 1.0).then_inc(rk, 1)
                        pool.wait_ge(rk, 4)
                        pool.affine_select(out=below[:, :], in_=ones[:, :], compare_op=ALU.is_gt, fill=0.0, base=0,
                                           pattern=[[1, P]], channel_multiplier=-1).then_inc(rk, 1)

                    @blk.scalar
                    def _(act):
                        act.wait_ge(rk, 4)
                        act.activation(ones_r[:, :], ones[:, :], ACT.Copy).then_inc(pm, 1)
                        act.wait_ge(xp, 1)
                        act.activation(ex[:, :], dd[:, :], ACT.Exp).then_inc(xp, 1)

                    @blk.tensor
                    def _(pe):
                        pe.wait_ge(rk, 5)
                        pe.wait_ge(pm, 2)
                        m = chosen[:, :, :].rearrange("p i e -> p (i e)")
                        pe.matmul(banks[0][:, 0:NT * E], below[:, :], m, start=True, stop=True)
                        pe.matmul(banks[1][:, 0:NT * E], ones_r[:, :], m, start=True, stop=True).then_inc(pm, 1)

                    @blk.vector
                    def _(dve):
                        count = [0]

                        def link(ins):
                            count[0] += 1
                            ins.then_inc(ch, 1)
                            dve.wait_ge(ch, count[0])

                        def first_of_largest(logits, m, oh):
                            link(dve.reduce_max(m[:, :], logits, AX))
                            link(dve.tensor_tensor(t3[:, :, :], logits, wide3(m[:, :]), ALU.is_equal))
                            link(dve.tensor_tensor(t3[:, :, :], t3[:, :, :], rank[:, :, :], ALU.mult))
                            link(dve.reduce_max(tm[:, :], t3[:, :, :], AX))
                            link(dve.tensor_tensor(oh[:, :, :], rank[:, :, :], wide3(tm[:, :]), ALU.is_equal))
                        dve.wait_ge(rk, 5)
                        link(dve.tensor_copy(rank[:, :, :], ranki[:, :, :]))
                        link(dve.tensor_copy(lim[:, :, :], limi[:, :, :]))
                        link(dve.tensor_copy(tl[:, :, :], tli[:, :, :]))
                        first_of_largest(LG[:, :, :], m1, oh1)
                        link(dve.scalar_tensor_tensor(out=LG2[:, :, :], in0=oh1[:, :, :], scalar=-BIG, in1=LG[:, :, :],
                                                      op0=ALU.mult, op1=ALU.add))
                        first_of_largest(LG2[:, :, :], m2, oh2)
                        dve.tensor_tensor(dd[:, :], m2[:, :], m1[:, :], ALU.subtract).then_inc(xp, 1)
                        dve.wait_ge(pm, 1)
                        dve.tensor_tensor(chosen[:, :, :], oh1[:, :, :], oh2[:, :, :], ALU.add).then_inc(pm, 1)
                        dve.wait_ge(xp, 2)
                        link(dve.tensor_scalar(tm[:, :], ex[:, :], 1.0, None, ALU.add))
                        link(dve.reciprocal(w12[:, 0, :], tm[:, :]))
                        link(dve.tensor_tensor(w12[:, 1, :], ex[:, :], w12[:, 0, :], ALU.mult))
                        dve.wait_ge(pm, 3)
                        link(dve.memset(before[:, 0, :], 0.0))
                        for i in range(1, NT):
                            link(dve.tensor_tensor(before[:, i, :], before[:, i - 1, :], banks[1][:, (i - 1) * E:i * E],
                                                   ALU.add))
                        link(dve.tensor_tensor(count_e[:, :], before[:, NT - 1, :], banks[1][:, (NT - 1) * E:NT * E], ALU.add))
                        link(dve.tensor_tensor(cmp8[:, :, :], wide3(count_e[:, :], E), lim[:, :, :], ALU.is_gt))
                        link(dve.reduce_sum(tiles_e[:, :], cmp8[:, :, :], AX))
                        link(dve.memset(first_e[:, 0:1], 0.0))
                        for e in range(1, E):
                            link(dve.tensor_tensor(first_e[:, e:e + 1], first_e[:, e - 1:e], tiles_e[:, e - 1:e], ALU.add))
                        link(dve.tensor_tensor(end_e[:, :], first_e[:, :], tiles_e[:, :], ALU.add))
                        link(dve.tensor_tensor(before[:, :, :], before[:, :, :],
                                               banks[0][:, 0:NT * E].rearrange("p (i e) -> p i e", e=E), ALU.add))
                        link(dve.scalar_tensor_tensor(out=slot[:, :, :], in0=first_e[:, :].unsqueeze(1).to_broadcast([P, NT, E]),
                                                      scalar=float(RT), in1=before[:, :, :], op0=ALU.mult, op1=ALU.add))
                        for k, oh in enumerate((oh1, oh2)):
                            link(dve.tensor_tensor(t3[:, :, :], oh[:, :, :], slot[:, :, :], ALU.mult))
                            link(dve.reduce_sum(tm[:, :], t3[:, :, :], AX))
                            link(dve.tensor_copy(pos[:, k, :], tm[:, :]))
                        link(dve.tensor_tensor(tl[:, :, :], end_e[:, :].unsqueeze(1).to_broadcast([P, NR + 1, E]),
                                               tl[:, :, :], ALU.is_le))
                        link(dve.reduce_sum(te[:, :], tl[:, :, :], AX))
                        link(dve.tensor_scalar(te[:, :], te[:, :], float(E - 1), None, ALU.min))
                        link(dve.tensor_copy(table[:, :], te[:, :]))

                (weighed,) = sems(ph, "weighed")

                def scatter(pool):
                    for k in range(2):
                        for i in range(NT):
                            pool.indirect_dma_start(rows_in[:, :], bass.IndirectOffsetOnAxis(ap=pos[:, k, i:i + 1], axis=0),
                                                    XN[:, i * D:(i + 1) * D], None).then_inc(scattered, 16)
                    pool.wait_ge(scattered, 16 * 2 * NT)
                shared_expert("s0", raw, loaded, XT_hi, XT_lo, on_pool=scatter)
                s_ex.close()
                loaded = request_shared(ph, "s1", E + 1, raw)
                routed_experts(table, rows_in, rows_out)
                with ExitStack() as s_ex:
                    back = sb(s_ex, "back", [P, 2, NT, D])

                    def gather(pool):
                        for i in range(NT):
                            for k in range(2):
                                pool.indirect_dma_start(back[:, k, i, :], None, rows_out[:, :],
                                                        bass.IndirectOffsetOnAxis(ap=pos[:, k, i:i + 1], axis=0))\
                                    .then_inc(gathered, 16)
                        pool.wait_ge(gathered, 16 * 2 * NT)
                        for k in range(2):
                            for i in range(NT):
                                pool.tensor_scalar(back[:, k, i, :], back[:, k, i, :], w12[:, k, i:i + 1], None,
                                                   ALU.mult).then_inc(weighed, 1)

                    def combine(dve, done, n):
                        dve.wait_ge(done, n)
                        for k in range(2):
                            dve.wait_ge(weighed, (k + 1) * NT)
                            for i in range(0, NT, 4):
                                x = X[:, i * D:(i + 4) * D].rearrange("p (i d) -> p i d", d=D)
                                m = dve.tensor_tensor(x, x, back[:, k, i:i + 4, :], ALU.add)
                            if k == 0:
                                m.then_inc(done, 1)
                                dve.wait_ge(done, n + 1)
                    shared_expert("s1", raw, loaded, XT_hi, XT_lo, on_pool=gather, after=combine)

        def cross_phase():
            with ExitStack() as ph:
                C2S = sb(ph, "C2S", [P, NT * D])
                scratch = nc.dram_tensor("s2c_rows", (1 + CP, D), F32, kind="Internal").ap()
                with ExitStack() as mid:
                    K_hi, K_lo = split_pair(mid, "K1", [P, DC, S])
                    V_hi, V_lo = split_pair(mid, "V1", [P, NT, D])

                    def keys_values(tag, n, src_hi, src_lo, W, bk):
                        (kh, kl), (vh, vl) = (m[:2] for m in W.values())

                        def k_products(pe, i, w, two):
                            for h in range(DC):
                                for c in range(DC):
                                    x = ds(i * P, w * P)
                                    m = mm3(pe, two[h][:, 0:w * P], kh[:, c, h * P:(h + 1) * P],
                                            kl[:, c, h * P:(h + 1) * P], src_hi[:, c, x], src_lo[:, c, x], c == 0, c == 1)
                            return m

                        def v_products(pe, bank, sh, sl):
                            for c in range(DC):
                                m = mm3(pe, bank[:, 0:D], sh[:, c, :], sl[:, c, :], vh[:, c, :], vl[:, c, :],
                                        c == 0, c == 1)
                            return m

                        def k_hi(act, i, w, two):
                            for h in range(DC):
                                m = act.activation(K_hi[:, h, ds(i * P, w * P)], two[h][:, 0:w * P], ACT.Identity,
                                                   bias=bk[:, h:h + 1])
                            return m

                        def k_lo(dve, i, w, two):
                            for h in range(DC):
                                k = K_hi[:, h, ds(i * P, w * P)].bitcast(F32)
                                m = dve.scalar_tensor_tensor(out=K_lo[:, h, ds(i * P, w * P)], in0=two[h][:, 0:w * P],
                                                             scalar=bk[:, h:h + 1], in1=k, op0=ALU.add, op1=ALU.subtract)
                            return m

                        def v_hi(act, i, p, bank):
                            return act.activation(V_hi[:, ds(i, 1), :], bank[:, 0:D].unsqueeze(1), ACT.Copy)

                        def v_lo(dve, i, p, bank):
                            return dve.tensor_tensor(V_lo[:, ds(i, 1), :], bank[:, 0:D].unsqueeze(1),
                                                     V_hi[:, ds(i, 1), :].bitcast(F32), ALU.subtract)
                        slot_pass(tag, n, DC, src_hi, src_lo, [(v_products, v_hi, v_lo)], (k_products, k_hi, k_lo))

                    def finish_into(dst, bv):
                        def finish(dve, i, bank, rinv):
                            return dve.scalar_tensor_tensor(out=dst[:, ds(i * D, D)], in0=bank[:, 0:D], scalar=rinv, in1=bv,
                                                            op0=ALU.mult, op1=ALU.add)
                        return finish

                    scale = D ** -0.5
                    with ExitStack() as q1:
                        XT_hi, XT_lo = split_pair(q1, "XT2", [P, DC, S])
                        with ExitStack() as ctx:
                            Ws = request(ctx, "wks", {"L1_xattn_Wk_sT": (DC, D), "L1_xattn_Wv_sT": (DC, D)})
                            ingest("i2", XT_hi, XT_lo)
                            split_now("wks", Ws)
                            keys_values("ks", NC, CT_hi, CT_lo, Ws, BKS)
                        with ExitStack() as ctx:
                            with ExitStack() as until:
                                W = request(ctx, "wac", {"L1_xattn_Wq_cT": (DC, D), "L1_xattn_Wk_cT": (DC, D),
                                                         "L1_xattn_Wv_cT": (DC, D)}, until)
                                split_now("wac", W)
                            Wq = {"L1_xattn_Wq_cT": W.pop("L1_xattn_Wq_cT")}
                            attention("ac", NT, XT_hi, XT_lo, *Wq["L1_xattn_Wq_cT"][:2], BQC, DC, scale, NC, C, K_hi, K_lo,
                                      V_hi, V_lo, D, None, finish_into(C2S, BV_S))
                            keys_values("kc", NT, XT_hi, XT_lo, W, BKC)
                    o_s2c = sb(mid, "o_s2c", [P, NC * D])
                    (stored_rows,) = sems(mid, "stored_rows")

                    def store_rows(sp, finished):
                        sp.dma_start(scratch[0:1, :].rearrange("a (p n) -> (a p) n", p=P),
                                     CT_hi[:, 0, C:C + D // P].bitcast(F32)).then_inc(stored_rows, 16)
                        with sp.Fori(0, NC) as i:
                            sp.wait_ge(finished, i + 2)
                            sp.dma_start(scratch[ds(i * P + 1, P), :], o_s2c[:, ds(i * D, D)]).then_inc(stored_rows, 16)
                        sp.wait_ge(stored_rows, 16 * (NC + 1))

                    with ExitStack() as ctx:
                        Wq = request(ctx, "wqs", {"L1_xattn_Wq_sT": (DC, D)})
                        split_now("wqs", Wq)
                        attention("as", NC, CT_hi, CT_lo, *Wq["L1_xattn_Wq_sT"][:2], BQS, DC, scale, NT, S, K_hi, K_lo,
                                  V_hi, V_lo, D, None, finish_into(o_s2c, BV_C), on_sync=store_rows)
                STEP = P * C // S
                Wg = request(ph, "wg", {"L1_xattn_WgT": (2 * DC, D)})
                S2CI = sb(ph, "S2CI", [P, NT * D])
                with ExitStack() as ctx:
                    tent = sb(ctx, "tent", [P, NT * P], F32R)
                    win_hi, win_lo = split_pair(ctx, "win", [P, NT * D])
                    with ExitStack() as c2:
                        win = sb(c2, "win", [P, NT * D])
                        posi = sb(c2, "posi", [P, S], I32)
                        keyi = sb(c2, "keyi", [P, NT], I32)
                        pos = sb(c2, "ipos", [P, S])
                        away = sb(c2, "away", [P, S])
                        key = sb(c2, "ikey", [P, NT])
                        io, cc, rr, wh = sems(c2, "io icc irr iwh")
                        window_read = sems(c2, "iw0 iw1 iw2 iw3")
                        blk = c2.enter_context(nc.Block())

                        def four(t, g):
                            return t[:, g * 4 * D:(g + 1) * 4 * D]

                        def read_windows(eng, groups):
                            for g in groups:
                                for i in range(4 * g, 4 * g + 4):
                                    eng.dma_start(win[:, i * D:(i + 1) * D], scratch[i * STEP:i * STEP + P, :])\
                                       .then_inc(window_read[g], 16)

                        @blk.sync
                        def _(sp):
                            read_windows(sp, (0, 1))

                        @blk.gpsimd
                        def _(pool):
                            pool.iota(posi[:, :], pattern=[[2 * C, S]], base=C - S, channel_multiplier=0).then_inc(io, 1)
                            pool.iota(keyi[:, :], pattern=[[STEP, NT]], base=-1, channel_multiplier=1).then_inc(io, 1)

                        @blk.vector
                        def _(dve):
                            dve.wait_ge(io, 2)
                            dve.tensor_copy(pos[:, :], posi[:, :]).then_inc(cc, 1)
                            dve.tensor_copy(key[:, :], keyi[:, :]).then_inc(cc, 1)
                            dve.wait_ge(cc, 2)
                            dve.tensor_scalar(pos[:, :], pos[:, :], 0.5 / S, 0.0, ALU.mult, ALU.max).then_inc(cc, 1)
                            dve.wait_ge(cc, 3)
                            dve.scalar_tensor_tensor(out=away[:, :].rearrange("p (i n) -> p i n", n=P),
                                                     in0=pos[:, :].rearrange("p (i n) -> p i n", n=P), scalar=float(C - 1),
                                                     in1=key[:, :].unsqueeze(2).to_broadcast([P, NT, P]),
                                                     op0=ALU.min, op1=ALU.subtract).then_inc(cc, 1)
                            for n, g in enumerate((0, 2, 1, 3)):
                                dve.wait_ge(wh, n + 1)
                                dve.tensor_tensor(four(win_lo, g), four(win, g), four(win_hi, g).bitcast(F32), ALU.subtract)

                        @blk.scalar
                        def _(act):
                            read_windows(act, (2, 3))

                            def high(g):
                                act.wait_ge(window_read[g], 64)
                                act.activation(four(win_hi, g), four(win, g), ACT.Copy).then_inc(wh, 1)
                            high(0)
                            high(2)
                            act.wait_ge(cc, 4)
                            act.activation(pos[:, :], away[:, :], ACT.Abs).then_inc(rr, 1)
                            act.wait_ge(rr, 1)
                            act.activation(tent[:, :], pos[:, :], ACT.Relu, bias=1.0, scale=-1.0).then_inc(rr, 1)
                            high(1)
                            high(3)

                    t_slot = sb(ctx, "t_slot", [P, 2 * P], F32R)
                    ts, md, de = sems(ctx, "w_t w_md w_de")
                    blk = ctx.enter_context(nc.Block())

                    @blk.vector
                    def _(dve):
                        def fill(i, p):
                            dve.tensor_copy(t_slot[:, p * P:(p + 1) * P], tent[:, ds(i * P, P)]).then_inc(ts, 1)
                        fill(0, 0)
                        fill(1, 1)

                        def step(i, p, more):
                            dve.wait_ge(md, i + 1)
                            if more:
                                fill(i + 2, p)
                            dve.tensor_copy(S2CI[:, ds(i * D, D)], banks[p][:, 0:D]).then_inc(de, 1)
                        pairs(dve, NT, step)

                    @blk.tensor
                    def _(pe):
                        pe.sem_inc(de, 2)

                        def step(i, p, more):
                            pe.wait_ge(ts, i + 1)
                            pe.wait_ge(de, i + 1)
                            t = t_slot[:, p * P:(p + 1) * P]
                            pe.matmul(banks[p][:, 0:D], t, win_hi[:, ds(i * D, D)], start=True, stop=False)
                            pe.matmul(banks[p][:, 0:D], t, win_lo[:, ds(i * D, D)], start=False, stop=True).then_inc(md, 1)
                        pairs(pe, NT, step)

                with ExitStack() as ctx:
                    gh, gl = Wg["L1_xattn_WgT"][:2]
                    LGT = sb(ctx, "LGT", [P, NT * D])
                    DIF = sb(ctx, "DIF", [P, NT * D])

                    def differences(pool):
                        for j in range(4):
                            sl = slice(j * 4 * D, (j + 1) * 4 * D)
                            pool.tensor_tensor(DIF[:, sl], C2S[:, sl], S2CI[:, sl], ALU.subtract)
                            pool.tensor_tensor(X[:, sl], X[:, sl], S2CI[:, sl], ALU.add)

                    def source(i):
                        return [C2S[:, ds(i * D, D)], S2CI[:, ds(i * D, D)]]

                    def products(pe, bank, sh, sl):
                        for c in range(2 * DC):
                            m = mm3(pe, bank[:, 0:D], sh[:, c, :], sl[:, c, :], gh[:, c, :], gl[:, c, :], c == 0, c == 3)
                        return m

                    def evac(dve, i, p, bank):
                        return dve.tensor_tensor(LGT[:, ds(i * D, D)], bank[:, 0:D], BG, ALU.add)
                    split_now("wg", Wg)
                    transpose_pass("gt", NT, 2 * DC, source, products, evac, on_pool=differences)

                    th = LGT
                    a, b, c = sems(ctx, "ga gb gc")
                    blk = ctx.enter_context(nc.Block())

                    @blk.scalar
                    def _(act):
                        with act.Fori(0, NT // 4) as i:
                            act.activation(th[:, ds(i * 4 * D, 4 * D)], LGT[:, ds(i * 4 * D, 4 * D)], ACT.Tanh,
                                           scale=0.5).then_inc(a, 1)

                    @blk.vector
                    def _(dve):
                        with dve.Fori(0, NT // 4) as i:
                            sl = ds(i * 4 * D, 4 * D)
                            dve.wait_ge(a, i + 1)
                            dve.scalar_tensor_tensor(out=th[:, sl], in0=th[:, sl], scalar=1.0, in1=DIF[:, sl], op0=ALU.add,
                                                     op1=ALU.mult).then_inc(b, 1)
                            dve.wait_ge(b, i + 1)
                            dve.scalar_tensor_tensor(out=X[:, sl], in0=th[:, sl], scalar=0.5, in1=X[:, sl], op0=ALU.mult,
                                                     op1=ALU.add)

        def last_phase():
            with ExitStack() as ph:
                Wg = request(ph, "wlg", {"L1_ffn_gate_WT": (DC, E)})["L1_ffn_gate_WT"]
                W = request(ph, "wl", {"expert01": (2 * DC, D), "L1_ffn_out_WT": (DC, D)})
                SC = sb(ph, "SC", [P, 2, NT])
                LG = sb(ph, "LG3", [P, NT, E])
                EW_hi, EW_lo = split_pair(ph, "EW", [P, DC, 2, D])
                XT_hi, XT_lo = split_pair(ph, "XT3", [P, DC, S])
                ingest("i3", XT_hi, XT_lo)
                split_now("wl", W)
                (eh, el), (oh, ol) = (m[:2] for m in W.values())
                row_logits("gl", Wg, XT_hi, XT_lo, LG, None)
                with ExitStack() as ctx:
                    PR = sb(ctx, "PR3", [P, NT, E])
                    m1, sm, cn = (sb(ctx, n, [P, NT]) for n in ("m13", "sm3", "cn3"))
                    ch, xp, ew, eh_done = sems(ctx, "r3ch r3xp r3ew r3eh")
                    blk = ctx.enter_context(nc.Block())

                    def wide3(t):
                        return t[:, :].unsqueeze(2).to_broadcast([P, NT, E])

                    def product(e):
                        return banks[e][:, :].rearrange("p (m n) -> p m n", n=D)

                    @blk.tensor
                    def _(pe):
                        for e in range(2):
                            for m in range(DC):
                                for k in range(DC):
                                    r = mm3(pe, product(e)[:, m, :], eh[:, e * DC + k, m * P:(m + 1) * P],
                                            el[:, e * DC + k, m * P:(m + 1) * P], oh[:, k, :], ol[:, k, :],
                                            k == 0, k == DC - 1)
                            r.then_inc(ew, 1)

                    @blk.scalar
                    def _(act):
                        act.wait_ge(xp, 1)
                        act.activation(PR[:, :, :], LG[:, :, :], ACT.Exp).then_inc(xp, 1)
                        for e in range(2):
                            act.wait_ge(ew, e + 1)
                            act.activation(EW_hi[:, :, e, :], product(e), ACT.Copy).then_inc(eh_done, 1)

                    @blk.vector
                    def _(dve):
                        count = [0]

                        def link(ins):
                            count[0] += 1
                            ins.then_inc(ch, 1)
                            dve.wait_ge(ch, count[0])
                        link(dve.reduce_max(m1[:, :], LG[:, :, :], AX))
                        dve.tensor_tensor(LG[:, :, :], LG[:, :, :], wide3(m1), ALU.subtract).then_inc(xp, 1)
                        dve.wait_ge(xp, 2)
                        link(dve.reduce_sum(sm[:, :], PR[:, :, :], AX))
                        link(dve.reciprocal(sm[:, :], sm[:, :]))
                        link(dve.tensor_tensor(PR[:, :, :], PR[:, :, :], wide3(sm), ALU.mult))
                        link(dve.tensor_scalar(LG[:, :, :], PR[:, :, :], 0.3, None, ALU.is_gt))
                        link(dve.reduce_sum(cn[:, :], LG[:, :, :], AX))
                        link(dve.tensor_tensor(SC[:, 1, :], cn[:, :], PR[:, :, 1], ALU.mult))
                        link(dve.tensor_scalar(cn[:, :], cn[:, :], -1.0, float(E), ALU.mult, ALU.add))
                        link(dve.tensor_tensor(SC[:, 0, :], cn[:, :], PR[:, :, 0], ALU.mult))
                        for e in range(2):
                            dve.wait_ge(eh_done, e + 1)
                            dve.tensor_tensor(EW_lo[:, :, e, :], product(e), EW_hi[:, :, e, :].bitcast(F32), ALU.subtract)

                (first_added,) = sems(ph, "first_added")

                def products(pe, bank, sh, sl):
                    for c in range(DC):
                        m = mm3(pe, bank[:, :], sh[:, c, :], sl[:, c, :], EW_hi[:, c, :, :].rearrange("p e n -> p (e n)"),
                                EW_lo[:, c, :, :].rearrange("p e n -> p (e n)"), c == 0, c == 1)
                    return m

                def evac(dve, i, p, bank):
                    x = X[:, ds(i * D, D)]
                    dve.scalar_tensor_tensor(out=x, in0=bank[:, 0:D], scalar=SC[:, 0, ds(i, 1)], in1=x,
                                             op0=ALU.mult, op1=ALU.add).then_inc(first_added, 1)
                    dve.wait_ge(first_added, i + 1)
                    return dve.scalar_tensor_tensor(out=x, in0=bank[:, D:2 * D], scalar=SC[:, 1, ds(i, 1)], in1=x,
                                                    op0=ALU.mult, op1=ALU.add)

                def store(sp, de):
                    (stored,) = sems(ph, "stored")
                    with sp.Fori(0, NT) as i:
                        sp.wait_ge(de, i + 1 + 2)
                        sp.dma_start(out[0, ds(i * P, P), :], X[:, ds(i * D, D)]).then_inc(stored, 16)
                    sp.wait_ge(stored, 16 * NT)
                slot_pass("oo", NT, DC, XT_hi, XT_lo, [(products, None, evac)], on_sync=store)

        rows_in = nc.dram_tensor("routed_rows", ((NR + 1) * RT, D), F32, kind="Internal").ap()
        with ExitStack() as ph:
            XT_hi, XT_lo = split_pair(ph, "XT0", [P, DC, S])
            Wb_hi, Wb_lo = split_pair(ph, "W0", [P, 2064])
            Fx = sb(ph, "Fx", [P, NT * D])
            zeros = sb(ph, "zeros", [P, 4 * D])

            def part_of(t, off, kc, n):
                return t[:, off:off + kc * n].rearrange("p (c n) -> p c n", c=kc)
            spec0, off = {}, 0
            for name, kc, n in (("L0_xattn_Wq", 2, HA), ("L0_xattn_Wk", 2, HA), ("L0_xattn_Wv", 2, HA),
                                ("L0_xattn_WoT", 2, HA), ("L0_xattn_Wfc", 2, D), ("bo2", 2, P), ("Wof", 1, D)):
                spec0[name] = (off, kc, n)
                off += kc * n
            assert off <= 2064

            def w0(name):
                return part_of(Wb_hi, *spec0[name]), part_of(Wb_lo, *spec0[name])
            with ExitStack() as ctx:
                raw = sb(ctx, "raw0", [P, 2064])
                ctf = sb(ctx, "ctf", [P, DC, CP])
                ldw, ldc, ldx, ldv, ldb, hi, lo, z, mh, pd, idn, aa, st, ve, rs = sems(
                    ctx, "p_ldw p_ldc p_ldx p_ldv p_ldb p_hi p_lo p_z p_mh p_pd p_idn p_aa p_st p_ve p_rs")
                blk = ctx.enter_context(nc.Block())
                wnames = [n for n in spec0 if n.startswith("L0")]
                nw = spec0["bo2"][0]

                @blk.sync
                def _(sp):
                    for name in wnames:
                        o, kc, n = spec0[name]
                        sp.dma_start(part_of(raw, o, kc, n), A[name].rearrange("(c p) n -> p c n", p=P)).then_inc(ldw, 16)
                    for c in range(DC):
                        sp.dma_start(ctf[:, c, 0:C], A["ctxT"][c * P:(c + 1) * P, :]).then_inc(ldc, 16)
                    for t, name in ((GAMMA, "L0_xattn_ln_gamma"), (BETA, "L0_xattn_ln_beta"), (BV_S, "L1_xattn_bv_s"),
                                    (BV_C, "L1_xattn_bv_c"), (BG, "L1_xattn_bg"), (BIASE, "L0_ffn_expert_bias")):
                        sp.dma_start(t, A[name].partition_broadcast(P)).then_inc(ldv, 16)
                    sp.wait_ge(ldv, 16 * 6)

                @blk.scalar
                def _(act):
                    for j, (t, name) in enumerate(((BO, "L0_xattn_bo"), (BQC, "L1_xattn_bq_c"), (BKS, "L1_xattn_bk_s"),
                                                   (BQS, "L1_xattn_bq_s"), (BKC, "L1_xattn_bk_c"))):
                        act.dma_start(t, A[name]).then_inc(ldb, 16)
                    for j in range(4):
                        act.dma_start(X[:, j * 4 * D:(j + 1) * 4 * D].rearrange("p (i d) -> p i d", d=D),
                                      A["x"][0, j * 512:(j + 1) * 512, :].rearrange("(i p) d -> p i d", p=P)).then_inc(ldx, 16)
                    act.wait_ge(ldb, 16 * 5)
                    act.wait_ge(z, 1)
                    act.wait_ge(ldw, 16 * len(wnames))
                    for c in range(DC):
                        act.activation(raw[:, nw + c * P:nw + (c + 1) * P], ident[:, :], ACT.Identity,
                                       bias=BO[:, c:c + 1], scale=0.0).then_inc(z, 1)
                    act.wait_ge(z, 3)
                    act.activation(Wb_hi[:, 0:nw + 2 * P], raw[:, 0:nw + 2 * P], ACT.Copy).then_inc(hi, 1)
                    act.wait_ge(ldc, 32)
                    act.wait_ge(pd, 1)
                    for c in range(DC):
                        act.activation(CT_hi[:, c, :], ctf[:, c, :], ACT.Copy).then_inc(hi, 1)
                    act.wait_ge(aa, 1)
                    o, _, n = spec0["Wof"]
                    act.activation(Wb_hi[:, o:o + n], banks[0][:, 0:D], ACT.Copy).then_inc(hi, 1)

                @blk.gpsimd
                def _(pool):
                    pool.memset(ident[:, :], 0.0).then_inc(idn, 1)
                    pool.memset(mhalf[:, :], -0.5).then_inc(mh, 1)
                    pool.wait_ge(idn, 1)
                    pool.affine_select(out=ident[:, :], in_=ident[:, :], compare_op=ALU.not_equal, fill=1.0, base=0,
                                       pattern=[[-1, P]], channel_multiplier=1).then_inc(z, 1)
                    pool.wait_ge(mh, 1)
                    inverse_deviations(pool, st, ve, rs)

                @blk.vector
                def _(dve):
                    dve.memset(zeros[:, :], 0.0)
                    dve.memset(ctf[:, :, C:CP], 0.0).then_inc(pd, 1)
                    dve.wait_ge(hi, 1)
                    dve.tensor_tensor(Wb_lo[:, 0:nw + 2 * P], raw[:, 0:nw + 2 * P], Wb_hi[:, 0:nw + 2 * P].bitcast(F32),
                                      ALU.subtract).then_inc(lo, 1)
                    for c in range(DC):
                        dve.wait_ge(hi, c + 2)
                        dve.tensor_tensor(CT_lo[:, c, :], ctf[:, c, :], CT_hi[:, c, :].bitcast(F32),
                                          ALU.subtract).then_inc(lo, 1)
                    dve.wait_ge(ldx, 64)
                    row_statistics(dve, X, st)
                    dve.wait_ge(aa, 2)
                    dve.tensor_copy(BFC, banks[1][:, 0:D]).then_inc(lo, 1)
                    dve.wait_ge(hi, 4)
                    o, _, n = spec0["Wof"]
                    dve.tensor_tensor(Wb_lo[:, o:o + n], banks[0][:, 0:D], Wb_hi[:, o:o + n].bitcast(F32),
                                      ALU.subtract).then_inc(lo, 1)

                @blk.tensor
                def _(pe):
                    pe.wait_ge(hi, 1)
                    pe.wait_ge(lo, 1)
                    (ah, al), (fh, fl), (bh, bl) = w0("L0_xattn_WoT"), w0("L0_xattn_Wfc"), w0("bo2")
                    for c in range(DC):
                        m = mm3(pe, banks[0][:, 0:D], ah[:, c, :], al[:, c, :], fh[:, c, :], fl[:, c, :], c == 0, c == 1)
                    m.then_inc(aa, 1)
                    for c in range(DC):
                        m = mm3(pe, banks[1][:, 0:D], bh[:, c, :], bl[:, c, :], fh[:, c, :], fl[:, c, :], c == 0, c == 1)
                    m.then_inc(aa, 1)

            ingest("i0", XT_hi, XT_lo, statistics=False)

            fch, fcl = w0("L0_xattn_Wfc")

            def fc_products(pe, bank, sh, sl):
                for c in range(DC):
                    m = mm3(pe, bank[:, 0:D], sh[:, c, :], sl[:, c, :], fch[:, c, :], fcl[:, c, :], c == 0, c == 1)
                return m

            def fc_out(dve, i, p, bank):
                return dve.tensor_tensor(Fx[:, ds(i * D, D)], bank[:, 0:D], BFC, ALU.add)
            slot_pass("f0", NT, DC, XT_hi, XT_lo, [(fc_products, None, fc_out)])

            with ExitStack() as at:
                K_hi, K_lo = split_pair(at, "K0", [P, 1, CP])
                V_hi, V_lo = split_pair(at, "V0", [P, NC, HA])
                CX = sb(at, "CX", [P, 1, S])
                CXl = sb(at, "CXl", [P, P])
                kh, kl = w0("L0_xattn_Wk")
                vh, vl = w0("L0_xattn_Wv")

                def k_products(pe, i, w, two):
                    for c in range(DC):
                        x = ds(i * P, w * P)
                        m = mm3(pe, two[0][:, 0:w * P], kh[:, c, :], kl[:, c, :], CT_hi[:, c, x], CT_lo[:, c, x], c == 0, c == 1)
                    return m

                def v_products(pe, bank, sh, sl):
                    for c in range(DC):
                        m = mm3(pe, bank[:, 0:P], sh[:, c, :], sl[:, c, :], vh[:, c, :], vl[:, c, :], c == 0, c == 1)
                    return m

                def k_hi(act, i, w, two):
                    return act.activation(K_hi[:, 0, ds(i * P, w * P)], two[0][:, 0:w * P], ACT.Copy)

                def k_lo(dve, i, w, two):
                    return dve.tensor_tensor(K_lo[:, 0, ds(i * P, w * P)], two[0][:, 0:w * P],
                                             K_hi[:, 0, ds(i * P, w * P)].bitcast(F32), ALU.subtract)

                def v_hi(act, i, p, bank):
                    return act.activation(V_hi[:, ds(i, 1), :], bank[:, 0:P].unsqueeze(1), ACT.Copy)

                def v_lo(dve, i, p, bank):
                    return dve.tensor_tensor(V_lo[:, ds(i, 1), :], bank[:, 0:P].unsqueeze(1),
                                             V_hi[:, ds(i, 1), :].bitcast(F32), ALU.subtract)
                slot_pass("kv0", NC, DC, CT_hi, CT_lo, [(v_products, v_hi, v_lo)], (k_products, k_hi, k_lo))

                RI = sb(at, "RI", [P, NT])

                def ctx_of_lo(act, i, bank):
                    return act.activation(CXl[:, :], bank[:, P:2 * P], ACT.Copy)

                def ctx_sum(dve, i, bank, rinv):
                    dve.tensor_copy(RI[:, ds(i, 1)], rinv)
                    return dve.tensor_tensor(CX[:, 0, ds(i * P, P)], bank[:, 0:P], CXl[:, :], ALU.add)

                FR = 4
                (cleared,) = sems(at, "cleared")

                def clear_table(sp, finished):
                    n = (NR + 1) * RT // (P * FR)
                    for j in range(n):
                        sp.dma_start(rows_in[j * P * FR:(j + 1) * P * FR, :].rearrange("(p r) d -> p (r d)", p=P),
                                     zeros[:, :]).then_inc(cleared, 16)
                    sp.wait_ge(cleared, 16 * n)
                attention("a0", NT, XT_hi, XT_lo, *w0("L0_xattn_Wq"), None, 1, HA ** -0.5, NC, C, K_hi, K_lo, V_hi, V_lo,
                          HA, ctx_of_lo, ctx_sum, on_sync=clear_table)

                wofh, wofl = w0("Wof")

                def of_products(pe, bank, sh, sl):
                    return mm3(pe, bank[:, 0:D], sh[:, 0, :], sl[:, 0, :], wofh[:, 0, :], wofl[:, 0, :], True, True)

                def of_out(dve, i, p, bank):
                    z = Fx[:, ds(i * D, D)]
                    return dve.scalar_tensor_tensor(out=z, in0=bank[:, 0:D], scalar=RI[:, ds(i, 1)], in1=z,
                                                    op0=ALU.mult, op1=ALU.add)
                slot_pass("of", NT, 1, CX, None, [(of_products, None, of_out)])

            with ExitStack() as ctx:
                a, b, c, d, e, ns, nm = sems(ctx, "ya yb yc yd ye yns ynm")
                blk = ctx.enter_context(nc.Block())
                G4 = 4 * D

                def on_four(t):
                    return t.unsqueeze(1).to_broadcast([P, 4, D])

                @blk.gpsimd
                def _(pool):
                    inverse_deviations(pool, c, e, a)
                    with pool.Fori(0, NT // 4) as j:
                        x = X[:, ds(j * G4, G4)].rearrange("p (i d) -> p i d", d=D)
                        pool.tensor_tensor(x, x, on_four(BETA), ALU.add).then_inc(d, 1)

                @blk.vector
                def _(dve):
                    row_statistics(dve, Fx, c)
                    dve.wait_ge(a, NT // 4)
                    dve.wait_ge(c, 2 * NT)
                    shifts(dve).then_inc(ns, 1)
                    with dve.Fori(0, NT // 4) as j:
                        z4 = Fx[:, ds(j * G4, G4)].rearrange("p (i d) -> p i d", d=D)
                        x4 = X[:, ds(j * G4, G4)].rearrange("p (i d) -> p i d", d=D)
                        dve.wait_ge(nm, j * 4 + 4)
                        dve.tensor_tensor(z4, z4, on_four(GAMMA), ALU.mult).then_inc(b, 1)
                        dve.wait_ge(b, j * 2 + 1)
                        dve.wait_ge(d, j + 1)
                        dve.tensor_tensor(x4, x4, z4, ALU.add).then_inc(b, 1)

                @blk.scalar
                def _(act):
                    act.wait_ge(ns, 1)
                    with act.Fori(0, NT // 4) as j:
                        for q in range(4):
                            z = Fx[:, ds((j * 4 + q) * D, D)]
                            act.activation(z, z, ACT.Identity, bias=SHIFT[:, ds(j * 4 + q, 1)],
                                           scale=RSTD[:, ds(j * 4 + q, 1)]).then_inc(nm, 1)

        moe_phase()
        cross_phase()
        last_phase()


_HOST_TRANSPOSED = {"L0_xattn_WoT": "L0_xattn_Wo", **{n + "T": n for n in (
    "L0_ffn_router_w", "L1_xattn_Wq_c", "L1_xattn_Wk_s", "L1_xattn_Wv_s", "L1_xattn_Wq_s", "L1_xattn_Wk_c",
    "L1_xattn_Wv_c", "L1_xattn_Wg", "L1_ffn_gate_W", "L1_ffn_out_W")}}
_IN_COLUMNS = ("L0_xattn_bo", "L1_xattn_bq_c", "L1_xattn_bk_s", "L1_xattn_bq_s", "L1_xattn_bk_c")


def kernel(**inputs):
    import numpy as _np
    import concourse.bacc as _bacc
    from concourse import mybir as _mybir
    from concourse.bass_utils import run_bass_kernel_spmd as _run

    nc = _bacc.Bacc("TRN2", target_bir_lowering=False, num_devices=1)
    laid_out = {k: _np.asarray(v) for k, v in inputs.items()}
    laid_out["ctxT"] = laid_out.pop("ctx_1024")[0].T
    for new, old in _HOST_TRANSPOSED.items():
        laid_out[new] = _np.swapaxes(laid_out.pop(old), -1, -2)
    for name in _IN_COLUMNS:
        laid_out[name] = laid_out[name].reshape(D // P, P).T
    for new, old in (("w1T", "w1"), ("w3T", "w3"), ("w2T", "w2")):
        laid_out[new] = _np.swapaxes(_np.concatenate(
            (laid_out.pop("L0_ffn_" + old), laid_out.pop("L0_ffn_s" + old))), -1, -2)
    laid_out["expert01"] = laid_out.pop("L1_ffn_expert_W")[:2].reshape(2 * D, D)
    arrays, aps = {}, {}
    for name, a in laid_out.items():
        arrays[name] = _np.ascontiguousarray(a)
        aps[name] = nc.dram_tensor(name, a.shape, _mybir.dt.from_np(a.dtype), kind="ExternalInput").ap()
    out = nc.dram_tensor("out", (1, S, D), _mybir.dt.float32, kind="ExternalOutput").ap()
    build(nc, aps, out)
    r = _run(nc, [arrays], core_ids=[0])
    return r.results[0]["out"]
```
